# Optimizing a Trainium2 kernel written in Bass

```python
import numpy as np
import jax
import jax.numpy as jnp

def _softmax(x, axis=-1):
    return jax.nn.softmax(x, axis=axis)

def _gelu(x):
    return jax.nn.gelu(x, approximate=True)

def _silu(x):
    return jax.nn.silu(x)

def _sigmoid(x):
    return jax.nn.sigmoid(x)

def _layernorm(x, axis=-1, eps=1e-05):
    m = jnp.mean(x, axis=axis, keepdims=True)
    v = jnp.var(x, axis=axis, keepdims=True)
    return (x - m) / jnp.sqrt(v + eps)

def _scatter_add(tgt, idx, src, axis=0):
    return tgt.at[idx].add(src)

def _segment_sum(src, seg, n):
    return jax.ops.segment_sum(src, seg, n)
kernel_name = 'mk_early_fusion_d2_tok_img1024_r4_b6b0b3'

def setup_inputs(seed: int=0):
    np.random.seed(seed)
    _w = jnp.asarray

    def _rec_inputs():
        import jax
        import jax.numpy as jnp
        _rk = jax.random.key(seed)
        x = -0.00016672 + 0.999947 * jax.random.normal(jax.random.fold_in(_rk, 1), (32, 3, 96, 96), jnp.float32)
        txt = 0.00140885 + 1.4139 * jax.random.normal(jax.random.fold_in(_rk, 2), (32, 32, 256), jnp.float32)
        return (x, txt)
    x, txt = _rec_inputs()

    def _L0_tok_setup():
        import jax, jax.numpy as jnp
        import numpy as np
        B, C, H, W = (64, 3, 96, 96)
        P = 16
        NP = H // P * (W // P)
        PD = C * P * P
        ED = 256
        NCLS = 1

        def _layernorm(x, g, b, eps=1e-05):
            mu = jnp.mean(x, axis=-1, keepdims=True)
            var = jnp.mean(jnp.square(x - mu), axis=-1, keepdims=True)
            return (x - mu) * jax.lax.rsqrt(var + eps) * g + b
        key = jax.random.key(seed)
        ks = jax.random.split(key, 8)
        x = jax.random.normal(ks[0], (B, C, H, W), dtype=jnp.float32)
        ln1_g = jnp.ones((PD,), jnp.float32)
        ln1_b = jnp.zeros((PD,), jnp.float32)
        W_proj = jax.random.normal(ks[1], (PD, ED), jnp.float32) / np.sqrt(PD)
        b_proj = jnp.zeros((ED,), jnp.float32)
        ln2_g = jnp.ones((ED,), jnp.float32)
        ln2_b = jnp.zeros((ED,), jnp.float32)
        cls_token = jax.random.normal(ks[2], (1, NCLS, ED), jnp.float32)
        pos_emb = jax.random.normal(ks[3], (1, NP + NCLS, ED), jnp.float32)
        return {'x': x, 'ln1_g': ln1_g, 'ln1_b': ln1_b, 'W_proj': W_proj, 'b_proj': b_proj, 'ln2_g': ln2_g, 'ln2_b': ln2_b, 'cls_token': cls_token, 'pos_emb': pos_emb}
    _L0_tok_all = _L0_tok_setup()
    _L0_tok_in = {k: v for k, v in _L0_tok_all.items() if k in ('ln1_g', 'ln1_b', 'W_proj', 'b_proj', 'ln2_g', 'ln2_b', 'cls_token', 'pos_emb')}
    del _L0_tok_all

    def _L0_attn_setup():
        import jax, jax.numpy as jnp
        import numpy as np
        DIM = 256
        HEADS = 16
        HEAD_DIM = DIM // HEADS
        SCALE = HEAD_DIM ** (-0.5)
        key = jax.random.key(seed)
        k1, k2, k3, k4 = jax.random.split(key, 4)
        x = jax.random.normal(k1, (2, 512, DIM), dtype=jnp.float32)
        w_qkv = jax.random.normal(k2, (DIM, 3 * DIM), dtype=jnp.float32) * DIM ** (-0.5)
        w_proj = jax.random.normal(k3, (DIM, DIM), dtype=jnp.float32) * DIM ** (-0.5)
        b_proj = jax.random.normal(k4, (DIM,), dtype=jnp.float32) * 0.01
        return {'x': x, 'w_qkv': w_qkv, 'w_proj': w_proj, 'b_proj': b_proj}
    _L0_attn_all = _L0_attn_setup()
    _L0_attn_in = {k: v for k, v in _L0_attn_all.items() if k in ('w_qkv', 'w_proj', 'b_proj')}
    del _L0_attn_all

    def _L0_ffn_setup():
        import math
        import jax, jax.numpy as jnp
        import numpy as np
        B, S, D, F, E = (8, 512, 256, 1024, 8)
        CAPACITY_FACTOR = 1.0
        key = jax.random.key(seed)
        k1, k2, k3, k4 = jax.random.split(key, 4)
        x = jax.random.normal(k1, (B, S, D), dtype=jnp.float32)
        Wr = jax.random.normal(k2, (D, E), dtype=jnp.float32) * (1.0 / math.sqrt(D))
        W1 = jax.random.normal(k3, (E, D, F), dtype=jnp.float32) * (1.0 / math.sqrt(D))
        W2 = jax.random.normal(k4, (E, F, D), dtype=jnp.float32) * (1.0 / math.sqrt(F))
        return {'x': x, 'Wr': Wr, 'W1': W1, 'W2': W2}
    _L0_ffn_all = _L0_ffn_setup()
    _L0_ffn_in = {k: v for k, v in _L0_ffn_all.items() if k in ('Wr', 'W1', 'W2')}
    del _L0_ffn_all

    def _L1_attn_setup():
        import math
        import jax, jax.numpy as jnp
        import numpy as np
        NUM_HEADS = 16
        EMBED = 256
        B, T = (2, 512)
        key = jax.random.key(seed)
        k1, k2 = jax.random.split(key)
        x = jax.random.normal(k1, (B, T, EMBED), dtype=jnp.float32)
        bound = 1.0 / math.sqrt(NUM_HEADS * EMBED)
        weight = jax.random.uniform(k2, (NUM_HEADS * EMBED, EMBED), dtype=jnp.float32, minval=-bound, maxval=bound)
        return {'x': x, 'weight': weight}
    _L1_attn_all = _L1_attn_setup()
    _L1_attn_in = {k: v for k, v in _L1_attn_all.items() if k in ('weight',)}
    del _L1_attn_all

    def _L1_ffn_setup():
        import jax, jax.numpy as jnp
        import numpy as np
        QMAX = 127.0

        def _ste_round(v):
            return v + jax.lax.stop_gradient(jnp.round(v) - v)

        def _act_fake_quant(x, clip_factor):
            scale = jax.nn.sigmoid(clip_factor) * jnp.max(jnp.abs(x)) / QMAX
            return jnp.clip(_ste_round(x / scale), -QMAX - 1.0, QMAX) * scale

        def _weight_fake_quant(w):
            scale = jnp.max(jnp.abs(w), axis=1, keepdims=True) / QMAX
            return jnp.clip(_ste_round(w / scale), -QMAX - 1.0, QMAX) * scale
        key = jax.random.key(seed)
        k1, k2, k3, k4 = jax.random.split(key, 4)
        B, S, H, I = (8, 2048, 256, 704)
        return {'x': jax.random.normal(k1, (B, S, H), dtype=jnp.float32), 'clip_x': jnp.full((1,), 4.0, dtype=jnp.float32), 'clip_down': jnp.full((1,), 4.0, dtype=jnp.float32), 'w_gate': jax.random.normal(k2, (I, H), dtype=jnp.float32) * 0.02, 'w_up': jax.random.normal(k3, (I, H), dtype=jnp.float32) * 0.02, 'w_down': jax.random.normal(k4, (H, I), dtype=jnp.float32) * 0.02}
    _L1_ffn_all = _L1_ffn_setup()
    _L1_ffn_in = {k: v for k, v in _L1_ffn_all.items() if k in ('clip_x', 'clip_down', 'w_gate', 'w_up', 'w_down')}
    del _L1_ffn_all
    return {'x': x, 'txt': txt, 'L0_tok_ln1_g': _L0_tok_in['ln1_g'], 'L0_tok_ln1_b': _L0_tok_in['ln1_b'], 'L0_tok_W_proj': _L0_tok_in['W_proj'], 'L0_tok_b_proj': _L0_tok_in['b_proj'], 'L0_tok_ln2_g': _L0_tok_in['ln2_g'], 'L0_tok_ln2_b': _L0_tok_in['ln2_b'], 'L0_tok_cls_token': _L0_tok_in['cls_token'], 'L0_tok_pos_emb': _L0_tok_in['pos_emb'], 'L0_attn_w_qkv': _L0_attn_in['w_qkv'], 'L0_attn_w_proj': _L0_attn_in['w_proj'], 'L0_attn_b_proj': _L0_attn_in['b_proj'], 'L0_ffn_Wr': _L0_ffn_in['Wr'], 'L0_ffn_W1': _L0_ffn_in['W1'], 'L0_ffn_W2': _L0_ffn_in['W2'], 'L1_attn_weight': _L1_attn_in['weight'], 'L1_ffn_clip_x': _L1_ffn_in['clip_x'], 'L1_ffn_clip_down': _L1_ffn_in['clip_down'], 'L1_ffn_w_gate': _L1_ffn_in['w_gate'], 'L1_ffn_w_up': _L1_ffn_in['w_up'], 'L1_ffn_w_down': _L1_ffn_in['w_down']}

def reference(x, txt, L0_tok_ln1_g, L0_tok_ln1_b, L0_tok_W_proj, L0_tok_b_proj, L0_tok_ln2_g, L0_tok_ln2_b, L0_tok_cls_token, L0_tok_pos_emb, L0_attn_w_qkv, L0_attn_w_proj, L0_attn_b_proj, L0_ffn_Wr, L0_ffn_W1, L0_ffn_W2, L1_attn_weight, L1_ffn_clip_x, L1_ffn_clip_down, L1_ffn_w_gate, L1_ffn_w_up, L1_ffn_w_down):
    import jax
    import jax.numpy as jnp

    def _L0_tok_ref(x, ln1_g, ln1_b, W_proj, b_proj, ln2_g, ln2_b, cls_token, pos_emb):
        import jax, jax.numpy as jnp
        import numpy as np
        B, C, H, W = (64, 3, 96, 96)
        P = 16
        NP = H // P * (W // P)
        PD = C * P * P
        ED = 256
        NCLS = 1

        def _layernorm(x, g, b, eps=1e-05):
            mu = jnp.mean(x, axis=-1, keepdims=True)
            var = jnp.mean(jnp.square(x - mu), axis=-1, keepdims=True)
            return (x - mu) * jax.lax.rsqrt(var + eps) * g + b
        b = x.shape[0]
        h, w = (H // P, W // P)
        patches = x.reshape(b, C, h, P, w, P)
        patches = patches.transpose(0, 2, 4, 3, 5, 1).reshape(b, h * w, P * P * C)
        z = _layernorm(patches, ln1_g, ln1_b)
        z = jnp.einsum('bnp,pe->bne', z, W_proj) + b_proj
        z = _layernorm(z, ln2_g, ln2_b)
        cls = jnp.broadcast_to(cls_token, (b, NCLS, ED))
        z = jnp.concatenate([cls, z], axis=1)
        z = z + pos_emb
        return z

    def _L0_attn_ref(x, w_qkv, w_proj, b_proj):
        import jax, jax.numpy as jnp
        import numpy as np
        DIM = 256
        HEADS = 16
        HEAD_DIM = DIM // HEADS
        SCALE = HEAD_DIM ** (-0.5)
        B, N, C = x.shape
        qkv = jnp.einsum('bnc,cd->bnd', x, w_qkv)
        qkv = qkv.reshape(B, N, 3, HEADS, HEAD_DIM).transpose(2, 0, 3, 1, 4)
        q, k, v = (qkv[0], qkv[1], qkv[2])
        attn = jnp.einsum('bhqd,bhkd->bhqk', q, k) * SCALE
        attn = jax.nn.softmax(attn, axis=-1)
        out = jnp.einsum('bhqk,bhkd->bhqd', attn, v)
        out = out.transpose(0, 2, 1, 3).reshape(B, N, C)
        return jnp.einsum('bnc,cd->bnd', out, w_proj) + b_proj

    def _L0_ffn_ref(x, Wr, W1, W2):
        import math
        import jax, jax.numpy as jnp
        import numpy as np
        B, S, D, F, E = (8, 512, 256, 1024, 8)
        CAPACITY_FACTOR = 1.0
        b, s, d = x.shape
        t = b * s
        cap = max(math.ceil(t * CAPACITY_FACTOR / E), 1)
        xf = x.reshape(t, d)
        probs = jax.nn.softmax(xf.astype(jnp.float32) @ Wr, axis=-1)
        eidx = jnp.argmax(probs, axis=-1)
        p_tok = jnp.take_along_axis(probs, eidx[:, None], axis=1)[:, 0]
        onehot = jax.nn.one_hot(eidx, E, dtype=jnp.int32)
        rank_all = jnp.cumsum(onehot, axis=0) - onehot
        rank = jnp.take_along_axis(rank_all, eidx[:, None], axis=1)[:, 0]
        keep = rank < cap
        slot = jnp.where(keep, rank, cap)
        dispatch = jnp.zeros((E, cap + 1), dtype=jnp.int32).at[eidx, slot].set(jnp.arange(t, dtype=jnp.int32))
        valid = jnp.zeros((E, cap + 1), dtype=bool).at[eidx, slot].set(keep)
        dispatch = dispatch[:, :cap]
        valid = valid[:, :cap]
        xe = xf[dispatch]
        h = jnp.maximum(jnp.einsum('ecd,edf->ecf', xe, W1), 0.0)
        ye = jnp.einsum('ecf,efd->ecd', h, W2)
        pe = p_tok[dispatch]
        ye = ye * (pe * valid.astype(ye.dtype))[:, :, None]
        y = jnp.zeros((t, d), dtype=x.dtype).at[dispatch.reshape(-1)].add(ye.reshape(E * cap, d).astype(x.dtype))
        return y.reshape(b, s, d)

    def _L1_attn_ref(x, weight):
        import math
        import jax, jax.numpy as jnp
        import numpy as np
        NUM_HEADS = 16
        EMBED = 256
        B, T = (2, 512)
        b, t, c = x.shape
        nh = NUM_HEADS
        hs = c // nh
        y = x.reshape(b, t, nh, hs).transpose(0, 2, 1, 3)
        scores = jnp.einsum('bhtk,bhsk->bhts', y, y) / math.sqrt(hs)
        attn = jax.nn.softmax(scores, axis=-1)
        o = jnp.einsum('bhts,bsc->bhtc', attn, x)
        o = o.transpose(0, 2, 1, 3).reshape(b, t, nh * c)
        return o @ weight

    def _L1_ffn_ref(x, clip_x, clip_down, w_gate, w_up, w_down):
        import jax, jax.numpy as jnp
        import numpy as np
        QMAX = 127.0

        def _ste_round(v):
            return v + jax.lax.stop_gradient(jnp.round(v) - v)

        def _act_fake_quant(x, clip_factor):
            scale = jax.nn.sigmoid(clip_factor) * jnp.max(jnp.abs(x)) / QMAX
            return jnp.clip(_ste_round(x / scale), -QMAX - 1.0, QMAX) * scale

        def _weight_fake_quant(w):
            scale = jnp.max(jnp.abs(w), axis=1, keepdims=True) / QMAX
            return jnp.clip(_ste_round(w / scale), -QMAX - 1.0, QMAX) * scale
        xq = _act_fake_quant(x, clip_x[0])
        gate = jnp.einsum('bsh,ih->bsi', xq, _weight_fake_quant(w_gate))
        up = jnp.einsum('bsh,ih->bsi', xq, _weight_fake_quant(w_up))
        h = _act_fake_quant(jax.nn.silu(gate) * up, clip_down[0])
        return jnp.einsum('bsi,hi->bsh', h, _weight_fake_quant(w_down))
    h = _L0_tok_ref(x, L0_tok_ln1_g, L0_tok_ln1_b, L0_tok_W_proj, L0_tok_b_proj, L0_tok_ln2_g, L0_tok_ln2_b, L0_tok_cls_token, L0_tok_pos_emb)
    h = jnp.concatenate([h, txt], axis=1)
    h = h + _L0_attn_ref(_layernorm(h, axis=-1), L0_attn_w_qkv, L0_attn_w_proj, L0_attn_b_proj)
    h = h + _L0_ffn_ref(_layernorm(h, axis=-1), L0_ffn_Wr, L0_ffn_W1, L0_ffn_W2)
    h = h + _L1_attn_ref(_layernorm(h, axis=-1), L1_attn_weight)
    h = h + _L1_ffn_ref(_layernorm(h, axis=-1), L1_ffn_clip_x, L1_ffn_clip_down, L1_ffn_w_gate, L1_ffn_w_up, L1_ffn_w_down)
    return h

_drawn_inputs = setup_inputs


def setup_inputs(seed=0):
    import zlib

    import numpy as np

    out = dict(_drawn_inputs(seed))
    spreads = {'L0_tok_ln1_g': (1.0, 0.2),
     'L0_tok_ln1_b': (0.0, 0.1),
     'L0_tok_b_proj': (0.0, 0.1),
     'L0_tok_ln2_g': (1.0, 0.2),
     'L0_tok_ln2_b': (0.0, 0.1)}
    factors = {'L0_attn_b_proj': 4.951,
     'L1_ffn_w_gate': 2.824,
     'L1_ffn_w_up': 2.815,
     'L1_ffn_w_down': 2.737}
    for name, (base, spread) in spreads.items():
        noise = np.random.default_rng([zlib.crc32(name.encode()), seed]).standard_normal(out[name].shape)
        drawn = base * np.exp(spread * noise) if base else spread * noise
        out[name] = jnp.asarray(drawn.astype(out[name].dtype))
    for name, factor in factors.items():
        out[name] = (out[name] * factor).astype(out[name].dtype)
    return out
```

```python
from contextlib import ExitStack

import concourse.bass as bass
from concourse import mybir

F32 = mybir.dt.float32
BF16 = mybir.dt.bfloat16
I32 = mybir.dt.int32
U32 = mybir.dt.uint32
ALU = mybir.AluOpType
ACT = mybir.ActivationFunctionType
X = mybir.AxisListType.X
EPS = 1e-5

NB = 32
NPT = 36
NT = 69
D = 256
NH = 16
HD = D // NH
HP = 32
PAIRS = NB // 2
SIDE = 6
PIX = 16
ROWS = 3 * PIX
NE = 8
CAP = NB * NT // NE
FF = 1024
CH = NH // 4
HALF = 8 * NT
CW = 4 * NT
W2T = 2 * NT


class Shared:
    pass


def clear(nc, used):
    with nc.Block() as block:
        @block.sync
        def _(sp):
            for s in used:
                sp.sem_clear(s)


def tokens(nc, k, ins):
    with ExitStack() as ctx:
        sb = lambda n, s, d=F32: ctx.enter_context(nc.sbuf_tensor(n, s, d))
        used = []
        sem = lambda n: used.append(ctx.enter_context(nc.semaphore(n))) or used[-1]
        img = [sb("img_hi", [128, ROWS, 96]), sb("img_lo", [64, ROWS, 96])]
        size = [128, 64]
        xn = [sb("xn_hi", [128, SIDE, ROWS * PIX]), sb("xn_lo", [64, SIDE, ROWS * PIX])]
        wt = sb("tok_w", [128, 2, 3, D])
        g1 = sb("tok_g1", [128, 2, 3])
        b1 = sb("tok_b1", [128, 2, 3])
        bp = sb("tok_bproj", [128, 2])
        g2 = sb("tok_g2", [NPT, D])
        pos = sb("tok_pos", [NPT, D])
        b2 = sb("tok_b2", [NPT, D])
        cls = sb("tok_cls", [1, D])
        pos0 = sb("tok_pos0", [1, D])
        st = [sb(f"tok_st{g}", [size[g], SIDE, 2, 6]) for g in range(2)]
        mv = [sb(f"tok_mv{g}", [size[g], SIDE, 2]) for g in range(2)]
        rs = [sb(f"tok_rs{g}", [size[g], SIDE]) for g in range(2)]
        xt = [sb(f"tok_xt{i}", [128, 6, 384]) for i in range(2)]
        zt = sb("tok_zt", [128, 2, NB, NPT])
        st2 = sb("tok_st2", [NPT, NB, 6])
        mv2 = sb("tok_mv2", [NPT, NB, 2])
        rs2 = sb("tok_rs2", [NPT, NB])
        zn = [sb(f"tok_zn{i}", [NPT, 4, D]) for i in range(2)]
        s_img = [sem("s_img_hi"), sem("s_img_lo")]
        s_w = sem("s_tok_w")
        s_col = sem("s_tok_columns")
        s_row = sem("s_tok_rows")
        s_txt = sem("s_txt")
        s_crow = sem("s_cls_row")
        s_cls = sem("s_cls_stored")
        s_st = sem("s_tok_stats")
        s_mv = sem("s_tok_meanvar")
        s_ve = sem("s_tok_vareps")
        s_rs = sem("s_tok_rstd")
        s_xn = sem("s_tok_xn")
        s_tp = sem("s_tok_transposed")
        s_te = [sem("s_tok_xt_by_act"), sem("s_tok_xt_by_dve")]
        s_z = sem("s_tok_z")
        s_ze = sem("s_tok_z_evacuated")
        s_zt = sem("s_tok_z_tokens")
        s_st2 = sem("s_tok_stats2")
        s_mv2 = sem("s_tok_meanvar2")
        s_ve2 = sem("s_tok_vareps2")
        s_rs2 = sem("s_tok_rstd2")
        s_zn = sem("s_tok_zn")
        zero = sb("zero", [92, 6 * D])
        s_zero = sem("s_zero")
        bk = k.bank
        block = ctx.enter_context(nc.Block())

        @block.sync
        def _(sp):
            for hh in range(SIDE):
                g, q = hh // 4, hh % 4
                src = ins["x"][:, :, PIX * hh:PIX * hh + PIX, :].rearrange("b c r w -> b c (r w)")
                dst = img[g][32 * q:32 * q + 32].rearrange("b (c r) w -> b c (r w)", c=3)
                sp.dma_start(dst, src).then_inc(s_img[g], 16)
            sp.dma_start(k.H[NPT + 1:NT, :, :], ins["txt"].rearrange("b s d -> s b d")).then_inc(s_txt, 16)
            sp.wait_ge(s_zero, 1)
            rows = k.xd.rearrange("(g p j) d -> g p (j d)", p=92, j=6)
            for g in range(NE * CAP // (92 * 6)):
                sp.dma_start(rows[g], zero[:]).then_inc(k.s_xd0, 16)
            k.xd0 = 16 * (NE * CAP // (92 * 6))
            sp.wait_ge(s_crow, 1)
            sp.dma_start(k.H[NPT:NPT + 1, :, :], cls[0:1, :].unsqueeze(1).broadcast_to([1, NB, D])).then_inc(s_cls, 16)
            sp.wait_ge(s_txt, 16)
            sp.wait_ge(s_cls, 16)

        @block.scalar
        def _(act):
            row = lambda n: ins[n].rearrange("(a d) -> a d", a=1)
            act.dma_start(wt[:], ins["L0_tok_W_proj"].rearrange("(h p c) e -> p h c e", h=2, c=3)).then_inc(s_w, 16)
            act.dma_start(g1[:], ins["L0_tok_ln1_g"].rearrange("(h p c) -> p h c", h=2, c=3)).then_inc(s_col, 16)
            act.dma_start(b1[:], ins["L0_tok_ln1_b"].rearrange("(h p c) -> p h c", h=2, c=3)).then_inc(s_col, 16)
            with nc.allow_non_contiguous_dma(reason="256 numbers, once"):
                act.dma_start(bp[:], ins["L0_tok_b_proj"].rearrange("(e p) -> p e", e=2)).then_inc(s_col, 16)
            act.dma_start(g2[:], row("L0_tok_ln2_g").broadcast_to([NPT, D])).then_inc(s_row, 16)
            act.dma_start(b2[:], row("L0_tok_ln2_b").broadcast_to([NPT, D])).then_inc(s_row, 16)
            act.dma_start(pos[:], ins["L0_tok_pos_emb"][0, 1:NPT + 1, :]).then_inc(s_row, 16)
            act.dma_start(pos0[:], ins["L0_tok_pos_emb"][0, 0:1, :]).then_inc(s_row, 16)
            act.dma_start(cls[:], ins["L0_tok_cls_token"][0, 0:1, :]).then_inc(s_row, 16)
            act.wait_ge(s_col, 48)
            for w in range(3):
                for c in range(0, 6, 2):
                    n = 6 * w + c
                    act.wait_ge(s_tp, n + 1)
                    if w >= 2:
                        act.wait_ge(s_z, 2 * (w - 1))
                    act.activation(xt[w % 2][:, c, :], bk[c % 2][:, 0:384], ACT.Identity,
                                   bias=b1[:, c % 2, c // 2:c // 2 + 1],
                                   scale=g1[:, c % 2, c // 2:c // 2 + 1]).then_inc(s_te[0], 1)
                for e in range(2):
                    act.wait_ge(s_z, 2 * w + e + 1)
                    src = bk[2 + e][:, 0:384].rearrange("p (w h b) -> p w h b", w=2, h=SIDE)
                    for v in range(2):
                        dst = zt[:, e].rearrange("p b (h w) -> p w h b", w=SIDE)[:, 2 * w + v]
                        i = act.activation(dst, src[:, v], ACT.Identity, bias=bp[:, e:e + 1])
                    i.then_inc(s_ze, 1)

        @block.gpsimd
        def _(pool):
            pool.memset(zero[:], 0.0).then_inc(s_zero, 1)
            for g in range(2):
                pool.wait_ge(s_mv, g + 1)
                pool.tensor_scalar(rs[g][:], mv[g][:, :, 1], EPS, None, ALU.add).then_inc(s_ve, 1)
                pool.wait_ge(s_ve, g + 1)
                pool.tensor_tensor(rs[g][:], rs[g][:], k.mhalf[0:size[g], 0:SIDE], ALU.pow).then_inc(s_rs, 1)
            for q in range(NB // 4):
                pool.wait_ge(s_mv2, q + 1)
                v = rs2[:, 4 * q:4 * q + 4]
                pool.tensor_scalar(v, mv2[:, 4 * q:4 * q + 4, 1], EPS, None, ALU.add).then_inc(s_ve2, 1)
                pool.wait_ge(s_ve2, q + 1)
                pool.tensor_tensor(v, v, k.mhalf[0:NPT, 0:4], ALU.pow).then_inc(s_rs2, 1)

        @block.vector
        def _(dve):
            for g in range(2):
                dve.wait_ge(s_img[g], 64 if g == 0 else 32)
                for w in range(SIDE):
                    for h in range(2):
                        i = dve.bn_stats(st[g][:, w, h, :], img[g][:, 24 * h:24 * h + 24, PIX * w:PIX * w + PIX])
                i.then_inc(s_st, 1)
                dve.wait_ge(s_st, g + 1)
                for w in range(SIDE):
                    i = dve.bn_aggr(mv[g][:, w, :], st[g][:, w].rearrange("p h s -> p (h s)"))
                i.then_inc(s_mv, 1)
            dve.wait_ge(s_row, 80)
            dve.tensor_tensor(cls[:], cls[:], pos0[:], ALU.add).then_inc(s_crow, 1)
            dve.tensor_tensor(pos[:], pos[:], b2[:], ALU.add).then_inc(s_crow, 1)
            dve.wait_ge(s_rs, 2)
            for w in range(SIDE):
                for g in range(2):
                    v = img[g][:, :, PIX * w:PIX * w + PIX]
                    o = xn[g][:, w, :].rearrange("p (r x) -> p r x", x=PIX)
                    i = dve.tensor_scalar(o, v, mv[g][:, w, 0:1], rs[g][:, w:w + 1], ALU.subtract, ALU.mult)
                i.then_inc(s_xn, 1)
            dve.wait_ge(s_col, 48)
            for w in range(3):
                for c in range(1, 6, 2):
                    dve.wait_ge(s_tp, 6 * w + c + 1)
                    if w >= 2:
                        dve.wait_ge(s_z, 2 * (w - 1))
                    dve.tensor_scalar(xt[w % 2][:, c, :], bk[c % 2][:, 0:384],
                                      g1[:, c % 2, c // 2:c // 2 + 1], b1[:, c % 2, c // 2:c // 2 + 1],
                                      ALU.mult, ALU.add).then_inc(s_te[1], 1)
            for q in range(NB // 4):
                dve.wait_ge(s_zt, q + 1)
                z = lambda j: bk[4 * (q % 2) + j // 2][0:NPT, D * (j % 2):D * (j % 2) + D]
                for j in range(4):
                    i = dve.bn_stats(st2[:, 4 * q + j, :], z(j))
                i.then_inc(s_st2, 1)
                dve.wait_ge(s_st2, q + 1)
                for j in range(4):
                    i = dve.bn_aggr(mv2[:, 4 * q + j, :], st2[:, 4 * q + j, :])
                i.then_inc(s_mv2, 1)
                dve.wait_ge(s_rs2, q + 1)
                for j in range(4):
                    b = 4 * q + j
                    i = dve.scalar_tensor_tensor(zn[q % 2][:, j, :], z(j), mv2[:, b, 0:1], g2[:],
                                                 ALU.subtract, ALU.mult)
                i.then_inc(s_zn, 1)
                dve.wait_ge(s_zn, q + 1)
                for j in range(4):
                    b = 4 * q + j
                    dve.scalar_tensor_tensor(k.H[0:NPT, b, :], zn[q % 2][:, j, :], rs2[:, b:b + 1], pos[:],
                                             ALU.mult, ALU.add)

        @block.tensor
        def _(pe):
            pe.wait_ge(s_w, 16)
            for w in range(3):
                pe.wait_ge(s_xn, 2 * w + 2)
                for c in range(6):
                    n = 6 * w + c
                    if n >= 2:
                        pe.wait_ge(s_te[c % 2], (n - 2) // 2 + 1)
                    for v in range(2):
                        for g in range(2):
                            src = xn[g][:, 2 * w + v, 128 * c:128 * c + 128]
                            i = pe.transpose(bk[c % 2][:, 192 * v + 128 * g:192 * v + 128 * g + size[g]], src,
                                             k.ident[0:size[g], 0:size[g]])
                    i.then_inc(s_tp, 1)
                pe.wait_ge(s_te[0], 3 * w + 3)
                pe.wait_ge(s_te[1], 3 * w + 3)
                for e in range(2):
                    if w >= 1:
                        pe.wait_ge(s_ze, 2 * (w - 1) + e + 1)
                    for c in range(6):
                        i = pe.matmul(bk[2 + e][:, 0:384], wt[:, c % 2, c // 2, 128 * e:128 * e + 128],
                                      xt[w % 2][:, c, :], start=(c == 0), stop=(c == 5))
                    i.then_inc(s_z, 1)
            pe.wait_ge(s_ze, 6)
            for q in range(NB // 4):
                if q >= 2:
                    pe.wait_ge(s_zn, q - 1)
                for j in range(4):
                    for e in range(2):
                        o = D * (j % 2) + 128 * e
                        i = pe.transpose(bk[4 * (q % 2) + j // 2][0:NPT, o:o + 128], zt[:, e, 4 * q + j, :],
                                         k.ident[:])
                i.then_inc(s_zt, 1)

    clear(nc, used)





def attention(nc, k, ins):
    with ExitStack() as ctx:
        sb = lambda n, s, d=F32: ctx.enter_context(nc.sbuf_tensor(n, s, d))
        sem = lambda n: ctx.enter_context(nc.semaphore(n))
        two = lambda n, s, d=F32: [sb(f"{n}{i}", s, d) for i in range(2)]
        H = k.H
        wqk = sb("at_wqk", [128, 2, 2, NH, HP])
        wv = sb("at_wv", [128, 2, D])
        wo = sb("at_wo", [128, CH, D])
        bo = sb("at_bo", [NT, 2, D])
        st = two("at_st", [NT, 2, 6])
        mv = two("at_mv", [NT, 2, 2])
        rs = two("at_rs", [NT, 2])
        hn = two("at_hn", [NT, 2, D])
        hT = two("at_hT", [128, 2, W2T])
        qT = two("at_qT", [128, CH, W2T])
        kd = two("at_kd", [128, 2, CH, CW])
        vp = two("at_vp", [NT, 2, NH, HP])
        eb = two("at_e", [NT, HALF])
        mx = two("at_mx", [NT, 8])
        sm = two("at_sum", [NT, 8])
        rc = two("at_rc", [NT, 8])
        ets = two("at_et", [NT, HALF])
        oT = two("at_oT", [128, CH, W2T])
        s_w = sem("s_at_w")
        s_w0 = sem("s_at_w_zeroed")
        s_z0 = sem("s_at_pads_zeroed")
        s_st, s_mv, s_ve, s_rs, s_hn = (sem(f"s_at_{n}") for n in ("stats", "meanvar", "vareps", "rstd", "hn"))
        s_full = [sem(f"s_at_bank_full{i}") for i in range(2)]
        s_drained = [sem(f"s_at_bank_drained{i}") for i in range(2)]
        s_S, s_mx, s_sub, s_exp, s_sum, s_rc, s_nrm = (
            sem(f"s_at_{n}") for n in ("scores", "max", "sub", "exp", "sum", "recip", "norm"))
        s_T, s_te, s_PV, s_xa, s_xd, s_hb = (
            sem(f"s_at_{n}") for n in ("turned", "turned_sb", "pv", "out_by_act", "out_by_dve", "bias"))
        sc = k.ps[:, 0:2, :]
        tb = k.ps[:, 2:4, :]
        vb = k.ps[:, 4:6, :]
        mb = [k.bank[6], k.bank[7]]
        LAST = PAIRS - 1

        HT, Q0, Q1, K0, K1, V, PROJ = range(7)

        def use(i, q, what):
            n = 7 * q + what
            return n % 2, i * 7 + 3 + n // 2

        def use0(what):
            return what % 2, what // 2

        def proj_use(i, q):
            bank, before = use(i, q, PROJ)
            return bank, before - 3 if isinstance(i, int) and 2 * i + q == LAST else before

        def unit(i, q, u):
            return i * 8 + (4 * q + u)

        def after(i, q):
            return (i, 1) if q == 0 else (i + 1, 0)

        def drained(eng, u):
            eng.wait_ge(s_drained[u[0]], u[1] + 1)

        def filled(eng, u):
            eng.wait_ge(s_full[u[0]], u[1] + 1)
            return mb[u[0]]

        def k_diag(eng, copy, q, what, u):
            b = filled(eng, u)
            m = 2 * (what - K0)
            for r in range(4):
                src = b[HP * r:HP * r + HP, 0:2 * W2T].rearrange("p (m j t) -> p m j t", m=2, j=2)
                dst = kd[q][HP * r:HP * r + HP, :, m:m + 2, NT * r:NT * r + NT].rearrange("p j m t -> p m j t")
                x = copy(dst, src)
            x.then_inc(s_drained[u[0]], 1)

        block = ctx.enter_context(nc.Block())

        @block.sync
        def _(sp):
            sp.wait_ge(s_w0, 2)
            for c in range(2):
                for t in range(2):
                    sp.dma_start(wqk[:, c, t, :, 0:HD],
                                 ins["L0_attn_w_qkv"][128 * c:128 * c + 128, D * t:D * t + D]
                                 .rearrange("p (h e) -> p h e", h=NH)).then_inc(s_w, 16)
                sp.dma_start(wv[:, c, :], ins["L0_attn_w_qkv"][128 * c:128 * c + 128, 2 * D:3 * D]).then_inc(s_w, 16)
            for r in range(4):
                for c in range(CH):
                    h = 4 * c + r
                    sp.dma_start(wo[HP * r:HP * r + HD, c, :],
                                 ins["L0_attn_w_proj"][HD * h:HD * h + HD, :]).then_inc(s_w, 16)
            for j in range(2):
                sp.dma_start(bo[:, j, :], ins["L0_attn_b_proj"].rearrange("(a d) -> a d", a=1)
                             .broadcast_to([NT, D])).then_inc(s_w, 16)

        @block.tensor
        def _(pe):
            def fill(u):
                pe.wait_ge(s_drained[u[0]], u[1])
                return mb[u[0]]

            def front(i, q, what, u):
                if what == HT:
                    pe.wait_ge(s_hn, i * 2 + (q + 1))
                    b = fill(u)
                    for j in range(2):
                        for c in range(2):
                            o = W2T * c + NT * j
                            x = pe.transpose(b[:, o:o + NT], hn[q][:, j, 128 * c:128 * c + 128],
                                             k.ident[0:NT, 0:NT])
                elif what == V:
                    b = fill(u)
                    for j in range(2):
                        for c in range(2):
                            x = pe.matmul(b[0:NT, D * j:D * j + D], hT[q][:, c, NT * j:NT * j + NT], wv[:, c, :],
                                          start=(c == 0), stop=(c == 1))
                else:
                    b = fill(u)
                    t, m = (what - Q0) // 2, 2 * ((what - Q0) % 2)
                    for h in range(2):
                        for c in range(2):
                            x = pe.matmul(b[:, W2T * h:W2T * h + W2T],
                                          wqk[:, c, t, 4 * (m + h):4 * (m + h) + 4, :], hT[q][:, c, :],
                                          start=(c == 0), stop=(c == 1))
                x.then_inc(s_full[u[0]], 1)

            def scores(i, q, u, ready=()):
                j, h = u // 2, u % 2
                for r in ready:
                    drained(pe, r)
                n = unit(i, q, u)
                pe.wait_ge(s_sub, n)
                for c in range(2):
                    x = pe.matmul(sc[0:NT, c, 0:CW], qT[q][:, 2 * h + c, NT * j:NT * j + NT],
                                  kd[q][:, j, 2 * h + c, :], start=True, stop=True)
                x.then_inc(s_S, 1)

            def turn(i, q, u):
                n = unit(i, q, u)
                pe.wait_ge(s_nrm, n + 1)
                pe.wait_ge(s_te, n)
                for h in range(8):
                    x = pe.transpose(tb[0:NT, h // 4, NT * (h % 4):NT * (h % 4) + NT],
                                     eb[u % 2][:, NT * h:NT * h + NT], k.ident[0:NT, 0:NT])
                x.then_inc(s_T, 1)

            def weigh(i, q, u):
                n = unit(i, q, u)
                j, h = u // 2, u % 2
                pe.wait_ge(s_te, n + 1)
                pe.wait_ge(s_xa, n)
                pe.wait_ge(s_xd, n)
                for c in range(2):
                    x = pe.matmul(vb[:, c, 0:CW], vp[q][:, j, 8 * h + 4 * c:8 * h + 4 * c + 4, :],
                                  ets[u % 2][:, CW * c:CW * c + CW], start=True, stop=True)
                x.then_inc(s_PV, 1)

            def project(i, q):
                n = unit(i, q, 4)
                pe.wait_ge(s_xa, n)
                pe.wait_ge(s_xd, n)
                u = proj_use(i, q)
                b = fill(u)
                for j in range(2):
                    for c in range(CH):
                        x = pe.matmul(b[0:NT, D * j:D * j + D], oT[q][:, c, NT * j:NT * j + NT], wo[:, c, :],
                                      start=(c == 0), stop=(c == CH - 1))
                x.then_inc(s_full[u[0]], 1)

            def pair(i, q, nxt, v_use):
                ni, nq = after(i, q)
                drained(pe, v_use)
                pieces = {0: (HT,), 1: (Q0, Q1, K0), 2: (K1, V), 3: ()}
                for u in range(4):
                    if u < 3:
                        scores(i, q, u + 1)
                    elif nxt:
                        scores(ni, nq, 0, (use(i, q, K0), use(i, q, K1)))
                    for w in pieces[u] if nxt else ():
                        if w == Q0:
                            drained(pe, use(i, q, HT))
                        front(ni, nq, w, use(i, q, w))
                    turn(i, q, u)
                    weigh(i, q, u)
                project(i, q)

            def v_use(i):
                return V % 2, i * 7 + V // 2

            pe.wait_ge(s_w, 16 * (6 + 16 + 2))
            pe.wait_ge(s_z0, 4)
            for w in (HT, Q0, Q1, K0, K1, V):
                if w == Q0:
                    drained(pe, use0(HT))
                front(0, 0, w, use0(w))
            scores(0, 0, 0, (use0(K0), use0(K1)))
            pair(0, 0, True, v_use(0))
            pair(0, 1, True, use(0, 0, V))
            with pe.Fori(1, PAIRS // 2 - 1) as i:
                pair(i, 0, True, v_use(i))
                pair(i, 1, True, use(i, 0, V))
            pair(LAST // 2, 0, True, v_use(LAST // 2))
            pair(LAST // 2, 1, False, use(LAST // 2, 0, V))

        @block.scalar
        def _(act):
            def copy(dst, src):
                return act.activation(dst, src, ACT.Copy)

            def to_sb(dst, u):
                b = filled(act, u)
                copy(dst.rearrange("p c t -> p (c t)"), b[:, 0:2 * W2T]).then_inc(s_drained[u[0]], 1)

            def exps(i, q, u):
                act.wait_ge(s_sub, unit(i, q, u) + 1)
                act.activation(eb[u % 2][:], eb[u % 2][:], ACT.Exp, scale=HD ** -0.5).then_inc(s_exp, 1)

            def turned(i, q, u):
                act.wait_ge(s_T, unit(i, q, u) + 1)
                copy(ets[u % 2][:].rearrange("p (c t) -> p c t", c=2), tb[0:NT, :, 0:CW]).then_inc(s_te, 1)

            def out_heads(i, q, u):
                j, h = u // 2, u % 2
                act.wait_ge(s_PV, unit(i, q, u) + 1)
                for r in (0, 1):
                    x = copy(oT[q][HP * r:HP * r + HP, 2 * h:2 * h + 2, NT * j:NT * j + NT],
                             vb[HP * r:HP * r + HP, :, NT * r:NT * r + NT])
                x.then_inc(s_xa, 1)

            def pair(i, q, nxt):
                ni, nq = after(i, q)
                for u in range(4):
                    if nxt and u == 0:
                        to_sb(hT[nq][:], use(i, q, HT))
                    if nxt and u == 1:
                        to_sb(qT[nq][:, 0:2, :], use(i, q, Q0))
                        to_sb(qT[nq][:, 2:4, :], use(i, q, Q1))
                    if nxt and u == 2:
                        k_diag(act, copy, nq, K1, use(i, q, K1))
                    turned(i, q, u)
                    if u < 3:
                        exps(i, q, u + 1)
                    elif nxt:
                        exps(ni, nq, 0)
                    out_heads(i, q, u)

            to_sb(hT[0][:], use0(HT))
            to_sb(qT[0][:, 0:2, :], use0(Q0))
            to_sb(qT[0][:, 2:4, :], use0(Q1))
            k_diag(act, copy, 0, K1, use0(K1))
            exps(0, 0, 0)
            pair(0, 0, True)
            pair(0, 1, True)
            with act.Fori(1, PAIRS // 2 - 1) as i:
                pair(i, 0, True)
                pair(i, 1, True)
            pair(LAST // 2, 0, True)
            pair(LAST // 2, 1, False)

        @block.vector
        def _(dve):
            def ln_stats(i, q):
                for j in range(2):
                    x = dve.bn_stats(st[q][:, j, :], k.sample(i * 4 + (2 * q + j)))
                x.then_inc(s_st, 1)
                dve.wait_ge(s_st, i * 2 + (q + 1))
                dve.sem_inc(k.s_hold, 1)
                for j in range(2):
                    x = dve.bn_aggr(mv[q][:, j, :], st[q][:, j, :])
                x.then_inc(s_mv, 1)
                dve.wait_ge(s_mv, i * 2 + (q + 1))
                dve.tensor_scalar(rs[q][:], mv[q][:, :, 1], EPS, None, ALU.add).then_inc(s_ve, 1)

            def ln_apply(i, q):
                dve.wait_ge(s_rs, i * 2 + (q + 1))
                for j in range(2):
                    x = dve.tensor_scalar(hn[q][:, j, :], k.sample(i * 4 + (2 * q + j)), mv[q][:, j, 0:1],
                                          rs[q][:, j:j + 1], ALU.subtract, ALU.mult)
                x.then_inc(s_hn, 1)

            def less_max(i, q, u):
                n = unit(i, q, u)
                dve.wait_ge(s_S, n + 1)
                s = sc[0:NT, :, 0:CW].rearrange("p c (h t) -> p c h t", h=4)
                m = mx[u % 2][:].rearrange("p (c h) -> p c h", c=2)
                dve.tensor_reduce(m, s, X, ALU.max).then_inc(s_mx, 1)
                dve.wait_ge(s_mx, n + 1)
                if not (isinstance(n, int) and n < 2):
                    dve.wait_ge(s_T, n - 1)
                e = eb[u % 2][:].rearrange("p (c h t) -> p c h t", c=2, h=4)
                dve.tensor_tensor(e, s, m.unsqueeze(3).broadcast_to([NT, 2, 4, NT]), ALU.subtract).then_inc(s_sub, 1)

            def sums(i, q, u):
                n = unit(i, q, u)
                dve.wait_ge(s_exp, n + 1)
                dve.tensor_reduce(sm[u % 2][:], eb[u % 2][:].rearrange("p (h t) -> p h t", h=8), X,
                                  ALU.add).then_inc(s_sum, 1)
                dve.wait_ge(s_sum, n + 1)
                dve.reciprocal(rc[u % 2][:], sm[u % 2][:]).then_inc(s_rc, 1)

            def out_heads(i, q, u):
                j, h = u // 2, u % 2
                dve.wait_ge(s_PV, unit(i, q, u) + 1)
                for r in (2, 3):
                    x = dve.tensor_copy(oT[q][HP * r:HP * r + HP, 2 * h:2 * h + 2, NT * j:NT * j + NT],
                                        vb[HP * r:HP * r + HP, :, NT * r:NT * r + NT])
                x.then_inc(s_xd, 1)

            def v_pad(q, u):
                b = filled(dve, u)
                dve.tensor_copy(vp[q][:, :, :, 0:HD].rearrange("p j h e -> p (j h) e"),
                                b[0:NT, :].rearrange("p (g e) -> p g e", e=HD)).then_inc(s_drained[u[0]], 1)

            def add_proj(i, q):
                u = proj_use(i, q)
                b = filled(dve, u)
                h = k.samples(i * 4 + 2 * q, 2)
                dve.tensor_tensor(h, h, b[0:NT, :], ALU.add).then_inc(s_drained[u[0]], 1)

            def pair(i, q, nxt, ln):
                ni, nq = after(i, q)
                for u in range(4):
                    if u < 3:
                        less_max(i, q, u + 1)
                    elif nxt:
                        less_max(ni, nq, 0)
                    if nxt and u == 1:
                        k_diag(dve, dve.tensor_copy, nq, K0, use(i, q, K0))
                    if nxt and u == 2:
                        v_pad(nq, use(i, q, V))
                    if u < 3:
                        sums(i, q, u + 1)
                    elif nxt:
                        sums(ni, nq, 0)
                    out_heads(i, q, u)
                    if ln and u == 0:
                        ln_stats(i + 1, q)
                    if ln and u == 2:
                        ln_apply(i + 1, q)
                add_proj(i, q)

            ln_stats(0, 0)
            ln_apply(0, 0)
            ln_stats(0, 1)
            ln_apply(0, 1)
            k_diag(dve, dve.tensor_copy, 0, K0, use0(K0))
            v_pad(0, use0(V))
            less_max(0, 0, 0)
            sums(0, 0, 0)
            pair(0, 0, True, True)
            pair(0, 1, True, True)
            with dve.Fori(1, PAIRS // 2 - 1) as i:
                pair(i, 0, True, True)
                pair(i, 1, True, True)
            pair(LAST // 2, 0, True, False)
            pair(LAST // 2, 1, False, False)

        @block.gpsimd
        def _(pool):
            def ln_rstd(i, q):
                pool.wait_ge(s_ve, i * 2 + (q + 1))
                pool.tensor_tensor(rs[q][:], rs[q][:], k.mhalf[0:NT, 0:2], ALU.pow).then_inc(s_rs, 1)

            def norm(i, q, u):
                pool.wait_ge(s_rc, unit(i, q, u) + 1)
                e = eb[u % 2][:].rearrange("p (h t) -> p h t", h=8)
                pool.tensor_tensor(e, e, rc[u % 2][:].unsqueeze(2).broadcast_to([NT, 8, NT]),
                                   ALU.mult).then_inc(s_nrm, 1)

            def bias(i, q):
                drained(pool, proj_use(i, q))
                h = k.samples(i * 4 + 2 * q, 2)
                pool.tensor_tensor(h, h, bo[:].rearrange("p j d -> p (j d)"), ALU.add).then_inc(s_hb, 1)

            def pair(i, q, nxt, ln):
                ni, nq = after(i, q)
                for u in range(4):
                    if u < 3:
                        norm(i, q, u + 1)
                    elif nxt:
                        norm(ni, nq, 0)
                    if ln and u == 0:
                        ln_rstd(i + 1, q)
                bias(i, q)

            pool.memset(wqk[:], 0.0).then_inc(s_w0, 1)
            pool.memset(wo[:], 0.0).then_inc(s_w0, 1)
            ln_rstd(0, 0)
            ln_rstd(0, 1)
            for q in range(2):
                pool.memset(kd[q][:], 0.0).then_inc(s_z0, 1)
                pool.memset(vp[q][:], 0.0).then_inc(s_z0, 1)
            pool.wait_ge(s_w, 16 * (6 + 16 + 2))
            norm(0, 0, 0)
            pair(0, 0, True, True)
            pair(0, 1, True, True)
            with pool.Fori(1, PAIRS // 2 - 1) as i:
                pair(i, 0, True, True)
                pair(i, 1, True, True)
            pair(LAST // 2, 0, True, False)
            pair(LAST // 2, 1, False, False)


def route(nc, k, ins):
    G = 4
    with ExitStack() as ctx:
        sb = lambda n, s, d=F32: ctx.enter_context(nc.sbuf_tensor(n, s, d))
        used = []
        sem = lambda n: used.append(ctx.enter_context(nc.semaphore(n))) or used[-1]
        two = lambda n, s, d=F32: [sb(f"{n}{i}", s, d) for i in range(2)]
        wr = sb("rt_w", [128, 2, NE])
        tri = sb("rt_before", [NT, NT])
        ones = sb("rt_ones", [NT, NT])
        lane = sb("rt_lane", [NT, G, NE])
        lane_i = sb("rt_lane_int", [NT, G, NE], I32)
        st = two("rt_st", [NT, G, 6])
        mv = two("rt_mv", [NT, G, 2])
        rs = two("rt_rs", [NT, G])
        xm = two("rt_x", [NT, G, D])
        xT = two("rt_xT", [128, 2, G * NT])
        lg = sb("rt_logits", [NT, G, NE])
        m8 = sb("rt_max", [NT, G, NE])
        i8 = sb("rt_maxi", [NT, G, NE], U32)
        ix = sb("rt_expert", [NT, G])
        dl = two("rt_less", [NT, G, NE])
        oh = two("rt_onehot", [NT, G, NE])
        seen = two("rt_seen", [NT, G, NE])
        own = sb("rt_own", [NT, G, NE])
        rk = sb("rt_rank", [NT, G])
        kp = sb("rt_keep", [NT, G])
        ad = sb("rt_addr", [NT, G])
        sl = two("rt_slot", [NT, G], U32)
        se = sb("rt_sum", [NT, G])
        s_w, s_c, s_st, s_ve, s_rs, s_x = (sem(f"s_rt_{n}") for n in ("w", "const", "stats", "vareps", "rstd", "x"))
        s_T, s_xT, s_lg, s_ch, s_dl, s_e = (
            sem(f"s_rt_{n}") for n in ("turned", "xT", "logits", "step", "less", "exp"))
        s_oh, s_rk, s_sl = (sem(f"s_rt_{n}") for n in ("onehot", "rank", "slot"))
        s_sc = [sem(f"s_rt_scattered{i}") for i in range(2)]
        bk = k.bank
        GN = NB // G
        STEPS = 18
        block = ctx.enter_context(nc.Block())

        @block.sync
        def _(sp):
            sp.dma_start(wr[:], ins["L0_ffn_Wr"].rearrange("(c p) e -> p c e", p=128)).then_inc(s_w, 16)
            for e in range(2):
                expert_weights(sp, k, ins, e, e)
            for q in range(2):
                sp.wait_ge(s_sc[q], 16 * G * GN // 2)

        @block.tensor
        def _(pe):
            def group(i, q):
                n = i * 2 + q
                pe.wait_ge(s_x, n + 1)
                if not (isinstance(i, int) and i == 0 and q == 0):
                    pe.wait_ge(s_xT, n)
                for c in range(2):
                    for j in range(G):
                        x = pe.transpose(bk[c][:, NT * j:NT * j + NT], xm[q][:, j, 128 * c:128 * c + 128],
                                         k.ident[0:NT, 0:NT])
                x.then_inc(s_T, 1)
                pe.wait_ge(s_xT, n + 1)
                for j in range(G):
                    for c in range(2):
                        x = pe.matmul(bk[2 + q][0:NT, NE * j:NE * j + NE], xT[q][:, c, NT * j:NT * j + NT],
                                      wr[:, c, :], start=(c == 0), stop=(c == 1))
                x.then_inc(s_lg, 1)
                pe.wait_ge(s_oh, n + 1)
                o = bk[4 + q][0:NT, 0:G * NE]
                pe.matmul(o, tri[:], oh[q][:].rearrange("p g e -> p (g e)"), start=True, stop=False)
                pe.matmul(o, ones[:], seen[q][:].rearrange("p g e -> p (g e)"), start=False,
                          stop=True).then_inc(s_rk, 1)

            pe.wait_ge(s_w, 16)
            group(0, 0)
            group(0, 1)
            with pe.Fori(1, GN // 2) as i:
                group(i, 0)
                group(i, 1)

        @block.scalar
        def _(act):
            def group(i, q):
                n = i * 2 + q
                act.wait_ge(s_T, n + 1)
                act.activation(xT[q][:], k.ps[:, 0:2, 0:G * NT], ACT.Copy).then_inc(s_xT, 1)
                act.wait_ge(s_dl, n + 1)
                act.activation(dl[q][:], dl[q][:], ACT.Exp).then_inc(s_e, 1)

            group(0, 0)
            group(0, 1)
            with act.Fori(1, GN // 2) as i:
                group(i, 0)
                group(i, 1)

        @block.gpsimd
        def _(pool):
            def rstd(i, q):
                pool.wait_ge(s_ve, i * 2 + (q + 1))
                pool.tensor_tensor(rs[q][:], rs[q][:], k.mhalf[0:NT, 0:G], ALU.pow).then_inc(s_rs, 1)

            def scatter(i, q):
                pool.wait_ge(s_sl, i * 2 + (q + 1))
                pool.sem_inc(k.s_hold, 1)
                for j in range(G):
                    pool.indirect_dma_start(out=k.xd[:], out_offset=bass.IndirectOffsetOnAxis(sl[q][:, j:j + 1], 0),
                                            in_=xm[q][:, j, :], in_offset=None, bounds_check=NE * CAP - 1,
                                            oob_is_err=False).then_inc(s_sc[q], 16)

            pool.memset(ones[:], 1.0)
            pool.memset(tri[:], 1.0).then_inc(s_c, 1)
            pool.iota(lane_i[:], pattern=[[0, G], [1, NE]], base=0, channel_multiplier=0).then_inc(s_c, 1)
            pool.wait_ge(s_c, 2)
            pool.tensor_copy(lane[:], lane_i[:])
            pool.affine_select(out=tri[:], in_=tri[:], compare_op=ALU.is_gt, fill=0.0, base=0,
                               pattern=[[1, NT]], channel_multiplier=-1).then_inc(s_c, 1)
            pool.wait_ge(s_c, 3)
            pool.affine_select(out=tri[:], in_=tri[:], compare_op=ALU.not_equal, fill=1.0, base=-NPT,
                               pattern=[[0, NT]], channel_multiplier=1).then_inc(s_c, 1)
            pool.wait_ge(s_c, 4)
            pool.memset(tri[:, NPT:NPT + 1], 0.0).then_inc(s_c, 1)
            rstd(0, 0)
            rstd(0, 1)
            pool.wait_ge(k.s_xd0, k.xd0)
            with pool.Fori(0, GN // 2 - 1) as i:
                scatter(i, 0)
                rstd(i + 1, 0)
                scatter(i, 1)
                rstd(i + 1, 1)
            scatter(GN // 2 - 1, 0)
            scatter(GN // 2 - 1, 1)

        @block.vector
        def _(dve):
            def ln_stats(i, q):
                for j in range(G):
                    x = dve.bn_stats(st[q][:, j, :], k.sample(i * 8 + (4 * q + j)))
                x.then_inc(s_st, 1)
                dve.wait_ge(s_st, i * 4 + (2 * q + 1))
                dve.sem_inc(k.s_hold, 1)
                for j in range(G):
                    x = dve.bn_aggr(mv[q][:, j, :], st[q][:, j, :])
                x.then_inc(s_st, 1)
                dve.wait_ge(s_st, i * 4 + (2 * q + 2))
                dve.tensor_scalar(rs[q][:], mv[q][:, :, 1], EPS, None, ALU.add).then_inc(s_ve, 1)

            def ln_apply(i, q):
                dve.wait_ge(s_rs, i * 2 + (q + 1))
                if not (isinstance(i, int) and i == 0):
                    dve.wait_ge(s_sc[q], i * (16 * G))
                for j in range(G):
                    x = dve.tensor_scalar(xm[q][:, j, :], k.sample(i * 8 + (4 * q + j)), mv[q][:, j, 0:1],
                                          rs[q][:, j:j + 1], ALU.subtract, ALU.mult)
                x.then_inc(s_x, 1)

            def route_group(i, q):
                n = [0]

                def step(x):
                    n[0] += 1
                    x.then_inc(s_ch, 1)
                    dve.wait_ge(s_ch, i * (2 * STEPS) + (q * STEPS + n[0]))

                b4 = lambda v: v.unsqueeze(2).broadcast_to([NT, G, NE])
                dve.wait_ge(s_lg, i * 2 + (q + 1))
                step(dve.tensor_copy(lg[:].rearrange("p g e -> p (g e)"), bk[2 + q][0:NT, 0:G * NE]))
                dve.sem_inc(k.s_hold, 1)
                for j in range(G):
                    x = dve.max(m8[:, j, :], lg[:, j, :])
                step(x)
                dve.sem_inc(k.s_hold, 1)
                for j in range(G):
                    x = dve.max_index(i8[:, j, :], m8[:, j, :], lg[:, j, :])
                step(x)
                dve.tensor_tensor(dl[q][:], lg[:], b4(m8[:, :, 0]), ALU.subtract).then_inc(s_dl, 1)
                step(dve.tensor_copy(ix[:], i8[:, :, 0]))
                step(dve.tensor_tensor(oh[q][:], lane[:], b4(ix[:]), ALU.is_equal))
                prev, poh = seen[1 - q], oh[1 - q]
                if isinstance(i, int) and i == 0 and q == 0:
                    step(dve.memset(seen[q][:, 0, :], 0.0))
                else:
                    step(dve.tensor_tensor(seen[q][:, 0, :], prev[:, G - 1, :], poh[:, G - 1, :], ALU.add))
                for j in range(1, G):
                    x = dve.tensor_tensor(seen[q][:, j, :], seen[q][:, j - 1, :], oh[q][:, j - 1, :], ALU.add)
                    if j < G - 1:
                        step(x)
                x.then_inc(s_oh, 1)
                dve.wait_ge(s_rk, i * 2 + (q + 1))
                step(dve.tensor_tensor(own[:].rearrange("p g e -> p (g e)"),
                                       oh[q][:].rearrange("p g e -> p (g e)"),
                                       bk[4 + q][0:NT, 0:G * NE], ALU.mult))
                step(dve.tensor_reduce(rk[:], own[:], X, ALU.add))
                step(dve.tensor_scalar(kp[:], rk[:], float(CAP), None, ALU.is_lt))
                step(dve.scalar_tensor_tensor(ad[:], ix[:], float(CAP), rk[:], ALU.mult, ALU.add))
                step(dve.tensor_scalar(ad[:], ad[:], float(NE * CAP), None, ALU.subtract))
                step(dve.tensor_tensor(ad[:], ad[:], kp[:], ALU.mult))
                if not (isinstance(i, int) and i == 0):
                    dve.wait_ge(s_sc[q], i * (16 * G))
                x = dve.tensor_scalar(sl[q][:], ad[:], float(NE * CAP), None, ALU.add)
                x.then_inc(s_sl, 1)
                dve.wait_ge(s_sl, i * 2 + (q + 1))
                step(dve.tensor_copy(k.slot[:, bass.ds(i * 8 + 4 * q, G)], sl[q][:]))
                dve.wait_ge(s_e, i * 2 + (q + 1))
                step(dve.tensor_reduce(se[:], dl[q][:], X, ALU.add))
                step(dve.reciprocal(se[:], se[:]))
                step(dve.tensor_tensor(k.gate[:, bass.ds(i * 8 + 4 * q, G)], se[:], kp[:], ALU.mult))
                assert n[0] == STEPS, n[0]

            def groups(i, nxt):
                for q in range(2):
                    if q == 0:
                        ln_apply(i, 1)
                        if nxt:
                            ln_stats(i + 1, 0)
                    elif nxt:
                        ln_apply(i + 1, 0)
                        ln_stats(i + 1, 1)
                    route_group(i, q)

            ln_stats(0, 0)
            ln_stats(0, 1)
            ln_apply(0, 0)
            dve.wait_ge(s_c, 5)
            groups(0, True)
            with dve.Fori(1, GN // 2 - 1) as i:
                groups(i, True)
            groups(GN // 2 - 1, False)

    clear(nc, used)



def expert_weights(sp, k, ins, e, q):
    pick = lambda n: ins[n][bass.ds(e, 1), :, :].rearrange("a r c -> (a r) c")
    sp.dma_start(k.w1[q][:], pick("L0_ffn_W1").rearrange("(c p) f -> p c f", p=128)).then_inc(k.s_w1[q], 16)
    sp.dma_start(k.w2[q][:], pick("L0_ffn_W2").rearrange("(f p) d -> p f d", p=128)).then_inc(k.s_w2[q], 16)


def experts(nc, k, ins):
    R, J = 92, 3
    NF = FF // 128
    with ExitStack() as ctx:
        sb = lambda n, s, d=F32: ctx.enter_context(nc.sbuf_tensor(n, s, d))
        sem = lambda n: ctx.enter_context(nc.semaphore(n))
        two = lambda n, s, d=F32: [sb(f"{n}{i}", s, d) for i in range(2)]
        xe = two("ex_x", [R, J, D])
        xT = two("ex_xT", [128, 2, CAP])
        hid = two("ex_h", [128, NF, CAP])
        yT = two("ex_yT", [128, 2, CAP])
        ye = two("ex_y", [R, J, D])
        s_xe = [sem(f"s_ex_x{i}") for i in range(2)]
        s_T, s_xT, s_h, s_y, s_yT, s_B, s_ye = (
            sem(f"s_ex_{n}") for n in ("turned", "xT", "hidden", "y", "yT", "back", "y_sb"))
        s_hs = [sem("s_ex_h_by_act"), sem("s_ex_h_by_dve")]
        s_out = [sem(f"s_ex_out{i}") for i in range(2)]
        bk = k.bank
        LAST = NE // 2 - 1
        xd = k.xd.rearrange("(e j p) d -> e p j d", e=NE, j=J)
        yd = k.yd.rearrange("(e j p) d -> e p j d", e=NE, j=J)
        pick = lambda t, e: t[bass.ds(e, 1)].rearrange("a p j d -> (a p) j d")
        block = ctx.enter_context(nc.Block())

        @block.sync
        def _(sp):
            def load(i, q):
                if not (isinstance(i, int) and i == 0):
                    sp.wait_ge(s_T, i * 2 + (q - 1))
                sp.dma_start(xe[q][:], pick(xd, i * 2 + q)).then_inc(s_xe[q], 16)

            def weights(i, q):
                sp.wait_ge(s_y, i * 2 + (q - 1))
                expert_weights(sp, k, ins, i * 2 + q, q)

            def store(i, q):
                sp.wait_ge(s_ye, i * 2 + (q + 1))
                sp.dma_start(pick(yd, i * 2 + q), ye[q][:]).then_inc(s_out[q], 16)

            load(0, 0)
            load(0, 1)
            with sp.Fori(1, NE // 2) as i:
                for q in range(2):
                    load(i, q)
                    weights(i, q)
                    store(i - 1, q)
            store(LAST, 0)
            store(LAST, 1)
            for q in range(2):
                sp.wait_ge(s_out[q], 16 * (NE // 2))

        @block.tensor
        def _(pe):
            def turn(i, q):
                n = i * 2 + q
                pe.wait_ge(s_xe[q], i * 16 + 16)
                if not (isinstance(i, int) and i == 0 and q == 0):
                    pe.wait_ge(s_xT, n)
                for c in range(2):
                    for j in range(J):
                        x = pe.transpose(bk[c][:, R * j:R * j + R], xe[q][:, j, 128 * c:128 * c + 128],
                                         k.ident[0:R, 0:R])
                x.then_inc(s_T, 1)

            def expert(i, q, nxt):
                n = i * 2 + q
                pe.wait_ge(s_xT, n + 1)
                pe.wait_ge(k.s_w1[q], i * 16 + 16)
                for f in range(NF):
                    if not (isinstance(i, int) and i == 0 and q == 0 and f < 2):
                        pe.wait_ge(s_hs[f % 2], n * (NF // 2) + f // 2)
                    for c in range(2):
                        x = pe.matmul(bk[2 + f % 2][:, 0:CAP], k.w1[q][:, c, 128 * f:128 * f + 128],
                                      xT[q][:, c, :], start=(c == 0), stop=(c == 1))
                    x.then_inc(s_h, 1)
                if nxt:
                    turn(*((i, 1) if q == 0 else (i + 1, 0)))
                pe.wait_ge(k.s_w2[q], i * 16 + 16)
                for e in range(2):
                    pe.wait_ge(s_hs[e], n * (NF // 2) + NF // 2)
                if not (isinstance(i, int) and i == 0 and q == 0):
                    pe.wait_ge(s_yT, n)
                for c in range(2):
                    for f in range(NF):
                        x = pe.matmul(bk[4 + c][:, 0:CAP], k.w2[q][:, f, 128 * c:128 * c + 128], hid[q][:, f, :],
                                      start=(f == 0), stop=(f == NF - 1))
                x.then_inc(s_y, 1)

            def back(i, q):
                n = i * 2 + q
                pe.wait_ge(s_yT, n + 1)
                if not (isinstance(i, int) and i == 0 and q == 0):
                    pe.wait_ge(s_ye, n)
                for j in range(J):
                    for c in range(2):
                        o = D * (j % 2) + 128 * c
                        x = pe.transpose(bk[6 + j // 2][0:R, o:o + 128], yT[q][:, c, R * j:R * j + R], k.ident[:])
                x.then_inc(s_B, 1)

            turn(0, 0)
            expert(0, 0, True)
            back(0, 0)
            expert(0, 1, True)
            back(0, 1)
            with pe.Fori(1, LAST) as i:
                for q in range(2):
                    expert(i, q, True)
                    back(i, q)
            expert(LAST, 0, True)
            back(LAST, 0)
            expert(LAST, 1, False)
            back(LAST, 1)

        @block.scalar
        def _(act):
            def expert(i, q):
                n = i * 2 + q
                for f in range(0, NF, 2):
                    act.wait_ge(s_h, n * NF + f + 1)
                    act.activation(hid[q][:, f, :], bk[2][:, 0:CAP], ACT.Relu).then_inc(s_hs[0], 1)
                act.wait_ge(s_y, n + 1)
                act.activation(yT[q][:], k.ps[:, 4:6, 0:CAP], ACT.Copy).then_inc(s_yT, 1)

            with act.Fori(0, NE // 2) as i:
                expert(i, 0)
                expert(i, 1)

        @block.vector
        def _(dve):
            def rows(i, q):
                dve.wait_ge(s_T, i * 2 + (q + 1))
                dve.tensor_copy(xT[q][:], k.ps[:, 0:2, 0:CAP]).then_inc(s_xT, 1)

            def expert(i, q, nxt):
                n = i * 2 + q
                for f in range(1, NF, 2):
                    dve.wait_ge(s_h, n * NF + f + 1)
                    dve.tensor_scalar(hid[q][:, f, :], bk[3][:, 0:CAP], 0.0, None, ALU.max).then_inc(s_hs[1], 1)
                if nxt:
                    rows(*((i, 1) if q == 0 else (i + 1, 0)))
                dve.wait_ge(s_B, n + 1)
                if not (isinstance(i, int) and i == 0):
                    dve.wait_ge(s_out[q], i * 16)
                dve.tensor_copy(ye[q][:, 0:2, :].rearrange("p j d -> p (j d)"), bk[6][0:R, :])
                dve.tensor_copy(ye[q][:, 2, :], bk[7][0:R, 0:D]).then_inc(s_ye, 1)

            rows(0, 0)
            expert(0, 0, True)
            expert(0, 1, True)
            with dve.Fori(1, LAST) as i:
                expert(i, 0, True)
                expert(i, 1, True)
            expert(LAST, 0, True)
            expert(LAST, 1, False)


def combine(nc, k, ins):
    with ExitStack() as ctx:
        sb = lambda n, s, d=F32: ctx.enter_context(nc.sbuf_tensor(n, s, d))
        sem = lambda n: ctx.enter_context(nc.semaphore(n))
        RING = 4
        yg = [sb(f"cb_y{i}", [NT, D]) for i in range(RING)]
        sl = [sb(f"cb_slot{i}", [NT, RING], U32) for i in range(2)]
        s_z, s_sl, s_h = sem("s_cb_zeroed"), sem("s_cb_slot"), sem("s_cb_added")
        s_y = [sem(f"s_cb_y{i}") for i in range(RING)]
        block = ctx.enter_context(nc.Block())
        N = NB // RING

        @block.sync
        def _(sp):
            tied_weights(sp, k, ins)
            sp.wait_ge(k.s_wl, 16 * k.WL_LOADS)

        @block.gpsimd
        def _(pool):
            for r in range(RING):
                pool.memset(yg[r][:], 0.0).then_inc(s_z, 1)
            pool.wait_ge(s_z, RING)

            def group(i, q):
                if not (isinstance(i, int) and i == 0 and q == 0):
                    pool.wait_ge(s_h, i * (2 * RING) + q * RING - RING + 1)
                pool.tensor_copy(sl[q][:], k.slot[:, bass.ds(i * (2 * RING) + q * RING, RING)]).then_inc(s_sl, 1)
                pool.wait_ge(s_sl, i * 2 + (q + 1))
                pool.sem_inc(k.s_hold, 1)
                for r in range(RING):
                    if not (isinstance(i, int) and i == 0 and q == 0):
                        pool.wait_ge(s_h, i * (2 * RING) + q * RING - RING + r + 1)
                        pool.sem_inc(k.s_hold, 1)
                    pool.indirect_dma_start(out=yg[r][:], out_offset=None, in_=k.yd[:],
                                            in_offset=bass.IndirectOffsetOnAxis(sl[q][:, r:r + 1], 0),
                                            bounds_check=NE * CAP - 1, oob_is_err=False).then_inc(s_y[r], 16)

            group(0, 0)
            group(0, 1)
            with pool.Fori(1, N // 2) as i:
                group(i, 0)
                group(i, 1)

        @block.vector
        def _(dve):
            with dve.Fori(0, N) as i:
                for r in range(RING):
                    dve.wait_ge(s_y[r], i * 16 + 16)
                    h = k.sample(i * RING + r)
                    dve.scalar_tensor_tensor(h, yg[r][:], k.gate[:, bass.ds(i * RING + r, 1)], h,
                                             ALU.mult, ALU.add).then_inc(s_h, 1)


def tied_attention(nc, k, ins):
    with ExitStack() as ctx:
        sb = lambda n, s, d=F32: ctx.enter_context(nc.sbuf_tensor(n, s, d))
        sem = lambda n: ctx.enter_context(nc.semaphore(n))
        two = lambda n, s, d=F32: [sb(f"{n}{i}", s, d) for i in range(2)]
        st = two("ta_st", [NT, 2, 6])
        mv = two("ta_mv", [NT, 2, 2])
        rs = two("ta_rs", [NT, 2])
        xn = two("ta_x", [NT, 2, D])
        xp = two("ta_xpad", [NT, 2, NH, HP])
        yT = two("ta_yT", [128, 2, CH, NT])
        yd = two("ta_ydiag", [128, 2, CH, CW])
        eb = two("ta_e", [NT, HALF])
        sm = two("ta_sum", [NT, 8])
        rc = two("ta_rc", [NT, 8])
        ats = two("ta_at", [NT, HALF])
        oT = two("ta_oT", [128, NH, 2, W2T])
        wT = two("ta_wT", [128, 2, W2T])
        s_z0 = sem("s_ta_zeroed")
        s_st, s_mv, s_ve, s_rs, s_xn, s_xp = (sem(f"s_ta_{n}") for n in ("stats", "mv", "vareps", "rstd", "x", "xpad"))
        s_F = [sem(f"s_ta_front{j}") for j in range(2)]
        s_yT = [sem(f"s_ta_yT{j}") for j in range(2)]
        s_yd = [sem(f"s_ta_ydiag{j}") for j in range(2)]
        s_S, s_exp, s_sum, s_rc, s_nrm, s_T, s_at = (
            sem(f"s_ta_{n}") for n in ("scores", "exp", "sum", "recip", "norm", "turned", "at"))
        s_av = [sem(f"s_ta_av{c}") for c in range(2)]
        s_ax = [sem("s_ta_av_by_act"), sem("s_ta_av_by_dve")]
        s_W = [sem(f"s_ta_w{e}") for e in range(2)]
        s_wT = [sem(f"s_ta_wT{e}") for e in range(2)]
        s_B, s_add = sem("s_ta_back"), sem("s_ta_added")
        sc = k.ps[:, 0:2, :]
        tb = k.ps[:, 2:4, :]
        vb = [k.bank[4], k.bank[5]]
        wb = [k.bank[6], k.bank[7]]
        HALVES = PAIRS // 2
        first = lambda i, q: isinstance(i, int) and i == 0 and q == 0
        pr = lambda i, q: i * 2 + q
        after = lambda i, q: (i, 1) if q == 0 else (i + 1, 0)
        before = lambda i, q: (i, 0) if q == 1 else (i - 1, 1)

        def unit(i, q, u):
            return i * 8 + (4 * q + u)

        def all_pairs(eng, step):
            step(0, 0, True, False, False)
            step(0, 1, True, True, False)
            with eng.Fori(1, HALVES - 1) as i:
                step(i, 0, True, True, True)
                step(i, 1, True, True, True)
            step(HALVES - 1, 0, True, True, True)
            step(HALVES - 1, 1, False, True, True)

        block = ctx.enter_context(nc.Block())

        @block.tensor
        def _(pe):
            def front(i, q, j):
                pe.wait_ge(s_xp, pr(i, q) + 1)
                for c in range(CH):
                    x = pe.transpose(wb[1 - j][:, NT * c:NT * c + NT],
                                     xp[q][:, j, 4 * c:4 * c + 4, :].rearrange("p h e -> p (h e)"),
                                     k.ident[0:NT, 0:NT])
                x.then_inc(s_F[j], 1)

            def scores(i, q, u):
                j, h = u // 2, u % 2
                if h == 0:
                    pe.wait_ge(s_yd[j], pr(i, q) + 1)
                if not (first(i, q) and u == 0):
                    pe.wait_ge(s_exp, unit(i, q, u))
                for c in range(2):
                    x = pe.matmul(sc[0:NT, c, 0:CW], yT[q][:, j, 2 * h + c, :], yd[q][:, j, 2 * h + c, :],
                                  start=True, stop=True)
                x.then_inc(s_S, 1)

            def turn(i, q, u):
                n = unit(i, q, u)
                pe.wait_ge(s_nrm, n + 1)
                if not (first(i, q) and u == 0):
                    pe.wait_ge(s_at, n)
                for h in range(8):
                    x = pe.transpose(tb[0:NT, h // 4, NT * (h % 4):NT * (h % 4) + NT],
                                     eb[u % 2][:, NT * h:NT * h + NT], k.ident[0:NT, 0:NT])
                x.then_inc(s_T, 1)

            def weigh(i, q, u, c):
                n = unit(i, q, u)
                if c == 0:
                    pe.wait_ge(s_at, n + 1)
                for m in range(2):
                    if not (first(i, q) and u == 0 and c == 0):
                        pe.wait_ge(s_ax[m], n * 2 + c)
                    pe.matmul(vb[m][:, 0:CW], xn[q][:, u // 2, 128 * c:128 * c + 128],
                              ats[u % 2][:, CW * m:CW * m + CW], start=True, stop=True).then_inc(s_av[m], 1)

            def times_w(i, q, u, part):
                e = u // 2
                lo = 16 * (u % 2) + 8 * part
                for t in range(lo, lo + 8):
                    x = pe.matmul(wb[e][:, 0:W2T], k.wl[:, t // 2, t % 2, 128 * e:128 * e + 128],
                                  oT[q][:, t // 2, t % 2, :], start=(t == 0), stop=(t == 31))
                if lo == 24:
                    x.then_inc(s_W[e], 1)

            def back(i, q):
                for e in range(2):
                    pe.wait_ge(s_wT[e], pr(i, q) + 1)
                for j in range(2):
                    for e in range(2):
                        o = D * j + 128 * e
                        x = pe.transpose(wb[1][0:NT, o:o + 128], wT[q][:, e, NT * j:NT * j + NT], k.ident[:])
                x.then_inc(s_B, 1)

            def product_half(i, q, u, part):
                if part == 0 and u == 0:
                    for m in range(2):
                        pe.wait_ge(s_ax[m], unit(i, q, 4) * 2)
                    if not (isinstance(i, int) and i == HALVES - 1 and q == 1):
                        pe.wait_ge(s_yT[1], pr(i, q) + 2)
                if part == 0 and u == 2 and not (isinstance(i, int) and i == HALVES - 1 and q == 1):
                    if not (isinstance(i, int) and i == HALVES - 1 and q == 0):
                        pe.wait_ge(s_yT[0], pr(i, q) + 3)
                    else:
                        pe.wait_ge(s_add, pr(i, q) - 0)
                times_w(i, q, u, part)

            def step(i, q, ahead, w, back_):
                ni, nq = after(i, q)
                bi, bq = before(i, q)
                for u in range(4):
                    if u < 3:
                        scores(i, q, u + 1)
                    elif ahead:
                        scores(ni, nq, 0)
                    if back_ and u == 0:
                        back(i - 1, q)
                    if ahead and u == 1:
                        if back_:
                            pe.wait_ge(s_add, pr(i, q) - 1)
                        front(ni, nq, 0)
                    if w:
                        product_half(bi, bq, u, 0)
                    turn(i, q, u)
                    if ahead and u == 2:
                        if w:
                            pe.wait_ge(s_wT[0], pr(bi, bq) + 1)
                        front(ni, nq, 1)
                    weigh(i, q, u, 0)
                    if w:
                        times_w(bi, bq, u, 1)
                    weigh(i, q, u, 1)

            pe.wait_ge(k.s_wl, 16 * k.WL_LOADS)
            front(0, 0, 0)
            front(0, 0, 1)
            scores(0, 0, 0)
            all_pairs(pe, step)
            L = HALVES - 1
            back(L, 0)
            for u in range(4):
                if u == 0:
                    for m in range(2):
                        pe.wait_ge(s_ax[m], unit(L, 1, 4) * 2)
                if u == 2:
                    pe.wait_ge(s_add, PAIRS - 1)
                times_w(L, 1, u, 0)
                times_w(L, 1, u, 1)
            back(L, 1)

        @block.scalar
        def _(act):
            def copy(dst, src):
                return act.activation(dst, src, ACT.Copy)

            def turned_tokens(i, q, j):
                act.wait_ge(s_F[j], pr(i, q) + 1)
                copy(yT[q][:, j].rearrange("p c t -> p (c t)"), wb[1 - j][:, 0:CW]).then_inc(s_yT[j], 1)

            def exps(i, q, u):
                act.wait_ge(s_S, unit(i, q, u) + 1)
                copy_out = eb[u % 2][:].rearrange("p (c t) -> p c t", c=2)
                act.activation(copy_out, sc[0:NT, :, 0:CW], ACT.Exp, scale=HD ** -0.5).then_inc(s_exp, 1)

            def turned(i, q, u):
                act.wait_ge(s_T, unit(i, q, u) + 1)
                copy(ats[u % 2][:].rearrange("p (c t) -> p c t", c=2), tb[0:NT, :, 0:CW]).then_inc(s_at, 1)

            def values(i, q, u, c):
                act.wait_ge(s_av[0], unit(i, q, u) * 2 + (c + 1))
                j, h = u // 2, u % 2
                copy(oT[q][:, 8 * h:8 * h + 4, c, NT * j:NT * j + NT],
                     vb[0][:, 0:CW].rearrange("p (h t) -> p h t", h=4)).then_inc(s_ax[0], 1)

            def product(i, q, e):
                act.wait_ge(s_W[e], pr(i, q) + 1)
                copy(wT[q][:, e, :], wb[e][:, 0:W2T]).then_inc(s_wT[e], 1)

            def step(i, q, ahead, w, back_):
                ni, nq = after(i, q)
                bi, bq = before(i, q)
                for u in range(4):
                    if u < 3:
                        exps(i, q, u + 1)
                    elif ahead:
                        exps(ni, nq, 0)
                    if ahead and u == 1:
                        turned_tokens(ni, nq, 0)
                    turned(i, q, u)
                    if w and u == 2:
                        product(bi, bq, 0)
                    if ahead and u == 2:
                        turned_tokens(ni, nq, 1)
                    values(i, q, u, 0)
                    values(i, q, u, 1)
                if w:
                    product(bi, bq, 1)

            turned_tokens(0, 0, 0)
            turned_tokens(0, 0, 1)
            exps(0, 0, 0)
            all_pairs(act, step)
            product(HALVES - 1, 1, 0)
            product(HALVES - 1, 1, 1)

        @block.vector
        def _(dve):
            def ln_stats(i, q):
                for j in range(2):
                    x = dve.bn_stats(st[q][:, j, :], k.sample(i * 4 + (2 * q + j)))
                x.then_inc(s_st, 1)
                dve.wait_ge(s_st, pr(i, q) + 1)
                dve.sem_inc(k.s_hold, 1)
                for j in range(2):
                    x = dve.bn_aggr(mv[q][:, j, :], st[q][:, j, :])
                x.then_inc(s_mv, 1)
                dve.wait_ge(s_mv, pr(i, q) + 1)
                dve.tensor_scalar(rs[q][:], mv[q][:, :, 1], EPS, None, ALU.add).then_inc(s_ve, 1)

            def ln_apply(i, q):
                dve.wait_ge(s_rs, pr(i, q) + 1)
                for j in range(2):
                    x = dve.tensor_scalar(xn[q][:, j, :], k.sample(i * 4 + (2 * q + j)), mv[q][:, j, 0:1],
                                          rs[q][:, j:j + 1], ALU.subtract, ALU.mult)
                x.then_inc(s_xn, 1)

            def sums(i, q, u):
                n = unit(i, q, u)
                dve.wait_ge(s_exp, n + 1)
                dve.tensor_reduce(sm[u % 2][:], eb[u % 2][:].rearrange("p (h t) -> p h t", h=8), X,
                                  ALU.add).then_inc(s_sum, 1)
                dve.wait_ge(s_sum, n + 1)
                dve.reciprocal(rc[u % 2][:], sm[u % 2][:]).then_inc(s_rc, 1)

            def values(i, q, u, c):
                dve.wait_ge(s_av[1], unit(i, q, u) * 2 + (c + 1))
                j, h = u // 2, u % 2
                dve.tensor_copy(oT[q][:, 8 * h + 4:8 * h + 8, c, NT * j:NT * j + NT],
                                vb[1][:, 0:CW].rearrange("p (h t) -> p h t", h=4)).then_inc(s_ax[1], 1)

            def add(i, q):
                dve.wait_ge(s_B, pr(i, q) + 1)
                h = k.samples(i * 4 + 2 * q, 2)
                dve.tensor_tensor(h, h, wb[1][0:NT, :], ALU.add).then_inc(s_add, 1)

            def step(i, q, ahead, w, back_):
                ni, nq = after(i, q)
                for u in range(4):
                    if u < 3:
                        sums(i, q, u + 1)
                    elif ahead:
                        sums(ni, nq, 0)
                    if ahead and u == 0:
                        ln_apply(ni, nq)
                    if back_ and u == 0:
                        add(i - 1, q)
                    if u == 2 and ahead and not (isinstance(i, int) and i == HALVES - 1):
                        ln_stats(i + 1, q)
                    values(i, q, u, 0)
                    values(i, q, u, 1)

            ln_stats(0, 0)
            ln_apply(0, 0)
            ln_stats(0, 1)
            sums(0, 0, 0)
            all_pairs(dve, step)
            add(HALVES - 1, 0)
            add(HALVES - 1, 1)

        @block.gpsimd
        def _(pool):
            def rstd(i, q):
                pool.wait_ge(s_ve, pr(i, q) + 1)
                pool.tensor_tensor(rs[q][:], rs[q][:], k.mhalf[0:NT, 0:2], ALU.pow).then_inc(s_rs, 1)

            def pad(i, q):
                pool.wait_ge(s_xn, pr(i, q) + 1)
                pool.sem_inc(k.s_hold, 1)
                pool.tensor_copy(xp[q][:, :, :, 0:HD].rearrange("p j h e -> p (j h) e"),
                                 xn[q][:].rearrange("p j (h e) -> p (j h) e", e=HD)).then_inc(s_xp, 1)

            def diagonal(i, q, j, sem, value):
                pool.wait_ge(sem, value)
                pool.wait_ge(s_yT[j], pr(i, q) + 1)
                pool.sem_inc(k.s_hold, 1)
                for r in range(4):
                    x = pool.tensor_copy(yd[q][HP * r:HP * r + HP, j, :, NT * r:NT * r + NT],
                                         yT[q][HP * r:HP * r + HP, j, :, :])
                x.then_inc(s_yd[j], 1)
                pool.wait_ge(s_yd[j], pr(i, q) + 1)

            def norm(i, q, u):
                pool.wait_ge(s_rc, unit(i, q, u) + 1)
                e = eb[u % 2][:].rearrange("p (h t) -> p h t", h=8)
                pool.tensor_tensor(e, e, rc[u % 2][:].unsqueeze(2).broadcast_to([NT, 8, NT]),
                                   ALU.mult).then_inc(s_nrm, 1)

            def step(i, q, ahead, w, back_):
                ni, nq = after(i, q)
                for u in range(4):
                    if u < 3:
                        norm(i, q, u + 1)
                    elif ahead:
                        norm(ni, nq, 0)
                    if ahead and u == 0:
                        pad(ni, nq)
                    if ahead and u == 1:
                        diagonal(ni, nq, 0, s_nrm, unit(i, q, 3))
                    if ahead and u == 2:
                        diagonal(ni, nq, 1, s_nrm, unit(i, q, 4))
                        if not (isinstance(i, int) and i == HALVES - 1):
                            rstd(i + 1, q)

            for q in range(2):
                pool.memset(xp[q][:], 0.0).then_inc(s_z0, 1)
                pool.memset(yd[q][:], 0.0).then_inc(s_z0, 1)
            pool.wait_ge(s_z0, 4)
            rstd(0, 0)
            pad(0, 0)
            rstd(0, 1)
            diagonal(0, 0, 0, s_rs, 2)
            diagonal(0, 0, 1, s_yd[0], 1)
            norm(0, 0, 0)
            all_pairs(pool, step)


def tied_weights(sp, k, ins):
    w = ins["L1_attn_weight"].rearrange("(h c p) e -> p h c e", c=2, p=128)
    k.WL_LOADS = 4
    for g in range(4):
        sp.dma_start(k.wl[:, 4 * g:4 * g + 4], w[:, 4 * g:4 * g + 4]).then_inc(k.s_wl, 16)


QMAX = 127.0
ROUND = 1.5 * 2.0 ** 23
FI = 704
MI = (FI + 127) // 128
PART = [min(128, FI - 128 * m) for m in range(MI)]


def mlp(nc, k, ins, out):
    G = 4
    GN = NB // G
    GT = G * NT
    with ExitStack() as ctx:
        sb = lambda n, s, d=F32: ctx.enter_context(nc.sbuf_tensor(n, s, d))
        sem = lambda n: ctx.enter_context(nc.semaphore(n))
        two = lambda n, s, d=F32: [sb(f"{n}{i}", s, d) for i in range(2)]
        identb = sb("ml_ident", [128, 128], BF16)
        wgT = sb("ml_wgT", [128, 2, FI], BF16)
        wuT = sb("ml_wuT", [128, 2, FI], BF16)
        wdT = sb("ml_wdT", [128, MI, D], BF16)
        sg = sb("ml_sg", [128, MI])
        su = sb("ml_su", [128, MI])
        sd = sb("ml_sd", [128, 2])
        srow = sb("ml_srow", [NT, D])
        clip = sb("ml_clip", [128, 2])
        sig = sb("ml_sig", [128, 2])
        amx = sb("ml_amx", [128, NB])
        gmx = sb("ml_gmx", [128, 1])
        amax = sb("ml_amax", [128, 1])
        sx = sb("ml_sx", [128, 1])
        ix = sb("ml_ix", [128, 1])
        xn = sb("ml_x", [NT, NB, D])
        hh = sb("ml_h", [128, MI, NB * NT])
        hmx = sb("ml_hmx", [128, GN * MI])
        sh = sb("ml_sh", [128, 1])
        ih = sb("ml_ih", [128, 1])
        bk = k.bank
        bkb = [b.bitcast(BF16) for b in bk]

        with ExitStack() as c2:
            wg = c2.enter_context(nc.sbuf_tensor("ml_wg", [128, MI, D], F32))
            wu = c2.enter_context(nc.sbuf_tensor("ml_wu", [128, MI, D], F32))
            wd = c2.enter_context(nc.sbuf_tensor("ml_wd", [128, 2, FI], F32))
            wgb = c2.enter_context(nc.sbuf_tensor("ml_wgb", [128, MI, D], BF16))
            wub = c2.enter_context(nc.sbuf_tensor("ml_wub", [128, MI, D], BF16))
            wdb = c2.enter_context(nc.sbuf_tensor("ml_wdb", [128, 2, FI], BF16))
            inv = c2.enter_context(nc.sbuf_tensor("ml_inv", [128, 2 * MI + 2], F32))
            s_w, s_z, s_id, s_ch, s_q, s_T, s_e, s_clip = (
                sem(f"s_mw_{n}") for n in ("loaded", "zero", "ident", "step", "whole", "turned", "sb", "clip"))
            with nc.Block() as block:
                @block.sync
                def _(sp):
                    sp.wait_ge(s_z, 2)
                    for w, n in ((wg, "w_gate"), (wu, "w_up")):
                        src = ins[f"L1_ffn_{n}"]
                        sp.dma_start(w[:, 0:MI - 1, :], src[0:128 * (MI - 1), :]
                                     .rearrange("(m p) d -> p m d", p=128)).then_inc(s_w, 16)
                        sp.dma_start(w[0:PART[-1], MI - 1, :], src[128 * (MI - 1):FI, :]).then_inc(s_w, 16)
                    sp.dma_start(wd[:], ins["L1_ffn_w_down"].rearrange("(c p) i -> p c i", p=128)).then_inc(s_w, 16)
                    for j, n in enumerate(("x", "down")):
                        sp.dma_start(clip[:, j:j + 1], ins[f"L1_ffn_clip_{n}"].rearrange("(a b) -> a b", a=1)
                                     .broadcast_to([128, 1])).then_inc(s_clip, 16)

                @block.gpsimd
                def _(pool):
                    pool.memset(wg[:, MI - 1, :], 1.0).then_inc(s_z, 1)
                    pool.memset(wu[:, MI - 1, :], 1.0).then_inc(s_z, 1)
                    pool.tensor_copy(identb[:], k.ident[:]).then_inc(s_id, 1)

                @block.vector
                def _(dve):
                    n = [0]

                    def step(x):
                        n[0] += 1
                        x.then_inc(s_ch, 1)
                        dve.wait_ge(s_ch, n[0])

                    dve.wait_ge(s_w, 80)
                    for w, s in ((wg, sg), (wu, su), (wd, sd)):
                        x = dve.tensor_reduce(s[:], w[:], X, ALU.max, apply_absolute_value=True)
                    step(x)
                    for s in (sg, su, sd):
                        x = dve.tensor_scalar(s[:], s[:], 1.0 / QMAX, None, ALU.mult)
                    step(x)
                    dve.reciprocal(inv[:, 0:MI], sg[:])
                    dve.reciprocal(inv[:, MI:2 * MI], su[:])
                    step(dve.reciprocal(inv[:, 2 * MI:2 * MI + 2], sd[:]))
                    for w, o, m in ((wg, 0, MI), (wu, MI, MI), (wd, 2 * MI, 2)):
                        for j in range(m):
                            x = dve.tensor_scalar(w[:, j, :], w[:, j, :], inv[:, o + j:o + j + 1], ROUND,
                                                  ALU.mult, ALU.add)
                    step(x)
                    for w, b in ((wg, wgb), (wu, wub), (wd, wdb)):
                        dve.tensor_scalar(b[:].rearrange("p m d -> p (m d)"), w[:].rearrange("p m d -> p (m d)"),
                                          ROUND, QMAX, ALU.subtract, ALU.min).then_inc(s_q, 1)

                @block.tensor
                def _(pe):
                    pe.wait_ge(s_id, 1)
                    pe.wait_ge(s_q, 3)
                    for w, b, o in ((wg, wgb, 0), (wu, wub, 2)):
                        for c in range(2):
                            for m in range(MI):
                                x = pe.transpose(bkb[o + c][:, 128 * m:128 * m + PART[m]],
                                                 b[0:PART[m], m, 128 * c:128 * c + 128],
                                                 identb[0:PART[m], 0:PART[m]])
                        x.then_inc(s_T, 1)
                    for m in range(MI):
                        for c in range(2):
                            o = D * (m % 4) + 128 * c
                            x = pe.transpose(bkb[4 + m // 4][0:PART[m], o:o + 128],
                                             wdb[:, c, 128 * m:128 * m + PART[m]], identb[:])
                    x.then_inc(s_T, 1)
                    for c in range(2):
                        x = pe.matmul(bk[6][0:NT, 128 * c:128 * c + 128], sd[:, c:c + 1].broadcast_to([128, NT]),
                                      k.ident[:], start=True, stop=True)
                    x.then_inc(s_T, 1)

                @block.scalar
                def _(act):
                    act.wait_ge(s_clip, 32)
                    act.activation(sig[:], clip[:], ACT.Sigmoid)
                    for t, (w, o) in enumerate(((wgT, 0), (wuT, 2))):
                        act.wait_ge(s_T, t + 1)
                        for c in range(2):
                            act.activation(w[:, c, :], bkb[o + c][:, 0:FI], ACT.Copy)
                    act.wait_ge(s_T, 3)
                    act.activation(wdT[:, 0:4, :].rearrange("p m d -> p (m d)"), bkb[4][:, 0:4 * D], ACT.Copy)
                    act.activation(wdT[:, 4, :], bkb[5][:, 0:D], ACT.Copy)
                    act.activation(wdT[0:PART[-1], 5, :], bkb[5][0:PART[-1], D:2 * D], ACT.Copy)
                    act.wait_ge(s_T, 4)
                    act.activation(srow[:], bk[6][0:NT, 0:D], ACT.Copy)

        with ExitStack() as c2:
            st = c2.enter_context(nc.sbuf_tensor("ml_st", [NT, NB, 6], F32))
            mv = c2.enter_context(nc.sbuf_tensor("ml_mv", [NT, NB, 2], F32))
            rs = c2.enter_context(nc.sbuf_tensor("ml_rs", [NT, NB], F32))
            s_z, s_st, s_mv, s_ve, s_rs, s_x, s_mx, s_g, s_gd = (
                sem(f"s_ml_{n}") for n in
                ("zero", "stats", "meanvar", "vareps", "rstd", "x", "max", "gmax", "scale"))
            with nc.Block() as block:
                @block.vector
                def _(dve):
                    with dve.Fori(0, NB) as b:
                        dve.bn_stats(st[:, bass.ds(b, 1), :].rearrange("p a s -> p (a s)"), k.sample(b)).then_inc(s_st, 1)
                    dve.wait_ge(s_st, NB)
                    for b in range(NB):
                        x = dve.bn_aggr(mv[:, b, :], st[:, b, :])
                    x.then_inc(s_mv, 1)
                    dve.wait_ge(s_mv, 1)
                    dve.tensor_scalar(rs[:], mv[:, :, 1], EPS, None, ALU.add).then_inc(s_ve, 1)
                    dve.memset(amx[:], 0.0).then_inc(s_z, 1)
                    dve.wait_ge(s_z, 1)
                    dve.wait_ge(s_rs, NB // 8)
                    with dve.Fori(0, NB) as b:
                        x1 = xn[:, bass.ds(b, 1), :].rearrange("p a d -> p (a d)")
                        dve.tensor_scalar(x1, k.sample(b), mv[:, bass.ds(b, 1), 0], rs[:, bass.ds(b, 1)],
                                          ALU.subtract, ALU.mult).then_inc(s_x, 1)
                    with dve.Fori(0, GN) as g:
                        dve.wait_ge(s_x, g * G + G)
                        dve.tensor_reduce(amx[0:NT, bass.ds(g * G, G)], xn[:, bass.ds(g * G, G), :], X, ALU.max,
                                          apply_absolute_value=True).then_inc(s_mx, 1)
                    dve.wait_ge(s_mx, GN)
                    dve.tensor_reduce(gmx[:], amx[:], X, ALU.max).then_inc(s_g, 1)
                    dve.wait_ge(s_gd, 1)
                    dve.scalar_tensor_tensor(sx[:], amax[:], 1.0 / QMAX, sig[:, 0:1], ALU.mult, ALU.mult).then_inc(s_g, 1)
                    dve.wait_ge(s_g, 2)
                    dve.reciprocal(ix[:], sx[:])
                    dve.tensor_scalar(sg[:], sg[:], sx[:, 0:1], None, ALU.mult)
                    dve.tensor_scalar(su[:], su[:], sx[:, 0:1], None, ALU.mult)

                @block.gpsimd
                def _(pool):
                    pool.wait_ge(s_ve, 1)
                    for j in range(NB // 8):
                        v = rs[:, 8 * j:8 * j + 8]
                        pool.tensor_tensor(v, v, k.mhalf[0:NT, :], ALU.pow).then_inc(s_rs, 1)
                    pool.wait_ge(s_g, 1)
                    pool.partition_all_reduce(amax[:], gmx[:], 128, bass.bass_isa.ReduceOp.max).then_inc(s_gd, 1)

        with ExitStack() as c2:
            xq = [c2.enter_context(nc.sbuf_tensor(f"ml_xq{i}", [NT, G, D], F32)) for i in range(2)]
            xb = [c2.enter_context(nc.sbuf_tensor(f"ml_xb{i}", [NT, G, D], BF16)) for i in range(2)]
            xT = [c2.enter_context(nc.sbuf_tensor(f"ml_xT{i}", [128, 2, GT], BF16)) for i in range(2)]
            gt = [c2.enter_context(nc.sbuf_tensor(f"ml_gt{i}", [128, GT], F32)) for i in range(2)]
            magic = c2.enter_context(nc.sbuf_tensor("ml_magic", [128, 1], F32))
            s_z, s_q1, s_q2, s_xb, s_T, s_xT, s_gate, s_up, s_gt, s_h, s_mx, s_g, s_gd = (
                sem(f"s_mg_{n}") for n in ("zero", "q1", "q2", "xb", "turned", "xT", "gate", "up", "silu", "h", "max",
                                           "gmax", "scale"))
            with nc.Block() as block:
                @block.gpsimd
                def _(pool):
                    pool.memset(hmx[:], 0.0).then_inc(s_z, 1)
                    pool.memset(hh[:, MI - 1, :], 0.0).then_inc(s_z, 1)
                    pool.memset(magic[:], -ROUND).then_inc(s_z, 1)
                    pool.wait_ge(s_g, 1)
                    pool.partition_all_reduce(amax[:], gmx[:], 128, bass.bass_isa.ReduceOp.max).then_inc(s_gd, 1)

                @block.tensor
                def _(pe):
                    def group(i, q):
                        n = i * 2 + q
                        pe.wait_ge(s_xb, n + 1)
                        if not (isinstance(i, int) and i == 0 and q == 0):
                            pe.wait_ge(s_xT, n)
                        for c in range(2):
                            for j in range(G):
                                x = pe.transpose(bkb[c][:, (NT + 1) * j:(NT + 1) * j + NT],
                                                 xb[q][:, j, 128 * c:128 * c + 128], identb[0:NT, 0:NT])
                        x.then_inc(s_T, 1)
                        pe.wait_ge(s_xT, n + 1)
                        for m in range(MI):
                            r = n * MI + m
                            b = m % 2
                            if not (isinstance(i, int) and i == 0 and q == 0 and m < 2):
                                pe.wait_ge(s_gt, r - 1)
                            for c in range(2):
                                x = pe.matmul(bk[2 + b][0:PART[m], 0:GT], wgT[:, c, 128 * m:128 * m + PART[m]],
                                              xT[q][:, c, :], start=(c == 0), stop=(c == 1))
                            x.then_inc(s_gate, 1)
                            if not (isinstance(i, int) and i == 0 and q == 0 and m < 2):
                                pe.wait_ge(s_h, r - 1)
                            for c in range(2):
                                x = pe.matmul(bk[4 + b][0:PART[m], 0:GT], wuT[:, c, 128 * m:128 * m + PART[m]],
                                              xT[q][:, c, :], start=(c == 0), stop=(c == 1))
                            x.then_inc(s_up, 1)

                    group(0, 0)
                    group(0, 1)
                    with pe.Fori(1, GN // 2) as i:
                        group(i, 0)
                        group(i, 1)

                @block.scalar
                def _(act):
                    def whole(i, q):
                        n = i * 2 + q
                        act.wait_ge(s_q2, n + 1)
                        if not (isinstance(i, int) and i == 0):
                            act.wait_ge(s_T, n - 1)
                        act.activation(xb[q][:], xq[q][:], ACT.Identity, bias=magic[0:NT, 0:1]).then_inc(s_xb, 1)

                    def group(i, q, nxt):
                        n = i * 2 + q
                        act.wait_ge(s_T, n + 1)
                        for c in range(2):
                            x = act.activation(xT[q][:, c, :].rearrange("p (j t) -> p j t", j=G),
                                               bkb[c][:, 0:G * (NT + 1)].rearrange("p (j t) -> p j t", j=G)[:, :, 0:NT],
                                               ACT.Copy)
                        x.then_inc(s_xT, 1)
                        for m in range(MI):
                            r = n * MI + m
                            act.wait_ge(s_gate, r + 1)
                            if not (isinstance(i, int) and i == 0 and q == 0 and m < 2):
                                act.wait_ge(s_h, r - 1)
                            p = PART[m]
                            act.activation(gt[m % 2][0:p, :], bk[2 + m % 2][0:p, 0:GT], ACT.Silu,
                                           scale=sg[0:p, m:m + 1]).then_inc(s_gt, 1)
                            if m == 2 and nxt:
                                whole(*((i, 1) if q == 0 else (i + 1, 0)))

                    act.wait_ge(s_z, 3)
                    whole(0, 0)
                    group(0, 0, True)
                    group(0, 1, True)
                    with act.Fori(1, GN // 2 - 1) as i:
                        group(i, 0, True)
                        group(i, 1, True)
                    group(GN // 2 - 1, 0, True)
                    group(GN // 2 - 1, 1, False)

                @block.vector
                def _(dve):
                    def scaled(i, q):
                        n = i * 2 + q
                        if not (isinstance(i, int) and i == 0):
                            dve.wait_ge(s_xb, n - 1)
                        x4 = xn[:, bass.ds(i * (2 * G) + q * G, G), :].rearrange("p j d -> p (j d)")
                        v = xq[q][:].rearrange("p j d -> p (j d)")
                        dve.tensor_scalar(v, x4, ix[0:NT, 0:1], QMAX, ALU.mult, ALU.min).then_inc(s_q1, 1)
                        dve.wait_ge(s_q1, n + 1)
                        dve.tensor_scalar(v, v, -QMAX - 1.0, ROUND, ALU.max, ALU.add).then_inc(s_q2, 1)

                    def group(i, q, nxt):
                        n = i * 2 + q
                        if nxt:
                            scaled(*((i, 1) if q == 0 else (i + 1, 0)))
                        for m in range(MI):
                            r = n * MI + m
                            p = PART[m]
                            dve.wait_ge(s_up, r + 1)
                            dve.wait_ge(s_gt, r + 1)
                            h = hh[0:p, m, bass.ds(i * (2 * GT) + q * GT, GT)]
                            dve.scalar_tensor_tensor(h, bk[4 + m % 2][0:p, 0:GT], su[0:p, m:m + 1],
                                                     gt[m % 2][0:p, :], ALU.mult, ALU.mult).then_inc(s_h, 1)
                            dve.wait_ge(s_h, r + 1)
                            dve.tensor_reduce(hmx[0:p, bass.ds(r, 1)], h, X, ALU.max,
                                              apply_absolute_value=True).then_inc(s_mx, 1)

                    dve.wait_ge(s_z, 3)
                    scaled(0, 0)
                    group(0, 0, True)
                    group(0, 1, True)
                    with dve.Fori(1, GN // 2 - 1) as i:
                        group(i, 0, True)
                        group(i, 1, True)
                    group(GN // 2 - 1, 0, True)
                    group(GN // 2 - 1, 1, False)
                    dve.wait_ge(s_mx, GN * MI)
                    dve.tensor_reduce(gmx[:], hmx[:], X, ALU.max).then_inc(s_g, 1)
                    dve.wait_ge(s_gd, 1)
                    dve.scalar_tensor_tensor(sh[:], amax[:], 1.0 / QMAX, sig[:, 1:2], ALU.mult, ALU.mult).then_inc(s_g, 1)
                    dve.wait_ge(s_g, 2)
                    dve.reciprocal(ih[:], sh[:])
                    dve.tensor_scalar(srow[:], srow[:], sh[0:NT, 0:1], None, ALU.mult)

        with ExitStack() as c2:
            hq = [c2.enter_context(nc.sbuf_tensor(f"ml_hq{i}", [128, MI, GT], F32)) for i in range(2)]
            hb = [c2.enter_context(nc.sbuf_tensor(f"ml_hb{i}", [128, MI, G, NT + 1], BF16)) for i in range(2)]
            dn = [c2.enter_context(nc.sbuf_tensor(f"ml_dn{i}", [NT, G, D], F32)) for i in range(2)]
            magic = c2.enter_context(nc.sbuf_tensor("ml_magic2", [128, 1], F32))
            s_z, s_q1, s_q2, s_hb, s_D, s_dn, s_res = (
                sem(f"s_md_{n}") for n in ("zero", "q1", "q2", "hb", "down", "scaled", "residual"))
            s_out = sem("s_out")
            with nc.Block() as block:
                @block.sync
                def _(sp):
                    with sp.Fori(0, GN) as g:
                        sp.wait_ge(s_res, g + 1)
                        for a, b, c in ((0, NPT, 1), (NPT, NPT + 1, 0), (NPT + 1, NT, NPT + 1)):
                            sp.dma_start(out[bass.ds(g * G, G), c:c + b - a, :].rearrange("b s d -> s b d"),
                                         k.H[a:b, bass.ds(g * G, G), :]).then_inc(s_out, 16)
                    sp.wait_ge(s_out, 48 * GN)

                @block.gpsimd
                def _(pool):
                    pool.memset(magic[:], -ROUND).then_inc(s_z, 1)
                    with pool.Fori(0, GN // 2) as i:
                        for q in range(2):
                            pool.wait_ge(s_dn, i * (2 * G) + (q * G + G))
                            h = k.samples(i * (2 * G) + q * G, G)
                            pool.tensor_tensor(h, h, dn[q][:].rearrange("p j d -> p (j d)"), ALU.add).then_inc(s_res, 1)

                @block.vector
                def _(dve):
                    def scaled(i, q):
                        n = i * 2 + q
                        if not (isinstance(i, int) and i == 0):
                            dve.wait_ge(s_hb, n - 1)
                        h = hh[:, :, bass.ds(i * (2 * GT) + q * GT, GT)]
                        dve.tensor_scalar(hq[q][:], h, ih[:, 0:1], QMAX, ALU.mult, ALU.min).then_inc(s_q1, 1)
                        dve.wait_ge(s_q1, n + 1)
                        v = hq[q][:].rearrange("p m t -> p (m t)")
                        dve.tensor_scalar(v, v, -QMAX - 1.0, ROUND, ALU.max, ALU.add).then_inc(s_q2, 1)

                    def group(i, q, nxt):
                        if nxt:
                            scaled(*((i, 1) if q == 0 else (i + 1, 0)))
                        if not (isinstance(i, int) and i == 0):
                            dve.wait_ge(s_res, i * 2 + (q - 1))
                        for j in range(G):
                            dve.wait_ge(s_D, i * (2 * G) + (q * G + j + 1))
                            dve.tensor_tensor(dn[q][:, j, :], bk[j % 4][0:NT, 0:D], srow[:], ALU.mult).then_inc(s_dn, 1)

                    scaled(0, 0)
                    group(0, 0, True)
                    group(0, 1, True)
                    with dve.Fori(1, GN // 2 - 1) as i:
                        group(i, 0, True)
                        group(i, 1, True)
                    group(GN // 2 - 1, 0, True)
                    group(GN // 2 - 1, 1, False)

                @block.scalar
                def _(act):
                    act.wait_ge(s_z, 1)

                    def whole(i, q):
                        n = i * 2 + q
                        act.wait_ge(s_q2, n + 1)
                        if not (isinstance(i, int) and i == 0):
                            act.wait_ge(s_D, i * (2 * G) + (q * G - G))
                        act.activation(hb[q][:, :, :, 0:NT].rearrange("p m j t -> p (m j) t"),
                                       hq[q][:].rearrange("p m (j t) -> p (m j) t", j=G), ACT.Identity,
                                       bias=magic[:, 0:1]).then_inc(s_hb, 1)

                    whole(0, 0)
                    whole(0, 1)
                    with act.Fori(1, GN // 2) as i:
                        whole(i, 0)
                        whole(i, 1)

                @block.tensor
                def _(pe):
                    def group(i, q):
                        pe.wait_ge(s_hb, i * 2 + (q + 1))
                        for j in range(G):
                            if not (isinstance(i, int) and i == 0 and q == 0):
                                pe.wait_ge(s_dn, i * (2 * G) + (q * G + j - G + 1))
                            for m in range(MI):
                                p = PART[m]
                                x = pe.matmul(bk[j % 4][0:NT, 0:D], hb[q][0:p, m, j, 0:NT], wdT[0:p, m, :],
                                              start=(m == 0), stop=(m == MI - 1))
                            x.then_inc(s_D, 1)

                    group(0, 0)
                    group(0, 1)
                    with pe.Fori(1, GN // 2) as i:
                        group(i, 0)
                        group(i, 1)


def build(nc, ins, out, stages):
    with ExitStack() as ctx:
        sb = lambda n, s, d=F32: ctx.enter_context(nc.sbuf_tensor(n, s, d))
        sem = lambda n: ctx.enter_context(nc.semaphore(n))
        k = Shared()
        k.ps = ctx.enter_context(nc.psum_tensor("ps", [128, 8, 512], F32))
        k.bank = [k.ps[:, b, :] for b in range(8)]
        k.H = sb("H", [NT, NB, D])
        k.sample = lambda b: k.H[:, bass.ds(b, 1), :].rearrange("p a d -> p (a d)")
        k.samples = lambda b, n: k.H[:, bass.ds(b, n), :].rearrange("p a d -> p (a d)")
        k.ident = sb("ident", [128, 128])
        k.mhalf = sb("minus_half", [128, 8])
        k.s_go = sem("s_constants")
        k.s_hold = sem("s_waits_held")
        constants(nc, k, sem)
        k.slot = sb("slot", [NT, NB], U32)
        k.gate = sb("gate", [NT, NB])
        k.xd = nc.dram_tensor("expert_rows", (NE * CAP, D), F32).ap()
        k.yd = nc.dram_tensor("expert_outputs", (NE * CAP, D), F32).ap()
        k.s_xd0 = sem("s_table_zeroed")
        tokens(nc, k, ins)
        if stages > 1:
            attention(nc, k, ins)
        if stages > 2:
            with ExitStack() as moe:
                k.w1 = [moe.enter_context(nc.sbuf_tensor(f"w1_{q}", [128, 2, FF], F32)) for q in range(2)]
                k.w2 = [moe.enter_context(nc.sbuf_tensor(f"w2_{q}", [128, FF // 128, D], F32)) for q in range(2)]
                k.s_w1 = [sem(f"s_w1_{q}") for q in range(2)]
                k.s_w2 = [sem(f"s_w2_{q}") for q in range(2)]
                route(nc, k, ins)
                experts(nc, k, ins)
            with ExitStack() as tied:
                k.wl = tied.enter_context(nc.sbuf_tensor("tied_w", [128, NH, 2, D], F32))
                k.s_wl = sem("s_tied_w")
                combine(nc, k, ins)
                if stages > 3:
                    tied_attention(nc, k, ins)
        if stages > 4:
            mlp(nc, k, ins, out)
            return
        dump(nc, k, out, sem)


def constants(nc, k, sem):
    s_zero = sem("s_ident_zeroed")
    with nc.Block() as block:
        @block.gpsimd
        def _(pool):
            pool.memset(k.mhalf[:], -0.5)
            pool.memset(k.ident[:], 0.0).then_inc(s_zero, 1)
            pool.wait_ge(s_zero, 1)
            pool.affine_select(out=k.ident[:], in_=k.ident[:], compare_op=ALU.not_equal, fill=1.0, base=0,
                               pattern=[[-1, 128]], channel_multiplier=1).then_inc(k.s_go, 1)


def dump(nc, k, out, sem):
    s_out = sem("s_out")
    with nc.Block() as block:
        @block.sync
        def _(sp):
            for a, b, c in ((0, NPT, 1), (NPT, NPT + 1, 0), (NPT + 1, NT, NPT + 1)):
                sp.dma_start(out[:, c:c + b - a, :].rearrange("b s d -> s b d"), k.H[a:b, :, :]).then_inc(s_out, 16)
            sp.wait_ge(s_out, 48)


_INS = ["x", "txt", "L0_tok_ln1_g", "L0_tok_ln1_b", "L0_tok_W_proj", "L0_tok_b_proj", "L0_tok_ln2_g", "L0_tok_ln2_b",
        "L0_tok_cls_token", "L0_tok_pos_emb", "L0_attn_w_qkv", "L0_attn_w_proj", "L0_attn_b_proj", "L0_ffn_Wr",
        "L0_ffn_W1", "L0_ffn_W2", "L1_attn_weight", "L1_ffn_clip_x", "L1_ffn_clip_down", "L1_ffn_w_gate",
        "L1_ffn_w_up", "L1_ffn_w_down"]
STAGES = 9


def kernel(**inputs):
    import numpy as _np
    import concourse.bacc as _bacc
    from concourse import mybir as _mybir
    from concourse.bass_utils import run_bass_kernel_spmd as _run

    nc = _bacc.Bacc("TRN2", target_bir_lowering=False, num_devices=1)
    arrays, args = {}, {}
    for name in _INS:
        a = _np.ascontiguousarray(inputs[name])
        arrays[f"in_{name}"] = a
        args[name] = nc.dram_tensor(f"in_{name}", a.shape, _mybir.dt.from_np(a.dtype), kind="ExternalInput").ap()
    out = nc.dram_tensor("out_0", (NB, NT, D), F32, kind="ExternalOutput").ap()
    build(nc, args, out, STAGES)
    r = _run(nc, [arrays], core_ids=[0])
    return r.results[0]["out_0"]
```

```python
from contextlib import ExitStack

import concourse.bass as bass
from concourse import mybir

F32 = mybir.dt.float32
F32R = mybir.dt.float32r
BF16 = mybir.dt.bfloat16
I32 = mybir.dt.int32
U32 = mybir.dt.uint32
ALU = mybir.AluOpType
ACT = mybir.ActivationFunctionType
X = mybir.AxisListType.X
EPS = 1e-5

NB = 32
NPT = 36
NT = 69
D = 256
NH = 16
HD = D // NH
HP = 32
PAIRS = NB // 2
SIDE = 6
PIX = 16
ROWS = 3 * PIX
NE = 8
CAP = NB * NT // NE
FF = 1024
CH = NH // 4
HALF = 8 * NT
CW = 4 * NT
W2T = 2 * NT
Q4 = 4 * NT


class Shared:
    pass


def clear(nc, used):
    with nc.Block() as block:
        @block.sync
        def _(sp):
            for s in used:
                sp.sem_clear(s)


def tokens(nc, k, ins):
    with ExitStack() as ctx:
        sb = lambda n, s, d=F32: ctx.enter_context(nc.sbuf_tensor(n, s, d))
        used = []
        sem = lambda n: used.append(ctx.enter_context(nc.semaphore(n))) or used[-1]
        img = [sb("img_hi", [128, ROWS, 96]), sb("img_lo", [64, ROWS, 96])]
        size = [128, 64]
        xn = [sb("xn_hi", [128, SIDE, ROWS * PIX]), sb("xn_lo", [64, SIDE, ROWS * PIX])]
        wt = sb("tok_w", [128, 2, 3, D])
        g1 = sb("tok_g1", [128, 2, 3])
        b1 = sb("tok_b1", [128, 2, 3])
        bp = sb("tok_bproj", [128, 2])
        g2 = sb("tok_g2", [NPT, D])
        pos = sb("tok_pos", [NPT, D])
        b2 = sb("tok_b2", [NPT, D])
        cls = sb("tok_cls", [1, D])
        pos0 = sb("tok_pos0", [1, D])
        st = [sb(f"tok_st{g}", [size[g], SIDE, 2, 6]) for g in range(2)]
        mv = [sb(f"tok_mv{g}", [size[g], SIDE, 2]) for g in range(2)]
        rs = [sb(f"tok_rs{g}", [size[g], SIDE]) for g in range(2)]
        xt = [sb(f"tok_xt{i}", [128, 6, 384]) for i in range(2)]
        zt = sb("tok_zt", [128, 2, NB, NPT])
        st2 = sb("tok_st2", [NPT, NB, 6])
        mv2 = sb("tok_mv2", [NPT, NB, 2])
        rs2 = sb("tok_rs2", [NPT, NB])
        zn = [sb(f"tok_zn{i}", [NPT, 4, D]) for i in range(2)]
        s_img = [sem("s_img_hi"), sem("s_img_lo")]
        s_w = sem("s_tok_w")
        s_col = sem("s_tok_columns")
        s_row = sem("s_tok_rows")
        s_txt = sem("s_txt")
        s_crow = sem("s_cls_row")
        s_cls = sem("s_cls_stored")
        s_st = sem("s_tok_stats")
        s_mv = sem("s_tok_meanvar")
        s_ve = sem("s_tok_vareps")
        s_rs = sem("s_tok_rstd")
        s_xn = sem("s_tok_xn")
        s_tp = sem("s_tok_transposed")
        s_te = [sem("s_tok_xt_by_act"), sem("s_tok_xt_by_dve")]
        s_z = sem("s_tok_z")
        s_ze = sem("s_tok_z_evacuated")
        s_zt = sem("s_tok_z_tokens")
        s_st2 = sem("s_tok_stats2")
        s_mv2 = sem("s_tok_meanvar2")
        s_ve2 = sem("s_tok_vareps2")
        s_rs2 = sem("s_tok_rstd2")
        s_zn = sem("s_tok_zn")
        zero = sb("zero", [92, 6 * D])
        s_zero = sem("s_zero")
        bk = k.bank
        block = ctx.enter_context(nc.Block())

        @block.sync
        def _(sp):
            for hh in range(SIDE):
                g, q = hh // 4, hh % 4
                src = ins["x"][:, :, PIX * hh:PIX * hh + PIX, :].rearrange("b c r w -> b c (r w)")
                dst = img[g][32 * q:32 * q + 32].rearrange("b (c r) w -> b c (r w)", c=3)
                sp.dma_start(dst, src).then_inc(s_img[g], 16)
            sp.dma_start(k.H[NPT + 1:NT, :, :], ins["txt"].rearrange("b s d -> s b d")).then_inc(s_txt, 16)
            attention_loads(sp, k, ins)
            sp.wait_ge(s_zero, 1)
            rows = k.xd.rearrange("(g p j) d -> g p (j d)", p=92, j=6)
            for g in range(NE * CAP // (92 * 6)):
                sp.dma_start(rows[g], zero[:]).then_inc(k.s_xd0, 16)
            k.xd0 = 16 * (NE * CAP // (92 * 6))
            sp.wait_ge(s_crow, 1)
            sp.dma_start(k.H[NPT:NPT + 1, :, :], cls[0:1, :].unsqueeze(1).broadcast_to([1, NB, D])).then_inc(s_cls, 16)
            sp.wait_ge(s_txt, 16)
            sp.wait_ge(s_cls, 16)

        @block.scalar
        def _(act):
            row = lambda n: ins[n].rearrange("(a d) -> a d", a=1)
            act.dma_start(wt[:], ins["L0_tok_W_proj"].rearrange("(h p c) e -> p h c e", h=2, c=3)).then_inc(s_w, 16)
            act.dma_start(g1[:], ins["L0_tok_ln1_g"].rearrange("(h p c) -> p h c", h=2, c=3)).then_inc(s_col, 16)
            act.dma_start(b1[:], ins["L0_tok_ln1_b"].rearrange("(h p c) -> p h c", h=2, c=3)).then_inc(s_col, 16)
            with nc.allow_non_contiguous_dma(reason="256 numbers, once"):
                act.dma_start(bp[:], ins["L0_tok_b_proj"].rearrange("(e p) -> p e", e=2)).then_inc(s_col, 16)
            act.dma_start(g2[:], row("L0_tok_ln2_g").broadcast_to([NPT, D])).then_inc(s_row, 16)
            act.dma_start(b2[:], row("L0_tok_ln2_b").broadcast_to([NPT, D])).then_inc(s_row, 16)
            act.dma_start(pos[:], ins["L0_tok_pos_emb"][0, 1:NPT + 1, :]).then_inc(s_row, 16)
            act.dma_start(pos0[:], ins["L0_tok_pos_emb"][0, 0:1, :]).then_inc(s_row, 16)
            act.dma_start(cls[:], ins["L0_tok_cls_token"][0, 0:1, :]).then_inc(s_row, 16)
            act.wait_ge(s_col, 48)
            for w in range(3):
                for c in range(0, 6, 2):
                    n = 6 * w + c
                    act.wait_ge(s_tp, n + 1)
                    if w >= 2:
                        act.wait_ge(s_z, 2 * (w - 1))
                    act.activation(xt[w % 2][:, c, :], bk[c % 2][:, 0:384], ACT.Identity,
                                   bias=b1[:, c % 2, c // 2:c // 2 + 1],
                                   scale=g1[:, c % 2, c // 2:c // 2 + 1]).then_inc(s_te[0], 1)
                for e in range(2):
                    act.wait_ge(s_z, 2 * w + e + 1)
                    src = bk[2 + e][:, 0:384].rearrange("p (w h b) -> p w h b", w=2, h=SIDE)
                    for v in range(2):
                        dst = zt[:, e].rearrange("p b (h w) -> p w h b", w=SIDE)[:, 2 * w + v]
                        i = act.activation(dst, src[:, v], ACT.Identity, bias=bp[:, e:e + 1])
                    i.then_inc(s_ze, 1)

        @block.gpsimd
        def _(pool):
            attention_zeros(pool, k)
            pool.memset(zero[:], 0.0).then_inc(s_zero, 1)
            for g in range(2):
                pool.wait_ge(s_mv, g + 1)
                pool.tensor_scalar(rs[g][:], mv[g][:, :, 1], EPS, None, ALU.add).then_inc(s_ve, 1)
                pool.wait_ge(s_ve, g + 1)
                pool.tensor_tensor(rs[g][:], rs[g][:], k.mhalf[0:size[g], 0:SIDE], ALU.pow).then_inc(s_rs, 1)
            for q in range(NB // 4):
                pool.wait_ge(s_mv2, q + 1)
                v = rs2[:, 4 * q:4 * q + 4]
                pool.tensor_scalar(v, mv2[:, 4 * q:4 * q + 4, 1], EPS, None, ALU.add).then_inc(s_ve2, 1)
                pool.wait_ge(s_ve2, q + 1)
                pool.tensor_tensor(v, v, k.mhalf[0:NPT, 0:4], ALU.pow).then_inc(s_rs2, 1)

        @block.vector
        def _(dve):
            for g in range(2):
                dve.wait_ge(s_img[g], 64 if g == 0 else 32)
                for w in range(SIDE):
                    for h in range(2):
                        i = dve.bn_stats(st[g][:, w, h, :], img[g][:, 24 * h:24 * h + 24, PIX * w:PIX * w + PIX])
                i.then_inc(s_st, 1)
                dve.wait_ge(s_st, g + 1)
                for w in range(SIDE):
                    i = dve.bn_aggr(mv[g][:, w, :], st[g][:, w].rearrange("p h s -> p (h s)"))
                i.then_inc(s_mv, 1)
            dve.wait_ge(s_row, 80)
            dve.tensor_tensor(cls[:], cls[:], pos0[:], ALU.add).then_inc(s_crow, 1)
            dve.tensor_tensor(pos[:], pos[:], b2[:], ALU.add).then_inc(s_crow, 1)
            dve.wait_ge(s_rs, 2)
            for w in range(SIDE):
                for g in range(2):
                    v = img[g][:, :, PIX * w:PIX * w + PIX]
                    o = xn[g][:, w, :].rearrange("p (r x) -> p r x", x=PIX)
                    i = dve.tensor_scalar(o, v, mv[g][:, w, 0:1], rs[g][:, w:w + 1], ALU.subtract, ALU.mult)
                i.then_inc(s_xn, 1)
            dve.wait_ge(s_col, 48)
            for w in range(3):
                for c in range(1, 6, 2):
                    dve.wait_ge(s_tp, 6 * w + c + 1)
                    if w >= 2:
                        dve.wait_ge(s_z, 2 * (w - 1))
                    dve.tensor_scalar(xt[w % 2][:, c, :], bk[c % 2][:, 0:384],
                                      g1[:, c % 2, c // 2:c // 2 + 1], b1[:, c % 2, c // 2:c // 2 + 1],
                                      ALU.mult, ALU.add).then_inc(s_te[1], 1)
            for q in range(NB // 4):
                dve.wait_ge(s_zt, q + 1)
                z = lambda j: bk[4 * (q % 2) + j // 2][0:NPT, D * (j % 2):D * (j % 2) + D]
                for j in range(4):
                    i = dve.bn_stats(st2[:, 4 * q + j, :], z(j))
                i.then_inc(s_st2, 1)
                dve.wait_ge(s_st2, q + 1)
                for j in range(4):
                    i = dve.bn_aggr(mv2[:, 4 * q + j, :], st2[:, 4 * q + j, :])
                i.then_inc(s_mv2, 1)
                dve.wait_ge(s_rs2, q + 1)
                for j in range(4):
                    b = 4 * q + j
                    i = dve.scalar_tensor_tensor(zn[q % 2][:, j, :], z(j), mv2[:, b, 0:1], g2[:],
                                                 ALU.subtract, ALU.mult)
                i.then_inc(s_zn, 1)
                dve.wait_ge(s_zn, q + 1)
                for j in range(4):
                    b = 4 * q + j
                    dve.scalar_tensor_tensor(k.H[0:NPT, b, :], zn[q % 2][:, j, :], rs2[:, b:b + 1], pos[:],
                                             ALU.mult, ALU.add)

        @block.tensor
        def _(pe):
            pe.wait_ge(s_w, 16)
            for w in range(3):
                pe.wait_ge(s_xn, 2 * w + 2)
                for c in range(6):
                    n = 6 * w + c
                    if n >= 2:
                        pe.wait_ge(s_te[c % 2], (n - 2) // 2 + 1)
                    for v in range(2):
                        for g in range(2):
                            src = xn[g][:, 2 * w + v, 128 * c:128 * c + 128]
                            i = pe.transpose(bk[c % 2][:, 192 * v + 128 * g:192 * v + 128 * g + size[g]], src,
                                             k.ident[0:size[g], 0:size[g]])
                    i.then_inc(s_tp, 1)
                pe.wait_ge(s_te[0], 3 * w + 3)
                pe.wait_ge(s_te[1], 3 * w + 3)
                for e in range(2):
                    if w >= 1:
                        pe.wait_ge(s_ze, 2 * (w - 1) + e + 1)
                    for c in range(6):
                        i = pe.matmul(bk[2 + e][:, 0:384], wt[:, c % 2, c // 2, 128 * e:128 * e + 128],
                                      xt[w % 2][:, c, :], start=(c == 0), stop=(c == 5))
                    i.then_inc(s_z, 1)
            pe.wait_ge(s_ze, 6)
            for q in range(NB // 4):
                if q >= 2:
                    pe.wait_ge(s_zn, q - 1)
                for j in range(4):
                    for e in range(2):
                        o = D * (j % 2) + 128 * e
                        i = pe.transpose(bk[4 * (q % 2) + j // 2][0:NPT, o:o + 128], zt[:, e, 4 * q + j, :],
                                         k.ident[:])
                i.then_inc(s_zt, 1)

    clear(nc, used)





def attention_tables(nc, k, ctx):
    sb = lambda n, s, d=F32: ctx.enter_context(nc.sbuf_tensor(n, s, d))
    k.wqk = sb("at_wqk", [128, 2, 2, D])
    k.wv = sb("at_wv", [128, 2, D])
    k.wo = sb("at_wo", [128, CH, D])
    k.bo = sb("at_bo", [NT, 2, D])
    k.vp = [sb(f"at_vp{i}", [NT, 2, NH, HP]) for i in range(2)]
    k.s_at_w = k.sem("s_at_w")
    k.s_at_z = k.sem("s_at_pads_zeroed")
    k.AT_LOADS = 2 * 3 + NH + 2


def attention_zeros(pool, k):
    pool.memset(k.wo[:], 0.0).then_inc(k.s_at_z, 1)
    for q in range(2):
        pool.memset(k.vp[q][:], 0.0).then_inc(k.s_at_z, 1)


def attention_loads(sp, k, ins):
    for c in range(2):
        for t in range(2):
            sp.dma_start(k.wqk[:, c, t, :], ins["L0_attn_w_qkv"][128 * c:128 * c + 128, D * t:D * t + D]
                         ).then_inc(k.s_at_w, 16)
        sp.dma_start(k.wv[:, c, :], ins["L0_attn_w_qkv"][128 * c:128 * c + 128, 2 * D:3 * D]).then_inc(k.s_at_w, 16)
    for j in range(2):
        sp.dma_start(k.bo[:, j, :], ins["L0_attn_b_proj"].rearrange("(a d) -> a d", a=1)
                     .broadcast_to([NT, D])).then_inc(k.s_at_w, 16)
    sp.wait_ge(k.s_at_z, 1)
    for r in range(4):
        for c in range(CH):
            h = 4 * c + r
            sp.dma_start(k.wo[HP * r:HP * r + HD, c, :],
                         ins["L0_attn_w_proj"][HD * h:HD * h + HD, :]).then_inc(k.s_at_w, 16)


def attention(nc, k, ins):
    with ExitStack() as ctx:
        sb = lambda n, s, d=F32: ctx.enter_context(nc.sbuf_tensor(n, s, d))
        used = []
        sem = lambda n: used.append(ctx.enter_context(nc.semaphore(n))) or used[-1]
        two = lambda n, s, d=F32: [sb(f"{n}{i}", s, d) for i in range(2)]
        four = lambda n, s, d=F32: [sb(f"{n}{i}", s, d) for i in range(4)]
        H = k.H
        st = two("at_st", [NT, 2, 6])
        mv = two("at_mv", [NT, 2, 2])
        rs = two("at_rs", [NT, 2])
        hn = two("at_hn", [NT, 2, D])
        hT = two("at_hT", [128, 2, W2T])
        qT = two("at_qT", [128, 2, W2T])
        kT = two("at_kT", [128, 2, W2T])
        kd = two("at_kd", [128, 2, 2, HALF])
        eb = four("at_e", [NT, HALF])
        mx = four("at_mx", [NT, 8])
        sm = four("at_sum", [NT, 8])
        rc = four("at_rc", [NT, 8])
        ets = two("at_et", [NT, HALF])
        oT = two("at_oT", [128, CH, W2T])
        pT = two("at_pT", [128, 2, W2T])
        s_st, s_mv, s_ve, s_rs, s_hn = (sem(f"s_at_{n}") for n in ("stats", "meanvar", "vareps", "rstd", "hn"))
        s_full = [sem(f"s_at_bank_full{i}") for i in range(2)]
        s_drained = [sem(f"s_at_bank_drained{i}") for i in range(2)]
        s_kd = [sem(f"s_at_kd{j}") for j in range(2)]
        s_S, s_mx, s_sub, s_exp, s_sum, s_rc, s_nrm = (
            sem(f"s_at_{n}") for n in ("scores", "max", "sub", "exp", "sum", "recip", "norm"))
        s_T, s_te, s_PV, s_xa, s_xd, s_hb = (
            sem(f"s_at_{n}") for n in ("turned", "turned_sb", "pv", "out_by_act", "out_by_dve", "bias"))
        sc = k.ps[:, 0:2, :]
        tb = k.ps[:, 2:4, :]
        vb = k.ps[:, 4:6, :]
        mb = [k.bank[6], k.bank[7]]
        LAST = PAIRS - 1

        HT, Q, K, V, PROJ, BACK = range(6)

        def use(i, q, what):
            b, idx = what % 2, what // 2
            if isinstance(i, int) and i == 0 and q == 0:
                return b, 2 + idx
            if isinstance(i, int) and 2 * i + q == LAST:
                return b, 3 * LAST + 1 + idx - 2
            if isinstance(i, int) and 2 * i + q == PAIRS:
                return b, 3 * LAST + 2 + idx - 2
            return b, i * 6 + (3 * q + 1 + idx)

        def use0(what):
            return what % 2, what // 2

        def unit(i, q, u):
            return i * 8 + (4 * q + u)

        def after(i, q):
            return (i, 1) if q == 0 else (i + 1, 0)

        def later(i, q, u, d):
            if u + d < 4:
                return i, q, u + d
            if isinstance(i, int) and 2 * i + q == LAST:
                return None
            return *after(i, q), u + d - 4

        def before(i, q):
            return (i, 0) if q == 1 else (i - 1, 1)

        def drained(eng, u):
            eng.wait_ge(s_drained[u[0]], u[1] + 1)

        def filled(eng, u):
            eng.wait_ge(s_full[u[0]], u[1] + 1)
            return mb[u[0]]

        def all_pairs(eng, pair):
            pair(0, 0, True, False, True)
            pair(0, 1, True, True, True)
            with eng.Fori(1, PAIRS // 2 - 1) as i:
                pair(i, 0, True, True, True)
                pair(i, 1, True, True, True)
            pair(LAST // 2, 0, True, True, False)
            pair(LAST // 2, 1, False, True, False)

        block = ctx.enter_context(nc.Block())

        @block.tensor
        def _(pe):
            def fill(u):
                pe.wait_ge(s_drained[u[0]], u[1])
                return mb[u[0]]

            def front(i, q, what, u):
                if what == HT:
                    pe.wait_ge(s_hn, i * 2 + (q + 1))
                    b = fill(u)
                    for j in range(2):
                        for c in range(2):
                            o = W2T * c + NT * j
                            x = pe.transpose(b[:, o:o + NT], hn[q][:, j, 128 * c:128 * c + 128],
                                             k.ident[0:NT, 0:NT])
                elif what == V:
                    b = fill(u)
                    for j in range(2):
                        for c in range(2):
                            x = pe.matmul(b[0:NT, D * j:D * j + D], hT[q][:, c, NT * j:NT * j + NT], k.wv[:, c, :],
                                          start=(c == 0), stop=(c == 1))
                else:
                    b = fill(u)
                    for m in range(2):
                        for c in range(2):
                            x = pe.matmul(b[:, W2T * m:W2T * m + W2T],
                                          k.wqk[:, c, what - Q, 128 * m:128 * m + 128], hT[q][:, c, :],
                                          start=(c == 0), stop=(c == 1))
                x.then_inc(s_full[u[0]], 1)

            def scores(i, q, u):
                j, h = u // 2, u % 2
                if h == 0:
                    pe.wait_ge(s_kd[j], i * 2 + (q + 1))
                n = unit(i, q, u)
                if not (isinstance(n, int) and n == 0):
                    pe.wait_ge(s_sub, n)
                for c in range(2):
                    x = pe.matmul(sc[0:NT, c, 0:CW], qT[q][:, h, NT * j:NT * j + NT],
                                  kd[q][:, j, h, CW * c:CW * c + CW], start=True, stop=True)
                x.then_inc(s_S, 1)

            def turn(i, q, u):
                n = unit(i, q, u)
                pe.wait_ge(s_nrm, n + 1)
                if not (isinstance(n, int) and n == 0):
                    pe.wait_ge(s_te, n)
                for h in range(8):
                    x = pe.transpose(tb[0:NT, h // 4, NT * (h % 4):NT * (h % 4) + NT],
                                     eb[u][:, NT * h:NT * h + NT], k.ident[0:NT, 0:NT])
                x.then_inc(s_T, 1)

            def weigh(i, q, u):
                n = unit(i, q, u)
                j, h = u // 2, u % 2
                pe.wait_ge(s_te, n + 1)
                if not (isinstance(n, int) and n == 0):
                    pe.wait_ge(s_xa, n)
                    pe.wait_ge(s_xd, n)
                for c in range(2):
                    x = pe.matmul(vb[:, c, 0:CW],
                                  k.vp[q][:, j, 8 * h + 4 * c:8 * h + 4 * c + 4, :].rearrange("p h e -> p (h e)"),
                                  ets[u % 2][:, CW * c:CW * c + CW], start=True, stop=True)
                x.then_inc(s_PV, 1)

            def project(i, q, u):
                n = unit(i, q, 4)
                pe.wait_ge(s_xa, n)
                pe.wait_ge(s_xd, n)
                b = fill(u)
                for e in range(2):
                    for c in range(CH):
                        x = pe.matmul(b[:, W2T * e:W2T * e + W2T], k.wo[:, c, 128 * e:128 * e + 128], oT[q][:, c, :],
                                      start=(c == 0), stop=(c == CH - 1))
                x.then_inc(s_full[u[0]], 1)

            def back(q, up, u):
                drained(pe, up)
                b = fill(u)
                for j in range(2):
                    for e in range(2):
                        o = D * j + 128 * e
                        x = pe.transpose(b[0:NT, o:o + 128], pT[q][:, e, NT * j:NT * j + NT], k.ident[:])
                x.then_inc(s_full[u[0]], 1)

            def pair(i, q, nxt, prev, ln):
                ni, nq = after(i, q)
                bi, bq = before(i, q)
                for u in range(4):
                    turn(i, q, u)
                    if nxt and u == 0:
                        front(ni, nq, HT, use(i, q, HT))
                    n2 = later(i, q, u, 2)
                    if n2:
                        scores(*n2)
                    if nxt and u == 0:
                        drained(pe, use(i, q, HT))
                        front(ni, nq, Q, use(i, q, Q))
                        front(ni, nq, K, use(i, q, K))
                    if nxt and u == 1:
                        front(ni, nq, V, use(i, q, V))
                    if prev and u == 2:
                        project(bi, bq, use(i, q, PROJ))
                    if prev and u == 3:
                        back(bq, use(i, q, PROJ), use(i, q, BACK))
                    if u == 0:
                        drained(pe, use0(V) if isinstance(i, int) and (i, q) == (0, 0) else use(*before(i, q), V))
                    weigh(i, q, u)

            pe.wait_ge(k.s_at_w, 16 * k.AT_LOADS)
            pe.wait_ge(k.s_at_z, 3)
            front(0, 0, HT, use0(HT))
            drained(pe, use0(HT))
            for w in (Q, K, V):
                front(0, 0, w, use0(w))
            scores(0, 0, 0)
            scores(0, 0, 1)
            all_pairs(pe, pair)
            end = (PAIRS // 2, 0)
            project(LAST // 2, 1, use(*end, PROJ))
            back(1, use(*end, PROJ), use(*end, BACK))

        @block.scalar
        def _(act):
            def copy(dst, src):
                return act.activation(dst, src, ACT.Copy)

            def to_sb(dst, u):
                b = filled(act, u)
                copy(dst[:].rearrange("p c t -> p (c t)"), b[:, 0:2 * W2T]).then_inc(s_drained[u[0]], 1)

            def exps(i, q, u):
                act.wait_ge(s_sub, unit(i, q, u) + 1)
                act.activation(eb[u][:], eb[u][:], ACT.Exp, scale=HD ** -0.5).then_inc(s_exp, 1)

            def turned(i, q, u):
                act.wait_ge(s_T, unit(i, q, u) + 1)
                copy(ets[u % 2][:].rearrange("p (c t) -> p c t", c=2), tb[0:NT, :, 0:CW]).then_inc(s_te, 1)

            def out_heads(i, q, u):
                j, h = u // 2, u % 2
                act.wait_ge(s_PV, unit(i, q, u) + 1)
                for r in (0, 1):
                    x = copy(oT[q][HP * r:HP * r + HP, 2 * h:2 * h + 2, NT * j:NT * j + NT],
                             vb[HP * r:HP * r + HP, :, NT * r:NT * r + NT])
                x.then_inc(s_xa, 1)

            def pair(i, q, nxt, prev, ln):
                ni, nq = after(i, q)
                bi, bq = before(i, q)
                for u in range(4):
                    turned(i, q, u)
                    if nxt and u == 0:
                        to_sb(hT[nq], use(i, q, HT))
                        to_sb(qT[nq], use(i, q, Q))
                    n2 = later(i, q, u, 2)
                    if n2:
                        exps(*n2)
                    if nxt and u == 0:
                        to_sb(kT[nq], use(i, q, K))
                    if prev and u == 2:
                        to_sb(pT[bq], use(i, q, PROJ))
                    out_heads(i, q, u)

            to_sb(hT[0], use0(HT))
            to_sb(qT[0], use0(Q))
            to_sb(kT[0], use0(K))
            exps(0, 0, 0)
            exps(0, 0, 1)
            all_pairs(act, pair)
            to_sb(pT[1], use(PAIRS // 2, 0, PROJ))

        @block.vector
        def _(dve):
            def ln_stats(i, q):
                for j in range(2):
                    x = dve.bn_stats(st[q][:, j, :], k.sample(i * 4 + (2 * q + j)))
                x.then_inc(s_st, 1)
                dve.wait_ge(s_st, i * 2 + (q + 1))
                dve.sem_inc(k.s_hold, 1)
                for j in range(2):
                    x = dve.bn_aggr(mv[q][:, j, :], st[q][:, j, :])
                x.then_inc(s_mv, 1)
                dve.wait_ge(s_mv, i * 2 + (q + 1))
                dve.tensor_scalar(rs[q][:], mv[q][:, :, 1], EPS, None, ALU.add).then_inc(s_ve, 1)

            def ln_apply(i, q):
                dve.wait_ge(s_rs, i * 2 + (q + 1))
                for j in range(2):
                    x = dve.tensor_scalar(hn[q][:, j, :], k.sample(i * 4 + (2 * q + j)), mv[q][:, j, 0:1],
                                          rs[q][:, j:j + 1], ALU.subtract, ALU.mult)
                x.then_inc(s_hn, 1)

            def less_max(i, q, u):
                n = unit(i, q, u)
                dve.wait_ge(s_S, n + 1)
                s = sc[0:NT, :, 0:CW].rearrange("p c (h t) -> p c h t", h=4)
                m = mx[u][:].rearrange("p (c h) -> p c h", c=2)
                dve.tensor_reduce(m, s, X, ALU.max).then_inc(s_mx, 1)
                dve.wait_ge(s_mx, n + 1)
                e = eb[u][:].rearrange("p (c h t) -> p c h t", c=2, h=4)
                dve.tensor_tensor(e, s, m.unsqueeze(3).broadcast_to([NT, 2, 4, NT]), ALU.subtract).then_inc(s_sub, 1)

            def sums(i, q, u):
                n = unit(i, q, u)
                dve.wait_ge(s_exp, n + 1)
                dve.tensor_reduce(sm[u][:], eb[u][:].rearrange("p (h t) -> p h t", h=8), X,
                                  ALU.add).then_inc(s_sum, 1)
                dve.wait_ge(s_sum, n + 1)
                dve.reciprocal(rc[u][:], sm[u][:]).then_inc(s_rc, 1)

            def out_heads(i, q, u):
                j, h = u // 2, u % 2
                dve.wait_ge(s_PV, unit(i, q, u) + 1)
                for r in (2, 3):
                    x = dve.tensor_copy(oT[q][HP * r:HP * r + HP, 2 * h:2 * h + 2, NT * j:NT * j + NT],
                                        vb[HP * r:HP * r + HP, :, NT * r:NT * r + NT])
                x.then_inc(s_xd, 1)

            def v_pad(q, u):
                b = filled(dve, u)
                dve.tensor_copy(k.vp[q][:, :, :, 0:HD].rearrange("p j h e -> p (j h) e"),
                                b[0:NT, :].rearrange("p (g e) -> p g e", e=HD)).then_inc(s_drained[u[0]], 1)

            def add_proj(i, q, u):
                b = filled(dve, u)
                h = k.samples(i * 4 + 2 * q, 2)
                dve.tensor_tensor(h, h, b[0:NT, :], ALU.add).then_inc(s_drained[u[0]], 1)

            def pair(i, q, nxt, prev, ln):
                ni, nq = after(i, q)
                bi, bq = before(i, q)
                for u in range(4):
                    n1, n2 = later(i, q, u, 1), later(i, q, u, 2)
                    if n1:
                        sums(*n1)
                    if n2:
                        less_max(*n2)
                    if nxt and u == 1:
                        v_pad(nq, use(i, q, V))
                    out_heads(i, q, u)
                    if prev and u == 3:
                        add_proj(bi, bq, use(i, q, BACK))
                    if ln and u == 0:
                        ln_stats(i + 1, q)
                    if ln and u == 2:
                        ln_apply(i + 1, q)

            for q in range(2):
                ln_stats(0, q)
                ln_apply(0, q)
            v_pad(0, use0(V))
            less_max(0, 0, 0)
            less_max(0, 0, 1)
            sums(0, 0, 0)
            all_pairs(dve, pair)
            add_proj(LAST // 2, 1, use(PAIRS // 2, 0, BACK))

        @block.gpsimd
        def _(pool):
            def ln_rstd(i, q):
                pool.wait_ge(s_ve, i * 2 + (q + 1))
                pool.tensor_tensor(rs[q][:], rs[q][:], k.mhalf[0:NT, 0:2], ALU.pow).then_inc(s_rs, 1)

            def norm(i, q, u):
                pool.wait_ge(s_rc, unit(i, q, u) + 1)
                e = eb[u][:].rearrange("p (h t) -> p h t", h=8)
                pool.tensor_tensor(e, e, rc[u][:].unsqueeze(2).broadcast_to([NT, 8, NT]),
                                   ALU.mult).then_inc(s_nrm, 1)

            def k_diag(i, q, j, u):
                drained(pool, u)
                for m in range(2):
                    x = pool.tensor_tensor(kd[q][:, j, m, :].rearrange("p (h t) -> p h t", h=8),
                                           kT[q][:, m, NT * j:NT * j + NT].unsqueeze(1).broadcast_to([128, 8, NT]),
                                           k.mask[:].unsqueeze(2).broadcast_to([128, 8, NT]), ALU.mult)
                x.then_inc(s_kd[j], 1)

            def bias(i, q, u):
                drained(pool, u)
                h = k.samples(i * 4 + 2 * q, 2)
                pool.tensor_tensor(h, h, k.bo[:].rearrange("p j d -> p (j d)"), ALU.add).then_inc(s_hb, 1)

            def pair(i, q, nxt, prev, ln):
                ni, nq = after(i, q)
                for u in range(4):
                    n1 = later(i, q, u, 1)
                    if n1:
                        norm(*n1)
                    if nxt and u == 0:
                        k_diag(ni, nq, 0, use(i, q, K))
                    if nxt and u == 1:
                        k_diag(ni, nq, 1, use(i, q, K))
                    if ln and u == 1:
                        ln_rstd(i + 1, q)
                    if prev and u == 3:
                        bias(*before(i, q), use(i, q, BACK))

            for q in range(2):
                ln_rstd(0, q)
            k_diag(0, 0, 0, use0(K))
            k_diag(0, 0, 1, use0(K))
            norm(0, 0, 0)
            all_pairs(pool, pair)
            bias(LAST // 2, 1, use(PAIRS // 2, 0, BACK))

    clear(nc, used)


def route(nc, k, ins):
    G = 4
    with ExitStack() as ctx:
        sb = lambda n, s, d=F32: ctx.enter_context(nc.sbuf_tensor(n, s, d))
        used = []
        sem = lambda n: used.append(ctx.enter_context(nc.semaphore(n))) or used[-1]
        two = lambda n, s, d=F32: [sb(f"{n}{i}", s, d) for i in range(2)]
        wr = sb("rt_w", [128, 2, NE])
        tri = sb("rt_before", [NT, NT])
        ones = sb("rt_ones", [NT, NT])
        lane = sb("rt_lane", [NT, G, NE])
        lane_i = sb("rt_lane_int", [NT, G, NE], I32)
        st = two("rt_st", [NT, G, 6])
        mv = two("rt_mv", [NT, G, 2])
        rs = two("rt_rs", [NT, G])
        xm = two("rt_x", [NT, G, D])
        xT = two("rt_xT", [128, 2, G * NT])
        lg = sb("rt_logits", [NT, G, NE])
        m8 = sb("rt_max", [NT, G, NE])
        i8 = sb("rt_maxi", [NT, G, NE], U32)
        ix = sb("rt_expert", [NT, G])
        dl = two("rt_less", [NT, G, NE])
        oh = two("rt_onehot", [NT, G, NE])
        seen = two("rt_seen", [NT, G, NE])
        own = sb("rt_own", [NT, G, NE])
        rk = sb("rt_rank", [NT, G])
        kp = sb("rt_keep", [NT, G])
        ad = sb("rt_addr", [NT, G])
        sl = two("rt_slot", [NT, G], U32)
        se = sb("rt_sum", [NT, G])
        s_w, s_c, s_st, s_ve, s_rs, s_x = (sem(f"s_rt_{n}") for n in ("w", "const", "stats", "vareps", "rstd", "x"))
        s_T, s_xT, s_lg, s_ch, s_dl, s_e = (
            sem(f"s_rt_{n}") for n in ("turned", "xT", "logits", "step", "less", "exp"))
        s_oh, s_rk, s_sl = (sem(f"s_rt_{n}") for n in ("onehot", "rank", "slot"))
        s_sc = [sem(f"s_rt_scattered{i}") for i in range(2)]
        bk = k.bank
        GN = NB // G
        STEPS = 18
        block = ctx.enter_context(nc.Block())

        @block.sync
        def _(sp):
            sp.dma_start(wr[:], ins["L0_ffn_Wr"].rearrange("(c p) e -> p c e", p=128)).then_inc(s_w, 16)
            for e in range(2):
                expert_weights(sp, k, ins, e, e)
            for q in range(2):
                sp.wait_ge(s_sc[q], 16 * G * GN // 2)

        @block.tensor
        def _(pe):
            def group(i, q):
                n = i * 2 + q
                pe.wait_ge(s_x, n + 1)
                if not (isinstance(i, int) and i == 0 and q == 0):
                    pe.wait_ge(s_xT, n)
                for c in range(2):
                    for j in range(G):
                        x = pe.transpose(bk[c][:, NT * j:NT * j + NT], xm[q][:, j, 128 * c:128 * c + 128],
                                         k.ident[0:NT, 0:NT])
                x.then_inc(s_T, 1)
                pe.wait_ge(s_xT, n + 1)
                for j in range(G):
                    for c in range(2):
                        x = pe.matmul(bk[2 + q][0:NT, NE * j:NE * j + NE], xT[q][:, c, NT * j:NT * j + NT],
                                      wr[:, c, :], start=(c == 0), stop=(c == 1))
                x.then_inc(s_lg, 1)
                pe.wait_ge(s_oh, n + 1)
                o = bk[4 + q][0:NT, 0:G * NE]
                pe.matmul(o, tri[:], oh[q][:].rearrange("p g e -> p (g e)"), start=True, stop=False)
                pe.matmul(o, ones[:], seen[q][:].rearrange("p g e -> p (g e)"), start=False,
                          stop=True).then_inc(s_rk, 1)

            pe.wait_ge(s_w, 16)
            group(0, 0)
            group(0, 1)
            with pe.Fori(1, GN // 2) as i:
                group(i, 0)
                group(i, 1)

        @block.scalar
        def _(act):
            def group(i, q):
                n = i * 2 + q
                act.wait_ge(s_T, n + 1)
                act.activation(xT[q][:], k.ps[:, 0:2, 0:G * NT], ACT.Copy).then_inc(s_xT, 1)
                act.wait_ge(s_dl, n + 1)
                act.activation(dl[q][:], dl[q][:], ACT.Exp).then_inc(s_e, 1)

            group(0, 0)
            group(0, 1)
            with act.Fori(1, GN // 2) as i:
                group(i, 0)
                group(i, 1)

        @block.gpsimd
        def _(pool):
            def rstd(i, q):
                pool.wait_ge(s_ve, i * 2 + (q + 1))
                pool.tensor_tensor(rs[q][:], rs[q][:], k.mhalf[0:NT, 0:G], ALU.pow).then_inc(s_rs, 1)

            def scatter(i, q):
                pool.wait_ge(s_sl, i * 2 + (q + 1))
                pool.sem_inc(k.s_hold, 1)
                for j in range(G):
                    pool.indirect_dma_start(out=k.xd[:], out_offset=bass.IndirectOffsetOnAxis(sl[q][:, j:j + 1], 0),
                                            in_=xm[q][:, j, :], in_offset=None, bounds_check=NE * CAP - 1,
                                            oob_is_err=False).then_inc(s_sc[q], 16)

            pool.memset(ones[:], 1.0)
            pool.memset(tri[:], 1.0).then_inc(s_c, 1)
            pool.iota(lane_i[:], pattern=[[0, G], [1, NE]], base=0, channel_multiplier=0).then_inc(s_c, 1)
            pool.wait_ge(s_c, 2)
            pool.tensor_copy(lane[:], lane_i[:])
            pool.affine_select(out=tri[:], in_=tri[:], compare_op=ALU.is_gt, fill=0.0, base=0,
                               pattern=[[1, NT]], channel_multiplier=-1).then_inc(s_c, 1)
            pool.wait_ge(s_c, 3)
            pool.affine_select(out=tri[:], in_=tri[:], compare_op=ALU.not_equal, fill=1.0, base=-NPT,
                               pattern=[[0, NT]], channel_multiplier=1).then_inc(s_c, 1)
            pool.wait_ge(s_c, 4)
            pool.memset(tri[:, NPT:NPT + 1], 0.0).then_inc(s_c, 1)
            rstd(0, 0)
            rstd(0, 1)
            pool.wait_ge(k.s_xd0, k.xd0)
            with pool.Fori(0, GN // 2 - 1) as i:
                rstd(i + 1, 0)
                scatter(i, 0)
                rstd(i + 1, 1)
                scatter(i, 1)
            scatter(GN // 2 - 1, 0)
            scatter(GN // 2 - 1, 1)

        @block.vector
        def _(dve):
            def ln_stats(i, q):
                for j in range(G):
                    x = dve.bn_stats(st[q][:, j, :], k.sample(i * 8 + (4 * q + j)))
                x.then_inc(s_st, 1)
                dve.wait_ge(s_st, i * 4 + (2 * q + 1))
                dve.sem_inc(k.s_hold, 1)
                for j in range(G):
                    x = dve.bn_aggr(mv[q][:, j, :], st[q][:, j, :])
                x.then_inc(s_st, 1)
                dve.wait_ge(s_st, i * 4 + (2 * q + 2))
                dve.tensor_scalar(rs[q][:], mv[q][:, :, 1], EPS, None, ALU.add).then_inc(s_ve, 1)

            def ln_apply(i, q):
                dve.wait_ge(s_rs, i * 2 + (q + 1))
                if not (isinstance(i, int) and i == 0):
                    dve.wait_ge(s_sc[q], i * (16 * G))
                for j in range(G):
                    x = dve.tensor_scalar(xm[q][:, j, :], k.sample(i * 8 + (4 * q + j)), mv[q][:, j, 0:1],
                                          rs[q][:, j:j + 1], ALU.subtract, ALU.mult)
                x.then_inc(s_x, 1)

            def route_group(i, q):
                n = [0]

                def step(x):
                    n[0] += 1
                    x.then_inc(s_ch, 1)
                    dve.wait_ge(s_ch, i * (2 * STEPS) + (q * STEPS + n[0]))

                b4 = lambda v: v.unsqueeze(2).broadcast_to([NT, G, NE])
                dve.wait_ge(s_lg, i * 2 + (q + 1))
                step(dve.tensor_copy(lg[:].rearrange("p g e -> p (g e)"), bk[2 + q][0:NT, 0:G * NE]))
                dve.sem_inc(k.s_hold, 1)
                for j in range(G):
                    x = dve.max(m8[:, j, :], lg[:, j, :])
                step(x)
                dve.sem_inc(k.s_hold, 1)
                for j in range(G):
                    x = dve.max_index(i8[:, j, :], m8[:, j, :], lg[:, j, :])
                step(x)
                dve.tensor_tensor(dl[q][:], lg[:], b4(m8[:, :, 0]), ALU.subtract).then_inc(s_dl, 1)
                step(dve.tensor_copy(ix[:], i8[:, :, 0]))
                step(dve.tensor_tensor(oh[q][:], lane[:], b4(ix[:]), ALU.is_equal))
                prev, poh = seen[1 - q], oh[1 - q]
                if isinstance(i, int) and i == 0 and q == 0:
                    step(dve.memset(seen[q][:, 0, :], 0.0))
                else:
                    step(dve.tensor_tensor(seen[q][:, 0, :], prev[:, G - 1, :], poh[:, G - 1, :], ALU.add))
                for j in range(1, G):
                    x = dve.tensor_tensor(seen[q][:, j, :], seen[q][:, j - 1, :], oh[q][:, j - 1, :], ALU.add)
                    if j < G - 1:
                        step(x)
                x.then_inc(s_oh, 1)
                dve.wait_ge(s_rk, i * 2 + (q + 1))
                step(dve.tensor_tensor(own[:].rearrange("p g e -> p (g e)"),
                                       oh[q][:].rearrange("p g e -> p (g e)"),
                                       bk[4 + q][0:NT, 0:G * NE], ALU.mult))
                step(dve.tensor_reduce(rk[:], own[:], X, ALU.add))
                step(dve.tensor_scalar(kp[:], rk[:], float(CAP), None, ALU.is_lt))
                step(dve.scalar_tensor_tensor(ad[:], ix[:], float(CAP), rk[:], ALU.mult, ALU.add))
                step(dve.tensor_scalar(ad[:], ad[:], float(NE * CAP), None, ALU.subtract))
                step(dve.tensor_tensor(ad[:], ad[:], kp[:], ALU.mult))
                if not (isinstance(i, int) and i == 0):
                    dve.wait_ge(s_sc[q], i * (16 * G))
                x = dve.tensor_scalar(sl[q][:], ad[:], float(NE * CAP), None, ALU.add)
                x.then_inc(s_sl, 1)
                dve.wait_ge(s_sl, i * 2 + (q + 1))
                step(dve.tensor_copy(k.slot[:, bass.ds(i * 8 + 4 * q, G)], sl[q][:]))
                dve.wait_ge(s_e, i * 2 + (q + 1))
                step(dve.tensor_reduce(se[:], dl[q][:], X, ALU.add))
                step(dve.reciprocal(se[:], se[:]))
                step(dve.tensor_tensor(k.gate[:, bass.ds(i * 8 + 4 * q, G)], se[:], kp[:], ALU.mult))
                assert n[0] == STEPS, n[0]

            def groups(i, nxt):
                for q in range(2):
                    if q == 0:
                        ln_apply(i, 1)
                        if nxt:
                            ln_stats(i + 1, 0)
                    elif nxt:
                        ln_apply(i + 1, 0)
                        ln_stats(i + 1, 1)
                    route_group(i, q)

            ln_stats(0, 0)
            ln_stats(0, 1)
            ln_apply(0, 0)
            dve.wait_ge(s_c, 5)
            groups(0, True)
            with dve.Fori(1, GN // 2 - 1) as i:
                groups(i, True)
            groups(GN // 2 - 1, False)

    clear(nc, used)



def expert_weights(sp, k, ins, e, q):
    pick = lambda n: ins[n][bass.ds(e, 1), :, :].rearrange("a r c -> (a r) c")
    sp.dma_start(k.w1[q][:], pick("L0_ffn_W1").rearrange("(c p) f -> p c f", p=128)).then_inc(k.s_w1[q], 16)
    sp.dma_start(k.w2[q][:], pick("L0_ffn_W2").rearrange("(f p) d -> p f d", p=128)).then_inc(k.s_w2[q], 16)


def experts(nc, k, ins):
    R, J = 92, 3
    NF = FF // 128
    with ExitStack() as ctx:
        sb = lambda n, s, d=F32: ctx.enter_context(nc.sbuf_tensor(n, s, d))
        sem = lambda n: ctx.enter_context(nc.semaphore(n))
        two = lambda n, s, d=F32: [sb(f"{n}{i}", s, d) for i in range(2)]
        xe = two("ex_x", [R, J, D])
        xT = two("ex_xT", [128, 2, CAP])
        hid = two("ex_h", [128, NF, CAP])
        yT = two("ex_yT", [128, 2, CAP])
        ye = two("ex_y", [R, J, D])
        wst = two("ex_tied_w", [128, 4, 2, D])
        s_win = [sem(f"s_ex_tied_w{i}") for i in range(2)]
        s_whi, s_wlo = sem("s_ex_tied_hi"), sem("s_ex_tied_lo")
        s_xe = [sem(f"s_ex_x{i}") for i in range(2)]
        s_T, s_xT, s_h, s_y, s_yT, s_B, s_ye = (
            sem(f"s_ex_{n}") for n in ("turned", "xT", "hidden", "y", "yT", "back", "y_sb"))
        s_hs = [sem("s_ex_h_by_act"), sem("s_ex_h_by_dve")]
        s_out = [sem(f"s_ex_out{i}") for i in range(2)]
        bk = k.bank
        LAST = NE // 2 - 1
        xd = k.xd.rearrange("(e j p) d -> e p j d", e=NE, j=J)
        yd = k.yd.rearrange("(e j p) d -> e p j d", e=NE, j=J)
        pick = lambda t, e: t[bass.ds(e, 1)].rearrange("a p j d -> (a p) j d")
        block = ctx.enter_context(nc.Block())

        @block.gpsimd
        def _(pool):
            tied_weights(nc, k, ins, pool, wst, s_win, s_whi, s_wlo)

        @block.sync
        def _(sp):
            def load(i, q):
                if not (isinstance(i, int) and i == 0):
                    sp.wait_ge(s_T, i * 2 + (q - 1))
                sp.dma_start(xe[q][:], pick(xd, i * 2 + q)).then_inc(s_xe[q], 16)

            def weights(i, q):
                sp.wait_ge(s_y, i * 2 + (q - 1))
                expert_weights(sp, k, ins, i * 2 + q, q)

            def store(i, q):
                sp.wait_ge(s_ye, i * 2 + (q + 1))
                sp.dma_start(pick(yd, i * 2 + q), ye[q][:]).then_inc(s_out[q], 16)

            load(0, 0)
            load(0, 1)
            with sp.Fori(1, NE // 2) as i:
                for q in range(2):
                    load(i, q)
                    weights(i, q)
                    store(i - 1, q)
            store(LAST, 0)
            store(LAST, 1)
            for q in range(2):
                sp.wait_ge(s_out[q], 16 * (NE // 2))

        @block.tensor
        def _(pe):
            def turn(i, q):
                n = i * 2 + q
                pe.wait_ge(s_xe[q], i * 16 + 16)
                if not (isinstance(i, int) and i == 0 and q == 0):
                    pe.wait_ge(s_xT, n)
                for c in range(2):
                    for j in range(J):
                        x = pe.transpose(bk[c][:, R * j:R * j + R], xe[q][:, j, 128 * c:128 * c + 128],
                                         k.ident[0:R, 0:R])
                x.then_inc(s_T, 1)

            def expert(i, q, nxt):
                n = i * 2 + q
                pe.wait_ge(s_xT, n + 1)
                pe.wait_ge(k.s_w1[q], i * 16 + 16)
                for f in range(NF):
                    if not (isinstance(i, int) and i == 0 and q == 0 and f < 2):
                        pe.wait_ge(s_hs[f % 2], n * (NF // 2) + f // 2)
                    for c in range(2):
                        x = pe.matmul(bk[2 + f % 2][:, 0:CAP], k.w1[q][:, c, 128 * f:128 * f + 128],
                                      xT[q][:, c, :], start=(c == 0), stop=(c == 1))
                    x.then_inc(s_h, 1)
                if nxt:
                    turn(*((i, 1) if q == 0 else (i + 1, 0)))
                pe.wait_ge(k.s_w2[q], i * 16 + 16)
                for e in range(2):
                    pe.wait_ge(s_hs[e], n * (NF // 2) + NF // 2)
                if not (isinstance(i, int) and i == 0 and q == 0):
                    pe.wait_ge(s_yT, n)
                for c in range(2):
                    for f in range(NF):
                        x = pe.matmul(bk[4 + c][:, 0:CAP], k.w2[q][:, f, 128 * c:128 * c + 128], hid[q][:, f, :],
                                      start=(f == 0), stop=(f == NF - 1))
                x.then_inc(s_y, 1)

            def back(i, q):
                n = i * 2 + q
                pe.wait_ge(s_yT, n + 1)
                if not (isinstance(i, int) and i == 0 and q == 0):
                    pe.wait_ge(s_ye, n)
                for j in range(J):
                    for c in range(2):
                        o = D * (j % 2) + 128 * c
                        x = pe.transpose(bk[6 + j // 2][0:R, o:o + 128], yT[q][:, c, R * j:R * j + R], k.ident[:])
                x.then_inc(s_B, 1)

            turn(0, 0)
            expert(0, 0, True)
            back(0, 0)
            expert(0, 1, True)
            back(0, 1)
            with pe.Fori(1, LAST) as i:
                for q in range(2):
                    expert(i, q, True)
                    back(i, q)
            expert(LAST, 0, True)
            back(LAST, 0)
            expert(LAST, 1, False)
            back(LAST, 1)

        @block.scalar
        def _(act):
            def expert(i, q):
                n = i * 2 + q
                for f in range(0, NF, 2):
                    act.wait_ge(s_h, n * NF + f + 1)
                    act.activation(hid[q][:, f, :], bk[2][:, 0:CAP], ACT.Relu).then_inc(s_hs[0], 1)
                act.wait_ge(s_y, n + 1)
                act.activation(yT[q][:], k.ps[:, 4:6, 0:CAP], ACT.Copy).then_inc(s_yT, 1)

            with act.Fori(0, NE // 2) as i:
                expert(i, 0)
                expert(i, 1)

        @block.vector
        def _(dve):
            def rows(i, q):
                dve.wait_ge(s_T, i * 2 + (q + 1))
                dve.tensor_copy(xT[q][:], k.ps[:, 0:2, 0:CAP]).then_inc(s_xT, 1)

            def expert(i, q, nxt):
                n = i * 2 + q
                for f in range(1, NF, 2):
                    dve.wait_ge(s_h, n * NF + f + 1)
                    dve.tensor_scalar(hid[q][:, f, :], bk[3][:, 0:CAP], 0.0, None, ALU.max).then_inc(s_hs[1], 1)
                if nxt:
                    rows(*((i, 1) if q == 0 else (i + 1, 0)))
                dve.wait_ge(s_B, n + 1)
                if not (isinstance(i, int) and i == 0):
                    dve.wait_ge(s_out[q], i * 16)
                dve.tensor_copy(ye[q][:, 0:2, :].rearrange("p j d -> p (j d)"), bk[6][0:R, :])
                dve.tensor_copy(ye[q][:, 2, :], bk[7][0:R, 0:D]).then_inc(s_ye, 1)

            rows(0, 0)
            expert(0, 0, True)
            expert(0, 1, True)
            with dve.Fori(1, LAST) as i:
                expert(i, 0, True)
                expert(i, 1, True)
            expert(LAST, 0, True)
            expert(LAST, 1, False)


def tied_weights(nc, k, ins, pool, wst, s_in, s_hi, s_lo):
    w = ins["L1_attn_weight"].rearrange("(h c p) e -> p h c e", c=2, p=128)

    def load(g):
        pool.dma_start(wst[g % 2][:], w[:, 4 * g:4 * g + 4]).then_inc(s_in[g % 2], 16)

    load(0)
    load(1)
    for g in range(4):
        flat = lambda t: t.rearrange("p h c e -> p (h c e)")
        hi, lo, src = flat(k.wlh[:, 4 * g:4 * g + 4]), flat(k.wll[:, 4 * g:4 * g + 4]), flat(wst[g % 2][:])
        pool.wait_ge(s_in[g % 2], 16 * (g // 2) + 16)
        pool.tensor_copy(hi, src).then_inc(s_hi, 1)
        pool.wait_ge(s_hi, g + 1)
        pool.tensor_tensor(lo, src, hi, ALU.subtract).then_inc(s_lo, 1)
        if g < 2:
            pool.wait_ge(s_lo, g + 1)
            load(g + 2)
    pool.wait_ge(s_lo, 4)


def tied_attention(nc, k, ins):
    with ExitStack() as ctx:
        sb = lambda n, s, d=F32: ctx.enter_context(nc.sbuf_tensor(n, s, d))
        used = []
        sem = lambda n: used.append(ctx.enter_context(nc.semaphore(n))) or used[-1]
        two = lambda n, s, d=F32: [sb(f"{n}{i}", s, d) for i in range(2)]
        four = lambda n, s, d=F32: [sb(f"{n}{i}", s, d) for i in range(4)]
        yg = [two(f"ta_row{p}_", [NT, D]) for p in range(2)]
        sl = two("ta_slot", [NT, 2], U32)
        st = sb("ta_st", [NT, 2, 6])
        mv = sb("ta_mv", [NT, 2, 2])
        rs = sb("ta_rs", [NT, 2])
        xn = two("ta_x", [NT, 2, D])
        xh = sb("ta_xhi", [NT, 4, D], F32R)
        xl = sb("ta_xlo", [NT, 4, D], F32R)
        yT = sb("ta_yT", [128, 2, Q4])
        yd = four("ta_ydiag", [128, HALF])
        eb = four("ta_e", [NT, HALF])
        sm = four("ta_sum", [NT, 8])
        rc = four("ta_rc", [NT, 8])
        ah = two("ta_at_hi", [NT, HALF], F32R)
        al = two("ta_at_lo", [NT, HALF], F32R)
        oh = two("ta_o_hi", [128, 4, 2, Q4], F32R)
        ol = two("ta_o_lo", [128, 4, 2, Q4], F32R)
        wT = sb("ta_wT", [128, 2, Q4])
        s_z, s_sl, s_row, s_st, s_mv, s_ve, s_rs, s_xn = (
            sem(f"s_ta_{n}") for n in ("zeroed", "slot", "row_added", "stats", "mv", "vareps", "rstd", "x"))
        s_yg = [sem(f"s_ta_rows{p}") for p in range(2)]
        s_xh, s_xl, s_F, s_yT = (sem(f"s_ta_{n}") for n in ("xhi", "xlo", "front", "yT"))
        s_yd, s_S, s_exp, s_sum, s_rc, s_nrm, s_T, s_ah, s_al = (
            sem(f"s_ta_{n}") for n in ("ydiag", "scores", "exp", "sum", "recip", "norm", "turned", "at_hi", "at_lo"))
        s_av, s_oh, s_ol = (sem(f"s_ta_{n}") for n in ("av", "o_hi", "o_lo"))
        s_W0 = sem("s_ta_first_half_by_w")
        s_Wg = sem("s_ta_group_by_w")
        s_wT = [sem(f"s_ta_wT{e}") for e in range(2)]
        s_B, s_add = sem("s_ta_back"), sem("s_ta_added")
        sc = k.ps[:, 0:2, :]
        tb = k.ps[:, 2:4, :]
        vb = k.ps[:, 4:6, :]
        wb = [k.bank[6], k.bank[7]]
        QUADS = NB // 4
        LAST = QUADS - 1
        zero = lambda n: isinstance(n, int) and n == 0

        def later(Q, u, d):
            if u + d < 8:
                return Q, u + d
            if isinstance(Q, int) and Q == LAST:
                return None
            return Q + 1, u + d - 8

        def unit(Q, u):
            return Q * 8 + u

        def all_quads(eng, quad):
            quad(0, True, True)
            with eng.Fori(1, LAST) as Q:
                quad(Q, False, True)
            quad(LAST, False, False)

        block = ctx.enter_context(nc.Block())

        @block.tensor
        def _(pe):
            def front(Q, p):
                pe.wait_ge(s_xn, Q * 2 + (p + 1))
                for c in range(2):
                    for j in range(2):
                        o = W2T * c + NT * j
                        x = pe.transpose(vb[:, 1, o:o + NT], xn[p][:, j, 128 * c:128 * c + 128],
                                         k.ident[0:NT, 0:NT])
                x.then_inc(s_F, 1)

            def back(Q, p):
                for e in range(2):
                    pe.wait_ge(s_wT[e], Q + 1)
                for j in range(2):
                    for e in range(2):
                        o, t = D * j + 128 * e, NT * (2 * p + j)
                        x = pe.transpose(vb[0:NT, 0, o:o + 128], wT[:, e, t:t + NT], k.ident[:])
                x.then_inc(s_B, 1)

            def scores(Q, u):
                g, p = u // 2, u % 2
                n = unit(Q, u)
                pe.wait_ge(s_yd, n + 1)
                if not zero(n):
                    pe.wait_ge(s_exp, n)
                for j in range(2):
                    t = NT * (2 * p + j)
                    x = pe.matmul(sc[0:NT, j, 0:CW], yT[:, g // 2, t:t + NT],
                                  yd[u % 4][:, CW * j:CW * j + CW], start=True, stop=True)
                x.then_inc(s_S, 1)

            def turn(Q, u):
                n = unit(Q, u)
                pe.wait_ge(s_nrm, n + 1)
                if not zero(n):
                    pe.wait_ge(s_al, n)
                for h in range(8):
                    x = pe.transpose(tb[0:NT, h // 4, NT * (h % 4):NT * (h % 4) + NT],
                                     eb[u % 4][:, NT * h:NT * h + NT], k.ident[0:NT, 0:NT])
                x.then_inc(s_T, 1)

            def weigh(Q, u, c):
                n, p = unit(Q, u), u % 2
                if not (zero(n) and c == 0):
                    pe.wait_ge(s_ol, n * 2 + c)
                for j in range(2):
                    x_hi = xh[:, 2 * p + j, 128 * c:128 * c + 128]
                    x_lo = xl[:, 2 * p + j, 128 * c:128 * c + 128]
                    a_hi, a_lo = ah[u % 2][:, CW * j:CW * j + CW], al[u % 2][:, CW * j:CW * j + CW]
                    o = vb[:, j, 0:CW]
                    pe.matmul(o, x_hi, a_hi, start=True, stop=False)
                    pe.matmul(o, x_hi, a_lo, start=False, stop=False)
                    x = pe.matmul(o, x_lo, a_hi, start=False, stop=True)
                x.then_inc(s_av, 1)

            def times_w(Q, u, part):
                e, g = u % 2, (u // 2 - 1) % 4
                if e == 0:
                    pe.wait_ge(s_ol, unit(Q, u) * 2 - 1 + part)
                if part == 0 and g == 0 and not zero(Q):
                    pe.wait_ge(s_wT[e], Q)
                for t in (range(3), range(3, 8))[part]:
                    c, h = t // 4, t % 4
                    w_hi = k.wlh[:, 4 * g + h, c, 128 * e:128 * e + 128]
                    w_lo = k.wll[:, 4 * g + h, c, 128 * e:128 * e + 128]
                    o_hi, o_lo = oh[g % 2][:, h, c, :], ol[g % 2][:, h, c, :]
                    o = wb[e][:, 0:Q4]
                    pe.matmul(o, w_hi, o_hi, start=(g == 0 and t == 0), stop=False)
                    pe.matmul(o, w_hi, o_lo, start=False, stop=False)
                    x = pe.matmul(o, w_lo, o_hi, start=False, stop=(g == 3 and t == 7))
                if part == 1 and e == 1:
                    x.then_inc(s_Wg, 1)
                elif part == 1 and g == 3:
                    x.then_inc(s_W0, 1)

            def quad(Q, first, nxt):
                for u in range(8):
                    n = unit(Q, u)
                    w = u >= 2 or not first
                    fr = nxt and u in (5, 6)
                    bk = not first and u in (2, 3)
                    turn(Q, u)
                    n2 = later(Q, u, 2)
                    if n2:
                        scores(*n2)
                    if fr or bk:
                        pe.wait_ge(s_ol, n * 2)
                    if fr:
                        front(Q + 1, u - 5)
                    if bk:
                        back(Q - 1, u - 2)
                    if w:
                        times_w(Q, u, 0)
                    pe.wait_ge(s_al, n + 1)
                    if u < 2:
                        pe.wait_ge(s_xl, Q * 2 + (u + 1))
                    if fr:
                        pe.wait_ge(s_yT, Q * 2 + (u - 2))
                    if bk:
                        pe.wait_ge(s_add, Q * 2 + (u - 3))
                    weigh(Q, u, 0)
                    if w:
                        times_w(Q, u, 1)
                    weigh(Q, u, 1)

            front(0, 0)
            pe.wait_ge(s_yT, 1)
            front(0, 1)
            scores(0, 0)
            scores(0, 1)
            all_quads(pe, quad)
            for u in range(2):
                for part in range(2):
                    times_w(QUADS, u, part)
            back(LAST, 0)
            pe.wait_ge(s_add, 2 * LAST + 1)
            back(LAST, 1)

        @block.scalar
        def _(act):
            def copy(dst, src):
                return act.activation(dst, src, ACT.Copy)

            def turned_tokens(Q, p):
                act.wait_ge(s_F, Q * 2 + (p + 1))
                copy(yT[:, :, W2T * p:W2T * p + W2T],
                     vb[:, 1, 0:2 * W2T].rearrange("p (c t) -> p c t", c=2)).then_inc(s_yT, 1)

            def x_high(Q, p):
                act.wait_ge(s_xn, Q * 2 + (p + 1))
                if not zero(Q):
                    act.wait_ge(s_av, Q * 16 + (2 * p - 2))
                copy(xh[:, 2 * p:2 * p + 2, :], xn[p][:]).then_inc(s_xh, 1)

            def exps(Q, u):
                act.wait_ge(s_S, unit(Q, u) + 1)
                act.activation(eb[u % 4][:].rearrange("p (c t) -> p c t", c=2), sc[0:NT, :, 0:CW], ACT.Exp,
                               scale=HD ** -0.5).then_inc(s_exp, 1)

            def turned(Q, u):
                act.wait_ge(s_T, unit(Q, u) + 1)
                copy(ah[u % 2][:].rearrange("p (c t) -> p c t", c=2), tb[0:NT, :, 0:CW]).then_inc(s_ah, 1)

            def values(Q, u, c):
                g, p = u // 2, u % 2
                act.wait_ge(s_av, unit(Q, u) * 2 + (c + 1))
                if c == 0 and p == 0 and not (zero(Q) and g < 2):
                    act.wait_ge(s_Wg, Q * 4 + (g - 1))
                copy(oh[g % 2][:, :, c, W2T * p:W2T * p + W2T].rearrange("p h (j t) -> p j h t", j=2),
                     vb[:, :, 0:CW].rearrange("p j (h t) -> p j h t", h=4)).then_inc(s_oh, 1)

            def product(Q, e):
                act.wait_ge(s_W0 if e == 0 else s_Wg, Q + 1 if e == 0 else Q * 4 + 4)
                copy(wT[:, e, :], wb[e][:, 0:Q4]).then_inc(s_wT[e], 1)

            def quad(Q, first, nxt):
                for u in range(8):
                    turned(Q, u)
                    n2 = later(Q, u, 2)
                    if n2:
                        exps(*n2)
                    if nxt and u in (5, 6):
                        turned_tokens(Q + 1, u - 5)
                    if nxt and u == 7:
                        x_high(Q + 1, 0)
                    if not first and u == 0:
                        x_high(Q, 1)
                    values(Q, u, 0)
                    values(Q, u, 1)
                    if not first and u < 2:
                        product(Q - 1, u)

            for p in range(2):
                turned_tokens(0, p)
                x_high(0, p)
            exps(0, 0)
            exps(0, 1)
            all_quads(act, quad)
            product(LAST, 0)
            product(LAST, 1)

        @block.vector
        def _(dve):
            def add_rows(Q, p):
                dve.wait_ge(s_yg[p], Q * 32 + 32)
                for j in range(2):
                    h = k.sample(Q * 4 + (2 * p + j))
                    x = dve.scalar_tensor_tensor(h, yg[p][j][:], k.gate[:, bass.ds(Q * 4 + (2 * p + j), 1)], h,
                                                 ALU.mult, ALU.add)
                x.then_inc(s_row, 1)

            def ln_stats(Q, p):
                m = Q * 2 + (p + 1)
                dve.wait_ge(s_row, m)
                dve.sem_inc(k.s_hold, 1)
                for j in range(2):
                    x = dve.bn_stats(st[:, j, :], k.sample(Q * 4 + (2 * p + j)))
                x.then_inc(s_st, 1)
                dve.wait_ge(s_st, m)
                dve.sem_inc(k.s_hold, 1)
                for j in range(2):
                    x = dve.bn_aggr(mv[:, j, :], st[:, j, :])
                x.then_inc(s_mv, 1)
                dve.wait_ge(s_mv, m)
                dve.tensor_scalar(rs[:], mv[:, :, 1], EPS, None, ALU.add).then_inc(s_ve, 1)

            def ln_apply(Q, p):
                dve.wait_ge(s_rs, Q * 2 + (p + 1))
                if not zero(Q):
                    dve.wait_ge(s_xl, Q * 2 + (p - 1))
                for j in range(2):
                    x = dve.tensor_scalar(xn[p][:, j, :], k.sample(Q * 4 + (2 * p + j)), mv[:, j, 0:1],
                                          rs[:, j:j + 1], ALU.subtract, ALU.mult)
                x.then_inc(s_xn, 1)

            def sums(Q, u):
                n = unit(Q, u)
                dve.wait_ge(s_exp, n + 1)
                dve.tensor_reduce(sm[u % 4][:], eb[u % 4][:].rearrange("p (h t) -> p h t", h=8), X,
                                  ALU.add).then_inc(s_sum, 1)
                dve.wait_ge(s_sum, n + 1)
                dve.reciprocal(rc[u % 4][:], sm[u % 4][:]).then_inc(s_rc, 1)

            def turned(Q, u):
                dve.wait_ge(s_ah, unit(Q, u) + 1)
                r = lambda t: t.rearrange("p (c t) -> p c t", c=2)
                dve.tensor_tensor(r(al[u % 2][:]), tb[0:NT, :, 0:CW], r(ah[u % 2][:]),
                                  ALU.subtract).then_inc(s_al, 1)

            def values(Q, u, c):
                g, p = u // 2, u % 2
                dve.wait_ge(s_oh, unit(Q, u) * 2 + (c + 1))
                r = lambda t: t[g % 2][:, :, c, W2T * p:W2T * p + W2T].rearrange("p h (j t) -> p j h t", j=2)
                dve.tensor_tensor(r(ol), vb[:, :, 0:CW].rearrange("p j (h t) -> p j h t", h=4), r(oh),
                                  ALU.subtract).then_inc(s_ol, 1)

            def add(Q, p):
                dve.wait_ge(s_B, Q * 2 + (p + 1))
                h = k.samples(Q * 4 + 2 * p, 2)
                dve.tensor_tensor(h, h, vb[0:NT, 0, :], ALU.add).then_inc(s_add, 1)

            def quad(Q, first, nxt):
                for u in range(8):
                    turned(Q, u)
                    n1 = later(Q, u, 1)
                    if not first and u in (2, 3):
                        add(Q - 1, u - 2)
                    if n1:
                        sums(*n1)
                    values(Q, u, 0)
                    if nxt and u in (3, 5):
                        ln_apply(Q + 1, (u - 3) // 2)
                    if nxt and u in (1, 3):
                        add_rows(Q + 1, (u - 1) // 2)
                    if nxt and u in (2, 4):
                        ln_stats(Q + 1, (u - 2) // 2)
                    values(Q, u, 1)

            for p in range(2):
                add_rows(0, p)
                ln_stats(0, p)
                ln_apply(0, p)
            sums(0, 0)
            all_quads(dve, quad)
            add(LAST, 0)
            add(LAST, 1)

        @block.gpsimd
        def _(pool):
            def rows(Q, p):
                if not zero(Q):
                    pool.wait_ge(s_row, Q * 2 + (p - 1))
                    pool.sem_inc(k.s_hold, 1)
                pool.tensor_copy(sl[p][:], k.slot[:, bass.ds(Q * 4 + 2 * p, 2)]).then_inc(s_sl, 1)
                pool.wait_ge(s_sl, Q * 2 + (p + 1))
                pool.sem_inc(k.s_hold, 1)
                for j in range(2):
                    pool.indirect_dma_start(out=yg[p][j][:], out_offset=None, in_=k.yd[:],
                                            in_offset=bass.IndirectOffsetOnAxis(sl[p][:, j:j + 1], 0),
                                            bounds_check=NE * CAP - 1, oob_is_err=False).then_inc(s_yg[p], 16)

            def rstd(Q, p):
                pool.wait_ge(s_ve, Q * 2 + (p + 1))
                pool.tensor_tensor(rs[:], rs[:], k.mhalf[0:NT, 0:2], ALU.pow).then_inc(s_rs, 1)

            def x_low(Q, p):
                pool.wait_ge(s_xh, Q * 2 + (p + 1))
                v = slice(2 * p, 2 * p + 2)
                pool.tensor_tensor(xl[:, v, :], xn[p][:], xh[:, v, :], ALU.subtract).then_inc(s_xl, 1)

            def diagonal(Q, u):
                g, p = u // 2, u % 2
                if u < 2:
                    pool.wait_ge(s_yT, Q * 2 + (u + 1))
                y = yT[:, g // 2, W2T * p:W2T * p + W2T].rearrange("p (j t) -> p j t", j=2)
                mask = k.mask[:, 4 * (g % 2):4 * (g % 2) + 4]
                pool.tensor_tensor(yd[u % 4][:].rearrange("p (j h t) -> p j h t", j=2, h=4),
                                   y.unsqueeze(2).broadcast_to([128, 2, 4, NT]),
                                   mask.unsqueeze(1).unsqueeze(3).broadcast_to([128, 2, 4, NT]),
                                   ALU.mult).then_inc(s_yd, 1)

            def norm(Q, u):
                pool.wait_ge(s_rc, unit(Q, u) + 1)
                e = eb[u % 4][:].rearrange("p (h t) -> p h t", h=8)
                pool.tensor_tensor(e, e, rc[u % 4][:].unsqueeze(2).broadcast_to([NT, 8, NT]),
                                   ALU.mult).then_inc(s_nrm, 1)

            def quad(Q, first, nxt):
                for u in range(8):
                    n1, n3 = later(Q, u, 1), later(Q, u, 3)
                    if n1:
                        norm(*n1)
                    if n3:
                        diagonal(*n3)
                    if nxt and u == 7:
                        x_low(Q + 1, 0)
                    if not first and u == 0:
                        x_low(Q, 1)
                    if nxt and u in (0, 1):
                        rows(Q + 1, u)
                    if nxt and u in (2, 4):
                        rstd(Q + 1, (u - 2) // 2)

            for p in range(2):
                for j in range(2):
                    pool.memset(yg[p][j][:], 0.0).then_inc(s_z, 1)
            pool.wait_ge(s_z, 4)
            rows(0, 0)
            rows(0, 1)
            rstd(0, 0)
            rstd(0, 1)
            for u in range(3):
                diagonal(0, u)
            x_low(0, 0)
            x_low(0, 1)
            norm(0, 0)
            all_quads(pool, quad)

    clear(nc, used)


QMAX = 127.0
ROUND = 1.5 * 2.0 ** 23
FI = 704
MI = (FI + 127) // 128
PART = [min(128, FI - 128 * m) for m in range(MI)]


def mlp(nc, k, ins, out):
    G = 4
    GN = NB // G
    GT = G * NT
    with ExitStack() as ctx:
        sb = lambda n, s, d=F32: ctx.enter_context(nc.sbuf_tensor(n, s, d))
        sem = lambda n: ctx.enter_context(nc.semaphore(n))
        two = lambda n, s, d=F32: [sb(f"{n}{i}", s, d) for i in range(2)]
        identb = sb("ml_ident", [128, 128], BF16)
        wgT = sb("ml_wgT", [128, 2, FI], BF16)
        wuT = sb("ml_wuT", [128, 2, FI], BF16)
        wdT = sb("ml_wdT", [128, MI, D], BF16)
        sg = sb("ml_sg", [128, MI])
        su = sb("ml_su", [128, MI])
        sd = sb("ml_sd", [128, 2])
        srow = sb("ml_srow", [NT, D])
        clip = sb("ml_clip", [128, 2])
        sig = sb("ml_sig", [128, 2])
        amx = sb("ml_amx", [128, NB])
        gmx = sb("ml_gmx", [128, 1])
        amax = sb("ml_amax", [128, 1])
        sx = sb("ml_sx", [128, 1])
        ix = sb("ml_ix", [128, 1])
        xn = sb("ml_x", [NT, NB, D])
        hh = sb("ml_h", [128, MI, NB * NT])
        hmx = sb("ml_hmx", [128, GN * MI])
        sh = sb("ml_sh", [128, 1])
        ih = sb("ml_ih", [128, 1])
        bk = k.bank
        bkb = [b.bitcast(BF16) for b in bk]

        with ExitStack() as c2:
            wg = c2.enter_context(nc.sbuf_tensor("ml_wg", [128, MI, D], F32))
            wu = c2.enter_context(nc.sbuf_tensor("ml_wu", [128, MI, D], F32))
            wd = c2.enter_context(nc.sbuf_tensor("ml_wd", [128, 2, FI], F32))
            wgb = c2.enter_context(nc.sbuf_tensor("ml_wgb", [128, MI, D], BF16))
            wub = c2.enter_context(nc.sbuf_tensor("ml_wub", [128, MI, D], BF16))
            wdb = c2.enter_context(nc.sbuf_tensor("ml_wdb", [128, 2, FI], BF16))
            inv = c2.enter_context(nc.sbuf_tensor("ml_inv", [128, 2 * MI + 2], F32))
            s_w, s_z, s_id, s_ch, s_q, s_T, s_e, s_clip = (
                sem(f"s_mw_{n}") for n in ("loaded", "zero", "ident", "step", "whole", "turned", "sb", "clip"))
            with nc.Block() as block:
                @block.sync
                def _(sp):
                    sp.wait_ge(s_z, 2)
                    for w, n in ((wg, "w_gate"), (wu, "w_up")):
                        src = ins[f"L1_ffn_{n}"]
                        sp.dma_start(w[:, 0:MI - 1, :], src[0:128 * (MI - 1), :]
                                     .rearrange("(m p) d -> p m d", p=128)).then_inc(s_w, 16)
                        sp.dma_start(w[0:PART[-1], MI - 1, :], src[128 * (MI - 1):FI, :]).then_inc(s_w, 16)
                    sp.dma_start(wd[:], ins["L1_ffn_w_down"].rearrange("(c p) i -> p c i", p=128)).then_inc(s_w, 16)
                    for j, n in enumerate(("x", "down")):
                        sp.dma_start(clip[:, j:j + 1], ins[f"L1_ffn_clip_{n}"].rearrange("(a b) -> a b", a=1)
                                     .broadcast_to([128, 1])).then_inc(s_clip, 16)

                @block.gpsimd
                def _(pool):
                    pool.memset(wg[:, MI - 1, :], 1.0).then_inc(s_z, 1)
                    pool.memset(wu[:, MI - 1, :], 1.0).then_inc(s_z, 1)
                    pool.tensor_copy(identb[:], k.ident[:]).then_inc(s_id, 1)

                @block.vector
                def _(dve):
                    n = [0]

                    def step(x):
                        n[0] += 1
                        x.then_inc(s_ch, 1)
                        dve.wait_ge(s_ch, n[0])

                    dve.wait_ge(s_w, 80)
                    for w, s in ((wg, sg), (wu, su), (wd, sd)):
                        x = dve.tensor_reduce(s[:], w[:], X, ALU.max, apply_absolute_value=True)
                    step(x)
                    for s in (sg, su, sd):
                        x = dve.tensor_scalar(s[:], s[:], 1.0 / QMAX, None, ALU.mult)
                    step(x)
                    dve.reciprocal(inv[:, 0:MI], sg[:])
                    dve.reciprocal(inv[:, MI:2 * MI], su[:])
                    step(dve.reciprocal(inv[:, 2 * MI:2 * MI + 2], sd[:]))
                    for w, o, m in ((wg, 0, MI), (wu, MI, MI), (wd, 2 * MI, 2)):
                        for j in range(m):
                            x = dve.tensor_scalar(w[:, j, :], w[:, j, :], inv[:, o + j:o + j + 1], ROUND,
                                                  ALU.mult, ALU.add)
                    step(x)
                    for w, b in ((wg, wgb), (wu, wub), (wd, wdb)):
                        dve.tensor_scalar(b[:].rearrange("p m d -> p (m d)"), w[:].rearrange("p m d -> p (m d)"),
                                          ROUND, QMAX, ALU.subtract, ALU.min).then_inc(s_q, 1)

                @block.tensor
                def _(pe):
                    pe.wait_ge(s_id, 1)
                    pe.wait_ge(s_q, 3)
                    for w, b, o in ((wg, wgb, 0), (wu, wub, 2)):
                        for c in range(2):
                            for m in range(MI):
                                x = pe.transpose(bkb[o + c][:, 128 * m:128 * m + PART[m]],
                                                 b[0:PART[m], m, 128 * c:128 * c + 128],
                                                 identb[0:PART[m], 0:PART[m]])
                        x.then_inc(s_T, 1)
                    for m in range(MI):
                        for c in range(2):
                            o = D * (m % 4) + 128 * c
                            x = pe.transpose(bkb[4 + m // 4][0:PART[m], o:o + 128],
                                             wdb[:, c, 128 * m:128 * m + PART[m]], identb[:])
                    x.then_inc(s_T, 1)
                    for c in range(2):
                        x = pe.matmul(bk[6][0:NT, 128 * c:128 * c + 128], sd[:, c:c + 1].broadcast_to([128, NT]),
                                      k.ident[:], start=True, stop=True)
                    x.then_inc(s_T, 1)

                @block.scalar
                def _(act):
                    act.wait_ge(s_clip, 32)
                    act.activation(sig[:], clip[:], ACT.Sigmoid)
                    for t, (w, o) in enumerate(((wgT, 0), (wuT, 2))):
                        act.wait_ge(s_T, t + 1)
                        for c in range(2):
                            act.activation(w[:, c, :], bkb[o + c][:, 0:FI], ACT.Copy)
                    act.wait_ge(s_T, 3)
                    act.activation(wdT[:, 0:4, :].rearrange("p m d -> p (m d)"), bkb[4][:, 0:4 * D], ACT.Copy)
                    act.activation(wdT[:, 4, :], bkb[5][:, 0:D], ACT.Copy)
                    act.activation(wdT[0:PART[-1], 5, :], bkb[5][0:PART[-1], D:2 * D], ACT.Copy)
                    act.wait_ge(s_T, 4)
                    act.activation(srow[:], bk[6][0:NT, 0:D], ACT.Copy)

        with ExitStack() as c2:
            st = c2.enter_context(nc.sbuf_tensor("ml_st", [NT, NB, 6], F32))
            mv = c2.enter_context(nc.sbuf_tensor("ml_mv", [NT, NB, 2], F32))
            rs = c2.enter_context(nc.sbuf_tensor("ml_rs", [NT, NB], F32))
            s_z, s_st, s_mv, s_ve, s_rs, s_x, s_mx, s_g, s_gd = (
                sem(f"s_ml_{n}") for n in
                ("zero", "stats", "meanvar", "vareps", "rstd", "x", "max", "gmax", "scale"))
            with nc.Block() as block:
                @block.vector
                def _(dve):
                    with dve.Fori(0, NB) as b:
                        dve.bn_stats(st[:, bass.ds(b, 1), :].rearrange("p a s -> p (a s)"), k.sample(b)).then_inc(s_st, 1)
                    dve.wait_ge(s_st, NB)
                    for b in range(NB):
                        x = dve.bn_aggr(mv[:, b, :], st[:, b, :])
                    x.then_inc(s_mv, 1)
                    dve.wait_ge(s_mv, 1)
                    dve.tensor_scalar(rs[:], mv[:, :, 1], EPS, None, ALU.add).then_inc(s_ve, 1)
                    dve.memset(amx[:], 0.0).then_inc(s_z, 1)
                    dve.wait_ge(s_z, 1)
                    dve.wait_ge(s_rs, NB // 8)
                    with dve.Fori(0, NB) as b:
                        x1 = xn[:, bass.ds(b, 1), :].rearrange("p a d -> p (a d)")
                        dve.tensor_scalar(x1, k.sample(b), mv[:, bass.ds(b, 1), 0], rs[:, bass.ds(b, 1)],
                                          ALU.subtract, ALU.mult).then_inc(s_x, 1)
                    with dve.Fori(0, GN) as g:
                        dve.wait_ge(s_x, g * G + G)
                        dve.tensor_reduce(amx[0:NT, bass.ds(g * G, G)], xn[:, bass.ds(g * G, G), :], X, ALU.max,
                                          apply_absolute_value=True).then_inc(s_mx, 1)
                    dve.wait_ge(s_mx, GN)
                    dve.tensor_reduce(gmx[:], amx[:], X, ALU.max).then_inc(s_g, 1)
                    dve.wait_ge(s_gd, 1)
                    dve.scalar_tensor_tensor(sx[:], amax[:], 1.0 / QMAX, sig[:, 0:1], ALU.mult, ALU.mult).then_inc(s_g, 1)
                    dve.wait_ge(s_g, 2)
                    dve.reciprocal(ix[:], sx[:])
                    dve.tensor_scalar(sg[:], sg[:], sx[:, 0:1], None, ALU.mult)
                    dve.tensor_scalar(su[:], su[:], sx[:, 0:1], None, ALU.mult)

                @block.gpsimd
                def _(pool):
                    pool.wait_ge(s_ve, 1)
                    for j in range(NB // 8):
                        v = rs[:, 8 * j:8 * j + 8]
                        pool.tensor_tensor(v, v, k.mhalf[0:NT, :], ALU.pow).then_inc(s_rs, 1)
                    pool.wait_ge(s_g, 1)
                    pool.partition_all_reduce(amax[:], gmx[:], 128, bass.bass_isa.ReduceOp.max).then_inc(s_gd, 1)

        with ExitStack() as c2:
            xq = [c2.enter_context(nc.sbuf_tensor(f"ml_xq{i}", [NT, G, D], F32)) for i in range(2)]
            xb = [c2.enter_context(nc.sbuf_tensor(f"ml_xb{i}", [NT, G, D], BF16)) for i in range(2)]
            xT = [c2.enter_context(nc.sbuf_tensor(f"ml_xT{i}", [128, 2, GT], BF16)) for i in range(2)]
            gt = [c2.enter_context(nc.sbuf_tensor(f"ml_gt{i}", [128, GT], F32)) for i in range(2)]
            magic = c2.enter_context(nc.sbuf_tensor("ml_magic", [128, 1], F32))
            s_z, s_q1, s_q2, s_xb, s_T, s_xT, s_gate, s_up, s_gt, s_h, s_mx, s_g, s_gd = (
                sem(f"s_mg_{n}") for n in ("zero", "q1", "q2", "xb", "turned", "xT", "gate", "up", "silu", "h", "max",
                                           "gmax", "scale"))
            with nc.Block() as block:
                @block.gpsimd
                def _(pool):
                    pool.memset(hmx[:], 0.0).then_inc(s_z, 1)
                    pool.memset(hh[:, MI - 1, :], 0.0).then_inc(s_z, 1)
                    pool.memset(magic[:], -ROUND).then_inc(s_z, 1)
                    pool.wait_ge(s_g, 1)
                    pool.partition_all_reduce(amax[:], gmx[:], 128, bass.bass_isa.ReduceOp.max).then_inc(s_gd, 1)

                @block.tensor
                def _(pe):
                    def group(i, q):
                        n = i * 2 + q
                        pe.wait_ge(s_xb, n + 1)
                        if not (isinstance(i, int) and i == 0 and q == 0):
                            pe.wait_ge(s_xT, n)
                        for c in range(2):
                            for j in range(G):
                                x = pe.transpose(bkb[c][:, (NT + 1) * j:(NT + 1) * j + NT],
                                                 xb[q][:, j, 128 * c:128 * c + 128], identb[0:NT, 0:NT])
                        x.then_inc(s_T, 1)
                        pe.wait_ge(s_xT, n + 1)
                        for m in range(MI):
                            r = n * MI + m
                            b = m % 2
                            if not (isinstance(i, int) and i == 0 and q == 0 and m < 2):
                                pe.wait_ge(s_gt, r - 1)
                            for c in range(2):
                                x = pe.matmul(bk[2 + b][0:PART[m], 0:GT], wgT[:, c, 128 * m:128 * m + PART[m]],
                                              xT[q][:, c, :], start=(c == 0), stop=(c == 1))
                            x.then_inc(s_gate, 1)
                            if not (isinstance(i, int) and i == 0 and q == 0 and m < 2):
                                pe.wait_ge(s_h, r - 1)
                            for c in range(2):
                                x = pe.matmul(bk[4 + b][0:PART[m], 0:GT], wuT[:, c, 128 * m:128 * m + PART[m]],
                                              xT[q][:, c, :], start=(c == 0), stop=(c == 1))
                            x.then_inc(s_up, 1)

                    group(0, 0)
                    group(0, 1)
                    with pe.Fori(1, GN // 2) as i:
                        group(i, 0)
                        group(i, 1)

                @block.scalar
                def _(act):
                    def whole(i, q):
                        n = i * 2 + q
                        act.wait_ge(s_q2, n + 1)
                        if not (isinstance(i, int) and i == 0):
                            act.wait_ge(s_T, n - 1)
                        act.activation(xb[q][:], xq[q][:], ACT.Identity, bias=magic[0:NT, 0:1]).then_inc(s_xb, 1)

                    def group(i, q, nxt):
                        n = i * 2 + q
                        act.wait_ge(s_T, n + 1)
                        for c in range(2):
                            x = act.activation(xT[q][:, c, :].rearrange("p (j t) -> p j t", j=G),
                                               bkb[c][:, 0:G * (NT + 1)].rearrange("p (j t) -> p j t", j=G)[:, :, 0:NT],
                                               ACT.Copy)
                        x.then_inc(s_xT, 1)
                        for m in range(MI):
                            r = n * MI + m
                            act.wait_ge(s_gate, r + 1)
                            if not (isinstance(i, int) and i == 0 and q == 0 and m < 2):
                                act.wait_ge(s_h, r - 1)
                            p = PART[m]
                            act.activation(gt[m % 2][0:p, :], bk[2 + m % 2][0:p, 0:GT], ACT.Silu,
                                           scale=sg[0:p, m:m + 1]).then_inc(s_gt, 1)
                            if m == 2 and nxt:
                                whole(*((i, 1) if q == 0 else (i + 1, 0)))

                    act.wait_ge(s_z, 3)
                    whole(0, 0)
                    group(0, 0, True)
                    group(0, 1, True)
                    with act.Fori(1, GN // 2 - 1) as i:
                        group(i, 0, True)
                        group(i, 1, True)
                    group(GN // 2 - 1, 0, True)
                    group(GN // 2 - 1, 1, False)

                @block.vector
                def _(dve):
                    def scaled(i, q):
                        n = i * 2 + q
                        if not (isinstance(i, int) and i == 0):
                            dve.wait_ge(s_xb, n - 1)
                        x4 = xn[:, bass.ds(i * (2 * G) + q * G, G), :].rearrange("p j d -> p (j d)")
                        v = xq[q][:].rearrange("p j d -> p (j d)")
                        dve.tensor_scalar(v, x4, ix[0:NT, 0:1], QMAX, ALU.mult, ALU.min).then_inc(s_q1, 1)
                        dve.wait_ge(s_q1, n + 1)
                        dve.tensor_scalar(v, v, -QMAX - 1.0, ROUND, ALU.max, ALU.add).then_inc(s_q2, 1)

                    def group(i, q, nxt):
                        n = i * 2 + q
                        if nxt:
                            scaled(*((i, 1) if q == 0 else (i + 1, 0)))
                        for m in range(MI):
                            r = n * MI + m
                            p = PART[m]
                            dve.wait_ge(s_up, r + 1)
                            dve.wait_ge(s_gt, r + 1)
                            h = hh[0:p, m, bass.ds(i * (2 * GT) + q * GT, GT)]
                            dve.scalar_tensor_tensor(h, bk[4 + m % 2][0:p, 0:GT], su[0:p, m:m + 1],
                                                     gt[m % 2][0:p, :], ALU.mult, ALU.mult).then_inc(s_h, 1)
                            dve.wait_ge(s_h, r + 1)
                            dve.tensor_reduce(hmx[0:p, bass.ds(r, 1)], h, X, ALU.max,
                                              apply_absolute_value=True).then_inc(s_mx, 1)

                    dve.wait_ge(s_z, 3)
                    scaled(0, 0)
                    group(0, 0, True)
                    group(0, 1, True)
                    with dve.Fori(1, GN // 2 - 1) as i:
                        group(i, 0, True)
                        group(i, 1, True)
                    group(GN // 2 - 1, 0, True)
                    group(GN // 2 - 1, 1, False)
                    dve.wait_ge(s_mx, GN * MI)
                    dve.tensor_reduce(gmx[:], hmx[:], X, ALU.max).then_inc(s_g, 1)
                    dve.wait_ge(s_gd, 1)
                    dve.scalar_tensor_tensor(sh[:], amax[:], 1.0 / QMAX, sig[:, 1:2], ALU.mult, ALU.mult).then_inc(s_g, 1)
                    dve.wait_ge(s_g, 2)
                    dve.reciprocal(ih[:], sh[:])
                    dve.tensor_scalar(srow[:], srow[:], sh[0:NT, 0:1], None, ALU.mult)

        with ExitStack() as c2:
            hq = [c2.enter_context(nc.sbuf_tensor(f"ml_hq{i}", [128, MI, GT], F32)) for i in range(2)]
            hb = [c2.enter_context(nc.sbuf_tensor(f"ml_hb{i}", [128, MI, G, NT + 1], BF16)) for i in range(2)]
            dn = [c2.enter_context(nc.sbuf_tensor(f"ml_dn{i}", [NT, G, D], F32)) for i in range(2)]
            magic = c2.enter_context(nc.sbuf_tensor("ml_magic2", [128, 1], F32))
            s_z, s_q1, s_q2, s_hb, s_D, s_dn, s_res = (
                sem(f"s_md_{n}") for n in ("zero", "q1", "q2", "hb", "down", "scaled", "residual"))
            s_out = sem("s_out")
            with nc.Block() as block:
                @block.sync
                def _(sp):
                    with sp.Fori(0, GN) as g:
                        sp.wait_ge(s_res, g + 1)
                        for a, b, c in ((0, NPT, 1), (NPT, NPT + 1, 0), (NPT + 1, NT, NPT + 1)):
                            sp.dma_start(out[bass.ds(g * G, G), c:c + b - a, :].rearrange("b s d -> s b d"),
                                         k.H[a:b, bass.ds(g * G, G), :]).then_inc(s_out, 16)
                    sp.wait_ge(s_out, 48 * GN)

                @block.gpsimd
                def _(pool):
                    pool.memset(magic[:], -ROUND).then_inc(s_z, 1)
                    with pool.Fori(0, GN // 2) as i:
                        for q in range(2):
                            pool.wait_ge(s_dn, i * (2 * G) + (q * G + G))
                            h = k.samples(i * (2 * G) + q * G, G)
                            pool.tensor_tensor(h, h, dn[q][:].rearrange("p j d -> p (j d)"), ALU.add).then_inc(s_res, 1)

                @block.vector
                def _(dve):
                    def scaled(i, q):
                        n = i * 2 + q
                        if not (isinstance(i, int) and i == 0):
                            dve.wait_ge(s_hb, n - 1)
                        h = hh[:, :, bass.ds(i * (2 * GT) + q * GT, GT)]
                        dve.tensor_scalar(hq[q][:], h, ih[:, 0:1], QMAX, ALU.mult, ALU.min).then_inc(s_q1, 1)
                        dve.wait_ge(s_q1, n + 1)
                        v = hq[q][:].rearrange("p m t -> p (m t)")
                        dve.tensor_scalar(v, v, -QMAX - 1.0, ROUND, ALU.max, ALU.add).then_inc(s_q2, 1)

                    def group(i, q, nxt):
                        if nxt:
                            scaled(*((i, 1) if q == 0 else (i + 1, 0)))
                        if not (isinstance(i, int) and i == 0):
                            dve.wait_ge(s_res, i * 2 + (q - 1))
                        for j in range(G):
                            dve.wait_ge(s_D, i * (2 * G) + (q * G + j + 1))
                            dve.tensor_tensor(dn[q][:, j, :], bk[j % 4][0:NT, 0:D], srow[:], ALU.mult).then_inc(s_dn, 1)

                    scaled(0, 0)
                    group(0, 0, True)
                    group(0, 1, True)
                    with dve.Fori(1, GN // 2 - 1) as i:
                        group(i, 0, True)
                        group(i, 1, True)
                    group(GN // 2 - 1, 0, True)
                    group(GN // 2 - 1, 1, False)

                @block.scalar
                def _(act):
                    act.wait_ge(s_z, 1)

                    def whole(i, q):
                        n = i * 2 + q
                        act.wait_ge(s_q2, n + 1)
                        if not (isinstance(i, int) and i == 0):
                            act.wait_ge(s_D, i * (2 * G) + (q * G - G))
                        act.activation(hb[q][:, :, :, 0:NT].rearrange("p m j t -> p (m j) t"),
                                       hq[q][:].rearrange("p m (j t) -> p (m j) t", j=G), ACT.Identity,
                                       bias=magic[:, 0:1]).then_inc(s_hb, 1)

                    whole(0, 0)
                    whole(0, 1)
                    with act.Fori(1, GN // 2) as i:
                        whole(i, 0)
                        whole(i, 1)

                @block.tensor
                def _(pe):
                    def group(i, q):
                        pe.wait_ge(s_hb, i * 2 + (q + 1))
                        for j in range(G):
                            if not (isinstance(i, int) and i == 0 and q == 0):
                                pe.wait_ge(s_dn, i * (2 * G) + (q * G + j - G + 1))
                            for m in range(MI):
                                p = PART[m]
                                x = pe.matmul(bk[j % 4][0:NT, 0:D], hb[q][0:p, m, j, 0:NT], wdT[0:p, m, :],
                                              start=(m == 0), stop=(m == MI - 1))
                            x.then_inc(s_D, 1)

                    group(0, 0)
                    group(0, 1)
                    with pe.Fori(1, GN // 2) as i:
                        group(i, 0)
                        group(i, 1)


def build(nc, ins, out, stages):
    with ExitStack() as ctx:
        sb = lambda n, s, d=F32: ctx.enter_context(nc.sbuf_tensor(n, s, d))
        sem = lambda n: ctx.enter_context(nc.semaphore(n))
        k = Shared()
        k.ps = ctx.enter_context(nc.psum_tensor("ps", [128, 8, 512], F32))
        k.bank = [k.ps[:, b, :] for b in range(8)]
        k.H = sb("H", [NT, NB, D])
        k.sample = lambda b: k.H[:, bass.ds(b, 1), :].rearrange("p a d -> p (a d)")
        k.samples = lambda b, n: k.H[:, bass.ds(b, n), :].rearrange("p a d -> p (a d)")
        k.ident = sb("ident", [128, 128])
        k.mhalf = sb("minus_half", [128, 8])
        k.mask = sb("head_mask", [128, 8])
        k.sem = sem
        k.s_go = sem("s_constants")
        k.s_hold = sem("s_waits_held")
        constants(nc, k, sem)
        k.slot = sb("slot", [NT, NB], U32)
        k.gate = sb("gate", [NT, NB])
        k.xd = nc.dram_tensor("expert_rows", (NE * CAP, D), F32).ap()
        k.yd = nc.dram_tensor("expert_outputs", (NE * CAP, D), F32).ap()
        k.s_xd0 = sem("s_table_zeroed")
        attn = ExitStack()
        attention_tables(nc, k, attn)
        tokens(nc, k, ins)
        if stages > 1:
            attention(nc, k, ins)
        attn.close()
        if stages > 2:
            with ExitStack() as tied:
                k.wlh = tied.enter_context(nc.sbuf_tensor("tied_w_hi", [128, NH, 2, D], F32R))
                k.wll = tied.enter_context(nc.sbuf_tensor("tied_w_lo", [128, NH, 2, D], F32R))
                with ExitStack() as moe:
                    k.w1 = [moe.enter_context(nc.sbuf_tensor(f"w1_{q}", [128, 2, FF], F32)) for q in range(2)]
                    k.w2 = [moe.enter_context(nc.sbuf_tensor(f"w2_{q}", [128, FF // 128, D], F32)) for q in range(2)]
                    k.s_w1 = [sem(f"s_w1_{q}") for q in range(2)]
                    k.s_w2 = [sem(f"s_w2_{q}") for q in range(2)]
                    route(nc, k, ins)
                    experts(nc, k, ins)
                tied_attention(nc, k, ins)
        if stages > 4:
            mlp(nc, k, ins, out)
            return
        dump(nc, k, out, sem)


def constants(nc, k, sem):
    s_zero = sem("s_ident_zeroed")
    s_mask = sem("s_mask_step")
    with nc.Block() as block:
        @block.gpsimd
        def _(pool):
            pool.memset(k.mhalf[:], -0.5)
            pool.memset(k.mask[:], 1.0).then_inc(s_mask, 1)
            pool.wait_ge(s_mask, 1)
            pool.affine_select(out=k.mask[:], in_=k.mask[:], compare_op=ALU.is_ge, fill=0.0, base=0,
                               pattern=[[-HD, 8]], channel_multiplier=1).then_inc(s_mask, 1)
            pool.wait_ge(s_mask, 2)
            pool.affine_select(out=k.mask[:], in_=k.mask[:], compare_op=ALU.is_ge, fill=0.0, base=HD - 1,
                               pattern=[[HD, 8]], channel_multiplier=-1)
            pool.memset(k.ident[:], 0.0).then_inc(s_zero, 1)
            pool.wait_ge(s_zero, 1)
            pool.affine_select(out=k.ident[:], in_=k.ident[:], compare_op=ALU.not_equal, fill=1.0, base=0,
                               pattern=[[-1, 128]], channel_multiplier=1).then_inc(k.s_go, 1)


def dump(nc, k, out, sem):
    s_out = sem("s_out")
    with nc.Block() as block:
        @block.sync
        def _(sp):
            for a, b, c in ((0, NPT, 1), (NPT, NPT + 1, 0), (NPT + 1, NT, NPT + 1)):
                sp.dma_start(out[:, c:c + b - a, :].rearrange("b s d -> s b d"), k.H[a:b, :, :]).then_inc(s_out, 16)
            sp.wait_ge(k.s_xd0, k.xd0)
            sp.wait_ge(s_out, 48)


_INS = ["x", "txt", "L0_tok_ln1_g", "L0_tok_ln1_b", "L0_tok_W_proj", "L0_tok_b_proj", "L0_tok_ln2_g", "L0_tok_ln2_b",
        "L0_tok_cls_token", "L0_tok_pos_emb", "L0_attn_w_qkv", "L0_attn_w_proj", "L0_attn_b_proj", "L0_ffn_Wr",
        "L0_ffn_W1", "L0_ffn_W2", "L1_attn_weight", "L1_ffn_clip_x", "L1_ffn_clip_down", "L1_ffn_w_gate",
        "L1_ffn_w_up", "L1_ffn_w_down"]
STAGES = 9


def kernel(**inputs):
    import numpy as _np
    import concourse.bacc as _bacc
    from concourse import mybir as _mybir
    from concourse.bass_utils import run_bass_kernel_spmd as _run

    nc = _bacc.Bacc("TRN2", target_bir_lowering=False, num_devices=1)
    arrays, args = {}, {}
    for name in _INS:
        a = _np.ascontiguousarray(inputs[name])
        arrays[f"in_{name}"] = a
        args[name] = nc.dram_tensor(f"in_{name}", a.shape, _mybir.dt.from_np(a.dtype), kind="ExternalInput").ap()
    out = nc.dram_tensor("out_0", (NB, NT, D), F32, kind="ExternalOutput").ap()
    build(nc, args, out, STAGES)
    r = _run(nc, [arrays], core_ids=[0])
    return r.results[0]["out_0"]
```

```python
from contextlib import ExitStack

import concourse.bass as bass
from concourse import mybir

F32 = mybir.dt.float32
F32R = mybir.dt.float32r
BF16 = mybir.dt.bfloat16
I32 = mybir.dt.int32
U32 = mybir.dt.uint32
ALU = mybir.AluOpType
ACT = mybir.ActivationFunctionType
X = mybir.AxisListType.X
EPS = 1e-5

NB = 32
NPT = 36
NT = 69
D = 256
NH = 16
HD = D // NH
HP = 32
PAIRS = NB // 2
SIDE = 6
PIX = 16
ROWS = 3 * PIX
NE = 8
CAP = NB * NT // NE
FF = 1024
CH = NH // 4
HALF = 8 * NT
CW = 4 * NT
W2T = 2 * NT
Q4 = 4 * NT


class Shared:
    pass


def clear(nc, used):
    with nc.Block() as block:
        @block.sync
        def _(sp):
            for s in used:
                sp.sem_clear(s)


def tokens(nc, k, ins):
    with ExitStack() as ctx:
        sb = lambda n, s, d=F32: ctx.enter_context(nc.sbuf_tensor(n, s, d))
        used = []
        sem = lambda n: used.append(ctx.enter_context(nc.semaphore(n))) or used[-1]
        img = [sb("img_hi", [128, ROWS, 96]), sb("img_lo", [64, ROWS, 96])]
        size = [128, 64]
        xn = [sb("xn_hi", [128, SIDE, ROWS * PIX]), sb("xn_lo", [64, SIDE, ROWS * PIX])]
        wt = sb("tok_w", [128, 2, 3, D])
        g1 = sb("tok_g1", [128, 2, 3])
        b1 = sb("tok_b1", [128, 2, 3])
        bp = sb("tok_bproj", [128, 2])
        g2 = sb("tok_g2", [NPT, D])
        pos = sb("tok_pos", [NPT, D])
        b2 = sb("tok_b2", [NPT, D])
        cls = sb("tok_cls", [1, D])
        pos0 = sb("tok_pos0", [1, D])
        st = [sb(f"tok_st{g}", [size[g], SIDE, 2, 6]) for g in range(2)]
        mv = [sb(f"tok_mv{g}", [size[g], SIDE, 2]) for g in range(2)]
        rs = [sb(f"tok_rs{g}", [size[g], SIDE]) for g in range(2)]
        xt = [sb(f"tok_xt{i}", [128, 6, 384]) for i in range(2)]
        zt = sb("tok_zt", [128, 2, NB, NPT])
        st2 = sb("tok_st2", [NPT, NB, 6])
        mv2 = sb("tok_mv2", [NPT, NB, 2])
        rs2 = sb("tok_rs2", [NPT, NB])
        zn = [sb(f"tok_zn{i}", [NPT, 4, D]) for i in range(2)]
        s_img = [sem("s_img_hi"), sem("s_img_lo")]
        s_w = sem("s_tok_w")
        s_col = sem("s_tok_columns")
        s_row = sem("s_tok_rows")
        s_txt = sem("s_txt")
        s_crow = sem("s_cls_row")
        s_cls = sem("s_cls_stored")
        s_st = sem("s_tok_stats")
        s_mv = sem("s_tok_meanvar")
        s_ve = sem("s_tok_vareps")
        s_rs = sem("s_tok_rstd")
        s_xn = sem("s_tok_xn")
        s_tp = sem("s_tok_transposed")
        s_te = [sem("s_tok_xt_by_act"), sem("s_tok_xt_by_dve")]
        s_z = sem("s_tok_z")
        s_ze = sem("s_tok_z_evacuated")
        s_zt = sem("s_tok_z_tokens")
        s_st2 = sem("s_tok_stats2")
        s_mv2 = sem("s_tok_meanvar2")
        s_ve2 = sem("s_tok_vareps2")
        s_rs2 = sem("s_tok_rstd2")
        nmr = sb("tok_nmr", [NPT, NB])
        s_nmr, s_zn, s_zg, s_pos = (sem(f"s_tok_{n}") for n in ("nmr", "zn", "zn_g", "tokens"))
        zero = sb("zero", [92, 6 * D])
        s_zero = sem("s_zero")
        bk = k.bank
        block = ctx.enter_context(nc.Block())

        @block.sync
        def _(sp):
            for hh in range(SIDE):
                g, q = hh // 4, hh % 4
                src = ins["x"][:, :, PIX * hh:PIX * hh + PIX, :].rearrange("b c r w -> b c (r w)")
                dst = img[g][32 * q:32 * q + 32].rearrange("b (c r) w -> b c (r w)", c=3)
                sp.dma_start(dst, src).then_inc(s_img[g], 16)
            sp.dma_start(k.H[NPT + 1:NT, :, :], ins["txt"].rearrange("b s d -> s b d")).then_inc(s_txt, 16)
            attention_loads(sp, k, ins)
            sp.wait_ge(s_zero, 1)
            rows = k.xd.rearrange("(g p j) d -> g p (j d)", p=92, j=6)
            for g in range(NE * CAP // (92 * 6)):
                sp.dma_start(rows[g], zero[:]).then_inc(k.s_xd0, 16)
            k.xd0 = 16 * (NE * CAP // (92 * 6))
            sp.wait_ge(s_crow, 1)
            sp.dma_start(k.H[NPT:NPT + 1, :, :], cls[0:1, :].unsqueeze(1).broadcast_to([1, NB, D])).then_inc(s_cls, 16)
            sp.wait_ge(s_txt, 16)
            sp.wait_ge(s_cls, 16)

        @block.scalar
        def _(act):
            row = lambda n: ins[n].rearrange("(a d) -> a d", a=1)
            act.dma_start(wt[:], ins["L0_tok_W_proj"].rearrange("(h p c) e -> p h c e", h=2, c=3)).then_inc(s_w, 16)
            act.dma_start(g1[:], ins["L0_tok_ln1_g"].rearrange("(h p c) -> p h c", h=2, c=3)).then_inc(s_col, 16)
            act.dma_start(b1[:], ins["L0_tok_ln1_b"].rearrange("(h p c) -> p h c", h=2, c=3)).then_inc(s_col, 16)
            with nc.allow_non_contiguous_dma(reason="256 numbers, once"):
                act.dma_start(bp[:], ins["L0_tok_b_proj"].rearrange("(e p) -> p e", e=2)).then_inc(s_col, 16)
            act.dma_start(g2[:], row("L0_tok_ln2_g").broadcast_to([NPT, D])).then_inc(s_row, 16)
            act.dma_start(b2[:], row("L0_tok_ln2_b").broadcast_to([NPT, D])).then_inc(s_row, 16)
            act.dma_start(pos[:], ins["L0_tok_pos_emb"][0, 1:NPT + 1, :]).then_inc(s_row, 16)
            act.dma_start(pos0[:], ins["L0_tok_pos_emb"][0, 0:1, :]).then_inc(s_row, 16)
            act.dma_start(cls[:], ins["L0_tok_cls_token"][0, 0:1, :]).then_inc(s_row, 16)
            act.wait_ge(s_col, 48)
            for w in range(3):
                for c in range(0, 6, 2):
                    n = 6 * w + c
                    act.wait_ge(s_tp, n + 1)
                    if w >= 2:
                        act.wait_ge(s_z, 2 * (w - 1))
                    act.activation(xt[w % 2][:, c, :], bk[c % 2][:, 0:384], ACT.Identity,
                                   bias=b1[:, c % 2, c // 2:c // 2 + 1],
                                   scale=g1[:, c % 2, c // 2:c // 2 + 1]).then_inc(s_te[0], 1)
                for e in range(2):
                    act.wait_ge(s_z, 2 * w + e + 1)
                    src = bk[2 + e][:, 0:384].rearrange("p (w h b) -> p w h b", w=2, h=SIDE)
                    for v in range(2):
                        dst = zt[:, e].rearrange("p b (h w) -> p w h b", w=SIDE)[:, 2 * w + v]
                        i = act.activation(dst, src[:, v], ACT.Identity, bias=bp[:, e:e + 1])
                    i.then_inc(s_ze, 1)
            for q in range(NB // 4):
                act.wait_ge(s_nmr, q + 1)
                if q >= 2:
                    act.wait_ge(s_pos, q - 1)
                for j in range(4):
                    b = 4 * q + j
                    i = act.activation(zn[q % 2][:, j, :], bk[2 * (q % 4) + j // 2][0:NPT, D * (j % 2):D * (j % 2) + D],
                                       ACT.Identity, bias=nmr[:, b:b + 1], scale=rs2[:, b:b + 1])
                i.then_inc(s_zn, 1)

        @block.gpsimd
        def _(pool):
            attention_zeros(pool, k)
            pool.memset(zero[:], 0.0).then_inc(s_zero, 1)
            for g in range(2):
                pool.wait_ge(s_mv, g + 1)
                pool.tensor_scalar(rs[g][:], mv[g][:, :, 1], EPS, None, ALU.add).then_inc(s_ve, 1)
                pool.wait_ge(s_ve, g + 1)
                pool.tensor_tensor(rs[g][:], rs[g][:], k.mhalf[0:size[g], 0:SIDE], ALU.pow).then_inc(s_rs, 1)

            def positions(q):
                pool.wait_ge(s_zg, q + 1)
                pool.tensor_tensor(k.H[0:NPT, 4 * q:4 * q + 4, :], zn[q % 2][:],
                                   pos[:].unsqueeze(1).broadcast_to([NPT, 4, D]), ALU.add).then_inc(s_pos, 1)

            for q in range(NB // 4):
                pool.wait_ge(s_mv2, q + 1)
                v = rs2[:, 4 * q:4 * q + 4]
                pool.tensor_scalar(v, mv2[:, 4 * q:4 * q + 4, 1], EPS, None, ALU.add).then_inc(s_ve2, 1)
                pool.wait_ge(s_ve2, q + 1)
                pool.tensor_tensor(v, v, k.mhalf[0:NPT, 0:4], ALU.pow).then_inc(s_rs2, 1)
                if q >= 2:
                    positions(q - 2)
            positions(NB // 4 - 2)
            positions(NB // 4 - 1)

        @block.vector
        def _(dve):
            for g in range(2):
                dve.wait_ge(s_img[g], 64 if g == 0 else 32)
                for w in range(SIDE):
                    for h in range(2):
                        i = dve.bn_stats(st[g][:, w, h, :], img[g][:, 24 * h:24 * h + 24, PIX * w:PIX * w + PIX])
                i.then_inc(s_st, 1)
                dve.wait_ge(s_st, g + 1)
                for w in range(SIDE):
                    i = dve.bn_aggr(mv[g][:, w, :], st[g][:, w].rearrange("p h s -> p (h s)"))
                i.then_inc(s_mv, 1)
            dve.wait_ge(s_row, 80)
            dve.tensor_tensor(cls[:], cls[:], pos0[:], ALU.add).then_inc(s_crow, 1)
            dve.tensor_tensor(pos[:], pos[:], b2[:], ALU.add).then_inc(s_crow, 1)
            dve.wait_ge(s_rs, 2)
            for w in range(SIDE):
                for g in range(2):
                    v = img[g][:, :, PIX * w:PIX * w + PIX]
                    o = xn[g][:, w, :].rearrange("p (r x) -> p r x", x=PIX)
                    i = dve.tensor_scalar(o, v, mv[g][:, w, 0:1], rs[g][:, w:w + 1], ALU.subtract, ALU.mult)
                i.then_inc(s_xn, 1)
            dve.wait_ge(s_col, 48)
            for w in range(3):
                for c in range(1, 6, 2):
                    dve.wait_ge(s_tp, 6 * w + c + 1)
                    if w >= 2:
                        dve.wait_ge(s_z, 2 * (w - 1))
                    dve.tensor_scalar(xt[w % 2][:, c, :], bk[c % 2][:, 0:384],
                                      g1[:, c % 2, c // 2:c // 2 + 1], b1[:, c % 2, c // 2:c // 2 + 1],
                                      ALU.mult, ALU.add).then_inc(s_te[1], 1)
            def stats(q):
                dve.wait_ge(s_zt, q + 1)
                for j in range(4):
                    i = dve.bn_stats(st2[:, 4 * q + j, :],
                                     bk[2 * (q % 4) + j // 2][0:NPT, D * (j % 2):D * (j % 2) + D])
                i.then_inc(s_st2, 1)
                dve.wait_ge(s_st2, q + 1)
                for j in range(4):
                    i = dve.bn_aggr(mv2[:, 4 * q + j, :], st2[:, 4 * q + j, :])
                i.then_inc(s_mv2, 1)

            def gain(q):
                dve.wait_ge(s_zn, q + 1)
                z = zn[q % 2][:]
                dve.tensor_tensor(z, z, g2[:].unsqueeze(1).broadcast_to([NPT, 4, D]), ALU.mult).then_inc(s_zg, 1)

            stats(0)
            for q in range(NB // 4):
                if q + 1 < NB // 4:
                    stats(q + 1)
                dve.wait_ge(s_rs2, q + 1)
                v = slice(4 * q, 4 * q + 4)
                dve.scalar_tensor_tensor(nmr[:, v], mv2[:, v, 0], -1.0, rs2[:, v], ALU.mult, ALU.mult).then_inc(s_nmr, 1)
                if q >= 1:
                    gain(q - 1)
            gain(NB // 4 - 1)

        @block.tensor
        def _(pe):
            pe.wait_ge(s_w, 16)
            for w in range(3):
                pe.wait_ge(s_xn, 2 * w + 2)
                for c in range(6):
                    n = 6 * w + c
                    if n >= 2:
                        pe.wait_ge(s_te[c % 2], (n - 2) // 2 + 1)
                    for v in range(2):
                        for g in range(2):
                            src = xn[g][:, 2 * w + v, 128 * c:128 * c + 128]
                            i = pe.transpose(bk[c % 2][:, 192 * v + 128 * g:192 * v + 128 * g + size[g]], src,
                                             k.ident[0:size[g], 0:size[g]])
                    i.then_inc(s_tp, 1)
                pe.wait_ge(s_te[0], 3 * w + 3)
                pe.wait_ge(s_te[1], 3 * w + 3)
                for e in range(2):
                    if w >= 1:
                        pe.wait_ge(s_ze, 2 * (w - 1) + e + 1)
                    for c in range(6):
                        i = pe.matmul(bk[2 + e][:, 0:384], wt[:, c % 2, c // 2, 128 * e:128 * e + 128],
                                      xt[w % 2][:, c, :], start=(c == 0), stop=(c == 5))
                    i.then_inc(s_z, 1)
            pe.wait_ge(s_ze, 6)
            for q in range(NB // 4):
                if q >= 4:
                    pe.wait_ge(s_zn, q - 3)
                for j in range(4):
                    for e in range(2):
                        o = D * (j % 2) + 128 * e
                        i = pe.transpose(bk[2 * (q % 4) + j // 2][0:NPT, o:o + 128], zt[:, e, 4 * q + j, :],
                                         k.ident[:])
                i.then_inc(s_zt, 1)

    clear(nc, used)



def attention_tables(nc, k, ctx):
    sb = lambda n, s, d=F32: ctx.enter_context(nc.sbuf_tensor(n, s, d))
    k.wqk = sb("at_wqk", [128, 2, 2, D])
    k.wv = sb("at_wv", [128, 2, D])
    k.wo = sb("at_wo", [128, CH, D])
    k.bo = sb("at_bo", [NT, 2, D])
    k.vp = [sb(f"at_vp{i}", [NT, 2, NH, HP]) for i in range(2)]
    k.s_at_w = k.sem("s_at_w")
    k.s_at_z = k.sem("s_at_pads_zeroed")
    k.AT_LOADS = 2 * 3 + NH + 2


def attention_zeros(pool, k):
    pool.memset(k.wo[:], 0.0).then_inc(k.s_at_z, 1)
    for q in range(2):
        pool.memset(k.vp[q][:], 0.0).then_inc(k.s_at_z, 1)


def attention_loads(sp, k, ins):
    for c in range(2):
        for t in range(2):
            sp.dma_start(k.wqk[:, c, t, :], ins["L0_attn_w_qkv"][128 * c:128 * c + 128, D * t:D * t + D]
                         ).then_inc(k.s_at_w, 16)
        sp.dma_start(k.wv[:, c, :], ins["L0_attn_w_qkv"][128 * c:128 * c + 128, 2 * D:3 * D]).then_inc(k.s_at_w, 16)
    for j in range(2):
        sp.dma_start(k.bo[:, j, :], ins["L0_attn_b_proj"].rearrange("(a d) -> a d", a=1)
                     .broadcast_to([NT, D])).then_inc(k.s_at_w, 16)
    sp.wait_ge(k.s_at_z, 1)
    for r in range(4):
        for c in range(CH):
            h = 4 * c + r
            sp.dma_start(k.wo[HP * r:HP * r + HD, c, :],
                         ins["L0_attn_w_proj"][HD * h:HD * h + HD, :]).then_inc(k.s_at_w, 16)


def attention(nc, k, ins):
    with ExitStack() as ctx:
        sb = lambda n, s, d=F32: ctx.enter_context(nc.sbuf_tensor(n, s, d))
        used = []
        sem = lambda n: used.append(ctx.enter_context(nc.semaphore(n))) or used[-1]
        two = lambda n, s, d=F32: [sb(f"{n}{i}", s, d) for i in range(2)]
        four = lambda n, s, d=F32: [sb(f"{n}{i}", s, d) for i in range(4)]
        H = k.H
        st = two("at_st", [NT, 2, 6])
        mv = two("at_mv", [NT, 2, 2])
        rs = two("at_rs", [NT, 2])
        hn = two("at_hn", [NT, 2, D])
        hT = two("at_hT", [128, 2, W2T])
        qT = two("at_qT", [128, 2, W2T])
        kT = two("at_kT", [128, 2, W2T])
        kd = two("at_kd", [128, 2, 2, HALF])
        eb = four("at_e", [NT, HALF])
        mx = four("at_mx", [NT, 8])
        sm = four("at_sum", [NT, 8])
        rc = four("at_rc", [NT, 8])
        ets = two("at_et", [NT, HALF])
        oT = two("at_oT", [128, CH, W2T])
        pT = two("at_pT", [128, 2, W2T])
        s_st, s_mv, s_ve, s_rs, s_hn = (sem(f"s_at_{n}") for n in ("stats", "meanvar", "vareps", "rstd", "hn"))
        s_full = [sem(f"s_at_bank_full{i}") for i in range(2)]
        s_drained = [sem(f"s_at_bank_drained{i}") for i in range(2)]
        s_kd = [sem(f"s_at_kd{j}") for j in range(2)]
        s_S, s_mx, s_sub, s_exp, s_sum, s_rc, s_nrm = (
            sem(f"s_at_{n}") for n in ("scores", "max", "sub", "exp", "sum", "recip", "norm"))
        s_T, s_te, s_PV, s_xa, s_xd, s_hb = (
            sem(f"s_at_{n}") for n in ("turned", "turned_sb", "pv", "out_by_act", "out_by_dve", "bias"))
        sc = k.ps[:, 0:2, :]
        tb = k.ps[:, 2:4, :]
        vb = k.ps[:, 4:6, :]
        mb = [k.bank[6], k.bank[7]]
        LAST = PAIRS - 1

        HT, Q, K, V, PROJ, BACK = range(6)
        NTH = {HT: 0, K: 1, PROJ: 2, Q: 0, V: 1, BACK: 2}

        def use(i, q, what):
            b = what % 2
            if isinstance(i, int) and i == 0 and q == 0:
                return b, 2 + NTH[what]
            if isinstance(i, int) and 2 * i + q == LAST:
                return b, 3 * LAST + 1
            if isinstance(i, int) and 2 * i + q == PAIRS:
                return b, 3 * LAST + 2
            return b, i * 6 + (3 * q + 1 + NTH[what])

        def use0(what):
            return what % 2, what // 2

        def unit(i, q, u):
            return i * 8 + (4 * q + u)

        def after(i, q):
            return (i, 1) if q == 0 else (i + 1, 0)

        def later(i, q, u, d):
            if u + d < 4:
                return i, q, u + d
            if isinstance(i, int) and 2 * i + q == LAST:
                return None
            return *after(i, q), u + d - 4

        def before(i, q):
            return (i, 0) if q == 1 else (i - 1, 1)

        def drained(eng, u):
            eng.wait_ge(s_drained[u[0]], u[1] + 1)

        def filled(eng, u):
            eng.wait_ge(s_full[u[0]], u[1] + 1)
            return mb[u[0]]

        def all_pairs(eng, pair):
            pair(0, 0, True, False, True)
            pair(0, 1, True, True, True)
            with eng.Fori(1, PAIRS // 2 - 1) as i:
                pair(i, 0, True, True, True)
                pair(i, 1, True, True, True)
            pair(LAST // 2, 0, True, True, False)
            pair(LAST // 2, 1, False, True, False)

        block = ctx.enter_context(nc.Block())

        @block.tensor
        def _(pe):
            def fill(u):
                pe.wait_ge(s_drained[u[0]], u[1])
                return mb[u[0]]

            def front(i, q, what, u):
                if what == HT:
                    pe.wait_ge(s_hn, i * 2 + (q + 1))
                    b = fill(u)
                    for j in range(2):
                        for c in range(2):
                            o = W2T * c + NT * j
                            x = pe.transpose(b[:, o:o + NT], hn[q][:, j, 128 * c:128 * c + 128],
                                             k.ident[0:NT, 0:NT])
                elif what == V:
                    b = fill(u)
                    for j in range(2):
                        for c in range(2):
                            x = pe.matmul(b[0:NT, D * j:D * j + D], hT[q][:, c, NT * j:NT * j + NT], k.wv[:, c, :],
                                          start=(c == 0), stop=(c == 1))
                else:
                    b = fill(u)
                    for m in range(2):
                        for c in range(2):
                            x = pe.matmul(b[:, W2T * m:W2T * m + W2T],
                                          k.wqk[:, c, what - Q, 128 * m:128 * m + 128], hT[q][:, c, :],
                                          start=(c == 0), stop=(c == 1))
                x.then_inc(s_full[u[0]], 1)

            def scores(i, q, u):
                j, h = u // 2, u % 2
                pe.wait_ge(s_kd[j], i * 4 + (2 * q + h + 1))
                n = unit(i, q, u)
                if not (isinstance(n, int) and n == 0):
                    pe.wait_ge(s_sub, n)
                for c in range(2):
                    x = pe.matmul(sc[0:NT, c, 0:CW], qT[q][:, h, NT * j:NT * j + NT],
                                  kd[q][:, j, h, CW * c:CW * c + CW], start=True, stop=True)
                x.then_inc(s_S, 1)

            def turn(i, q, u):
                n = unit(i, q, u)
                pe.wait_ge(s_nrm, n + 1)
                if not (isinstance(n, int) and n == 0):
                    pe.wait_ge(s_te, n)
                for h in range(8):
                    x = pe.transpose(tb[0:NT, h // 4, NT * (h % 4):NT * (h % 4) + NT],
                                     eb[u][:, NT * h:NT * h + NT], k.ident[0:NT, 0:NT])
                x.then_inc(s_T, 1)

            def weigh(i, q, u):
                n = unit(i, q, u)
                j, h = u // 2, u % 2
                pe.wait_ge(s_te, n + 1)
                if not (isinstance(n, int) and n == 0):
                    pe.wait_ge(s_xa, n)
                    pe.wait_ge(s_xd, n)
                for c in range(2):
                    x = pe.matmul(vb[:, c, 0:CW],
                                  k.vp[q][:, j, 8 * h + 4 * c:8 * h + 4 * c + 4, :].rearrange("p h e -> p (h e)"),
                                  ets[u % 2][:, CW * c:CW * c + CW], start=True, stop=True)
                x.then_inc(s_PV, 1)

            def project(i, q, u):
                n = unit(i, q, 4)
                pe.wait_ge(s_xa, n)
                pe.wait_ge(s_xd, n)
                b = fill(u)
                for e in range(2):
                    for c in range(CH):
                        x = pe.matmul(b[:, W2T * e:W2T * e + W2T], k.wo[:, c, 128 * e:128 * e + 128], oT[q][:, c, :],
                                      start=(c == 0), stop=(c == CH - 1))
                x.then_inc(s_full[u[0]], 1)

            def back(q, up, u):
                drained(pe, up)
                b = fill(u)
                for j in range(2):
                    for e in range(2):
                        o = D * j + 128 * e
                        x = pe.transpose(b[0:NT, o:o + 128], pT[q][:, e, NT * j:NT * j + NT], k.ident[:])
                x.then_inc(s_full[u[0]], 1)

            def pair(i, q, nxt, prev, ln):
                ni, nq = after(i, q)
                bi, bq = before(i, q)
                for u in range(4):
                    turn(i, q, u)
                    if nxt and u == 0:
                        front(ni, nq, HT, use(i, q, HT))
                    n2 = later(i, q, u, 2)
                    if nxt and u == 2:
                        drained(pe, use(i, q, Q))
                    if n2:
                        scores(*n2)
                    if nxt and u == 1:
                        front(ni, nq, Q, use(i, q, Q))
                    if prev and u == 2:
                        project(bi, bq, use(i, q, PROJ))
                    if prev and u == 3:
                        back(bq, use(i, q, PROJ), use(i, q, BACK))
                    if u == 0:
                        drained(pe, use0(V) if isinstance(i, int) and (i, q) == (0, 0) else use(*before(i, q), V))
                    weigh(i, q, u)
                    if nxt and u == 0:
                        drained(pe, use(i, q, HT))
                        front(ni, nq, K, use(i, q, K))
                    if nxt and u == 1:
                        front(ni, nq, V, use(i, q, V))

            pe.wait_ge(k.s_at_w, 16 * k.AT_LOADS)
            pe.wait_ge(k.s_at_z, 3)
            front(0, 0, HT, use0(HT))
            drained(pe, use0(HT))
            for w in (Q, K, V):
                front(0, 0, w, use0(w))
            scores(0, 0, 0)
            scores(0, 0, 1)
            all_pairs(pe, pair)
            end = (PAIRS // 2, 0)
            project(LAST // 2, 1, use(*end, PROJ))
            back(1, use(*end, PROJ), use(*end, BACK))

        @block.scalar
        def _(act):
            def copy(dst, src):
                return act.activation(dst, src, ACT.Copy)

            def to_sb(dst, u):
                b = filled(act, u)
                copy(dst[:].rearrange("p c t -> p (c t)"), b[:, 0:2 * W2T]).then_inc(s_drained[u[0]], 1)

            def exps(i, q, u):
                act.wait_ge(s_sub, unit(i, q, u) + 1)
                act.activation(eb[u][:], eb[u][:], ACT.Exp, scale=HD ** -0.5).then_inc(s_exp, 1)

            def turned(i, q, u):
                act.wait_ge(s_T, unit(i, q, u) + 1)
                copy(ets[u % 2][:].rearrange("p (c t) -> p c t", c=2), tb[0:NT, :, 0:CW]).then_inc(s_te, 1)

            def out_heads(i, q, u):
                j, h = u // 2, u % 2
                act.wait_ge(s_PV, unit(i, q, u) + 1)
                for r in (0, 1):
                    x = copy(oT[q][HP * r:HP * r + HP, 2 * h:2 * h + 2, NT * j:NT * j + NT],
                             vb[HP * r:HP * r + HP, :, NT * r:NT * r + NT])
                x.then_inc(s_xa, 1)

            def pair(i, q, nxt, prev, ln):
                ni, nq = after(i, q)
                bi, bq = before(i, q)
                for u in range(4):
                    turned(i, q, u)
                    if nxt and u == 0:
                        to_sb(hT[nq], use(i, q, HT))
                    if nxt and u == 1:
                        to_sb(qT[nq], use(i, q, Q))
                    n2 = later(i, q, u, 2)
                    if n2:
                        exps(*n2)
                    if prev and u == 2:
                        to_sb(pT[bq], use(i, q, PROJ))
                    out_heads(i, q, u)
                    if nxt and u == 0:
                        to_sb(kT[nq], use(i, q, K))

            to_sb(hT[0], use0(HT))
            to_sb(qT[0], use0(Q))
            to_sb(kT[0], use0(K))
            exps(0, 0, 0)
            exps(0, 0, 1)
            all_pairs(act, pair)
            to_sb(pT[1], use(PAIRS // 2, 0, PROJ))

        @block.vector
        def _(dve):
            def ln_stats(i, q):
                for j in range(2):
                    x = dve.bn_stats(st[q][:, j, :], k.sample(i * 4 + (2 * q + j)))
                x.then_inc(s_st, 1)
                dve.wait_ge(s_st, i * 2 + (q + 1))
                dve.sem_inc(k.s_hold, 1)
                for j in range(2):
                    x = dve.bn_aggr(mv[q][:, j, :], st[q][:, j, :])
                x.then_inc(s_mv, 1)
                dve.wait_ge(s_mv, i * 2 + (q + 1))
                dve.tensor_scalar(rs[q][:], mv[q][:, :, 1], EPS, None, ALU.add).then_inc(s_ve, 1)

            def ln_apply(i, q):
                dve.wait_ge(s_rs, i * 2 + (q + 1))
                for j in range(2):
                    x = dve.tensor_scalar(hn[q][:, j, :], k.sample(i * 4 + (2 * q + j)), mv[q][:, j, 0:1],
                                          rs[q][:, j:j + 1], ALU.subtract, ALU.mult)
                x.then_inc(s_hn, 1)

            def less_max(i, q, u):
                n = unit(i, q, u)
                dve.wait_ge(s_S, n + 1)
                s = sc[0:NT, :, 0:CW].rearrange("p c (h t) -> p c h t", h=4)
                m = mx[u][:].rearrange("p (c h) -> p c h", c=2)
                dve.tensor_reduce(m, s, X, ALU.max).then_inc(s_mx, 1)
                dve.wait_ge(s_mx, n + 1)
                e = eb[u][:].rearrange("p (c h t) -> p c h t", c=2, h=4)
                dve.tensor_tensor(e, s, m.unsqueeze(3).broadcast_to([NT, 2, 4, NT]), ALU.subtract).then_inc(s_sub, 1)

            def sums(i, q, u):
                n = unit(i, q, u)
                dve.wait_ge(s_exp, n + 1)
                dve.tensor_reduce(sm[u][:], eb[u][:].rearrange("p (h t) -> p h t", h=8), X,
                                  ALU.add).then_inc(s_sum, 1)
                dve.wait_ge(s_sum, n + 1)
                dve.reciprocal(rc[u][:], sm[u][:]).then_inc(s_rc, 1)

            def out_heads(i, q, u):
                j, h = u // 2, u % 2
                dve.wait_ge(s_PV, unit(i, q, u) + 1)
                for r in (2, 3):
                    x = dve.tensor_copy(oT[q][HP * r:HP * r + HP, 2 * h:2 * h + 2, NT * j:NT * j + NT],
                                        vb[HP * r:HP * r + HP, :, NT * r:NT * r + NT])
                x.then_inc(s_xd, 1)

            def v_pad(q, u):
                b = filled(dve, u)
                dve.tensor_copy(k.vp[q][:, :, :, 0:HD].rearrange("p j h e -> p (j h) e"),
                                b[0:NT, :].rearrange("p (g e) -> p g e", e=HD)).then_inc(s_drained[u[0]], 1)

            def add_proj(i, q, u):
                b = filled(dve, u)
                h = k.samples(i * 4 + 2 * q, 2)
                dve.tensor_tensor(h, h, b[0:NT, :], ALU.add).then_inc(s_drained[u[0]], 1)

            def pair(i, q, nxt, prev, ln):
                ni, nq = after(i, q)
                bi, bq = before(i, q)
                for u in range(4):
                    n1, n2 = later(i, q, u, 1), later(i, q, u, 2)
                    if n1:
                        sums(*n1)
                    if n2:
                        less_max(*n2)
                    out_heads(i, q, u)
                    if prev and u == 3:
                        add_proj(bi, bq, use(i, q, BACK))
                    if nxt and u == 1:
                        v_pad(nq, use(i, q, V))
                    if ln and u == 0:
                        ln_stats(i + 1, q)
                    if ln and u == 2:
                        ln_apply(i + 1, q)

            for q in range(2):
                ln_stats(0, q)
                ln_apply(0, q)
            v_pad(0, use0(V))
            less_max(0, 0, 0)
            less_max(0, 0, 1)
            sums(0, 0, 0)
            all_pairs(dve, pair)
            add_proj(LAST // 2, 1, use(PAIRS // 2, 0, BACK))

        @block.gpsimd
        def _(pool):
            def ln_rstd(i, q):
                pool.wait_ge(s_ve, i * 2 + (q + 1))
                pool.tensor_tensor(rs[q][:], rs[q][:], k.mhalf[0:NT, 0:2], ALU.pow).then_inc(s_rs, 1)

            def norm(i, q, u):
                pool.wait_ge(s_rc, unit(i, q, u) + 1)
                e = eb[u][:].rearrange("p (h t) -> p h t", h=8)
                pool.tensor_tensor(e, e, rc[u][:].unsqueeze(2).broadcast_to([NT, 8, NT]),
                                   ALU.mult).then_inc(s_nrm, 1)

            def k_diag(i, q, j, m, u):
                drained(pool, u)
                pool.tensor_tensor(kd[q][:, j, m, :].rearrange("p (h t) -> p h t", h=8),
                                   kT[q][:, m, NT * j:NT * j + NT].unsqueeze(1).broadcast_to([128, 8, NT]),
                                   k.mask[:].unsqueeze(2).broadcast_to([128, 8, NT]), ALU.mult).then_inc(s_kd[j], 1)

            def bias(i, q, u):
                drained(pool, u)
                h = k.samples(i * 4 + 2 * q, 2)
                pool.tensor_tensor(h, h, k.bo[:].rearrange("p j d -> p (j d)"), ALU.add).then_inc(s_hb, 1)

            def pair(i, q, nxt, prev, ln):
                ni, nq = after(i, q)
                for u in range(4):
                    n1 = later(i, q, u, 1)
                    if nxt and u == 1:
                        k_diag(ni, nq, 0, 0, use(i, q, K))
                    if n1:
                        norm(*n1)
                    if nxt and u == 2:
                        k_diag(ni, nq, 0, 1, use(i, q, K))
                        k_diag(ni, nq, 1, 0, use(i, q, K))
                    if nxt and u == 3:
                        k_diag(ni, nq, 1, 1, use(i, q, K))
                    if ln and u == 1:
                        ln_rstd(i + 1, q)
                    if prev and u == 3:
                        bias(*before(i, q), use(i, q, BACK))

            for q in range(2):
                ln_rstd(0, q)
            for j in range(2):
                for m in range(2):
                    k_diag(0, 0, j, m, use0(K))
            norm(0, 0, 0)
            all_pairs(pool, pair)
            bias(LAST // 2, 1, use(PAIRS // 2, 0, BACK))

    clear(nc, used)


def route(nc, k, ins):
    G = 4
    with ExitStack() as ctx:
        sb = lambda n, s, d=F32: ctx.enter_context(nc.sbuf_tensor(n, s, d))
        used = []
        sem = lambda n: used.append(ctx.enter_context(nc.semaphore(n))) or used[-1]
        two = lambda n, s, d=F32: [sb(f"{n}{i}", s, d) for i in range(2)]
        wr = sb("rt_w", [128, 2, NE])
        tri = sb("rt_before", [NT, NT])
        ones = sb("rt_ones", [NT, NT])
        lane = sb("rt_lane", [NT, G, NE])
        lane_i = sb("rt_lane_int", [NT, G, NE], I32)
        st = two("rt_st", [NT, G, 6])
        mv = two("rt_mv", [NT, G, 2])
        rs = two("rt_rs", [NT, G])
        xm = two("rt_x", [NT, G, D])
        xT = two("rt_xT", [128, 2, G * NT])
        lg = sb("rt_logits", [NT, G, NE])
        m8 = sb("rt_max", [NT, G, NE])
        i8 = sb("rt_maxi", [NT, G, NE], U32)
        ix = sb("rt_expert", [NT, G])
        dl = two("rt_less", [NT, G, NE])
        oh = two("rt_onehot", [NT, G, NE])
        seen = two("rt_seen", [NT, G, NE])
        own = sb("rt_own", [NT, G, NE])
        rk = sb("rt_rank", [NT, G])
        kp = sb("rt_keep", [NT, G])
        ad = sb("rt_addr", [NT, G])
        sl = two("rt_slot", [NT, G], U32)
        se = sb("rt_sum", [NT, G])
        s_w, s_c, s_st, s_ve, s_rs, s_x = (sem(f"s_rt_{n}") for n in ("w", "const", "stats", "vareps", "rstd", "x"))
        s_T, s_xT, s_lg, s_ch, s_dl, s_e = (
            sem(f"s_rt_{n}") for n in ("turned", "xT", "logits", "step", "less", "exp"))
        s_oh, s_rk, s_sl = (sem(f"s_rt_{n}") for n in ("onehot", "rank", "slot"))
        s_sc = [sem(f"s_rt_scattered{i}") for i in range(2)]
        bk = k.bank
        GN = NB // G
        STEPS = 18
        weights = MlpWeights(nc, k, ins, ctx, sem)
        block = ctx.enter_context(nc.Block())

        @block.sync
        def _(sp):
            sp.dma_start(wr[:], ins["L0_ffn_Wr"].rearrange("(c p) e -> p c e", p=128)).then_inc(s_w, 16)
            weights.load(sp)
            for e in range(2):
                expert_weights(sp, k, ins, e, e)
            for q in range(2):
                sp.wait_ge(s_sc[q], 16 * G * GN // 2)

        @block.tensor
        def _(pe):
            def group(i, q):
                n = i * 2 + q
                pe.wait_ge(s_x, n + 1)
                if not (isinstance(i, int) and i == 0 and q == 0):
                    pe.wait_ge(s_xT, n)
                for c in range(2):
                    for j in range(G):
                        x = pe.transpose(bk[c][:, NT * j:NT * j + NT], xm[q][:, j, 128 * c:128 * c + 128],
                                         k.ident[0:NT, 0:NT])
                x.then_inc(s_T, 1)
                pe.wait_ge(s_xT, n + 1)
                for j in range(G):
                    for c in range(2):
                        x = pe.matmul(bk[2 + q][0:NT, NE * j:NE * j + NE], xT[q][:, c, NT * j:NT * j + NT],
                                      wr[:, c, :], start=(c == 0), stop=(c == 1))
                x.then_inc(s_lg, 1)
                pe.wait_ge(s_oh, n + 1)
                o = bk[4 + q][0:NT, 0:G * NE]
                pe.matmul(o, tri[:], oh[q][:].rearrange("p g e -> p (g e)"), start=True, stop=False)
                pe.matmul(o, ones[:], seen[q][:].rearrange("p g e -> p (g e)"), start=False,
                          stop=True).then_inc(s_rk, 1)

            pe.wait_ge(s_w, 16)
            for n in range(GN):
                group(n // 2, n % 2)
                if n == 4:
                    weights.turn(pe, 0)
                if n == 5:
                    weights.turn(pe, 1)
                if n == 6:
                    weights.turn_down(pe)

        @block.scalar
        def _(act):
            def group(i, q):
                n = i * 2 + q
                act.wait_ge(s_T, n + 1)
                act.activation(xT[q][:], k.ps[:, 0:2, 0:G * NT], ACT.Copy).then_inc(s_xT, 1)
                act.wait_ge(s_dl, n + 1)
                act.activation(dl[q][:], dl[q][:], ACT.Exp).then_inc(s_e, 1)

            weights.sigmoid(act)
            for n in range(GN):
                group(n // 2, n % 2)
                if n == 2:
                    weights.rounded(act, 0)
                    weights.rounded(act, 1)
                if n == 3:
                    weights.rounded(act, 2)
                    weights.whole(act)
                if n == 4:
                    weights.turned(act, 0)
                if n == 5:
                    weights.turned(act, 1)
                if n == 6:
                    weights.turned_down(act)

        @block.gpsimd
        def _(pool):
            def rstd(i, q):
                pool.wait_ge(s_ve, i * 2 + (q + 1))
                pool.tensor_tensor(rs[q][:], rs[q][:], k.mhalf[0:NT, 0:G], ALU.pow).then_inc(s_rs, 1)

            def scatter(i, q):
                pool.wait_ge(s_sl, i * 2 + (q + 1))
                pool.sem_inc(k.s_hold, 1)
                for j in range(G):
                    pool.indirect_dma_start(out=k.xd[:], out_offset=bass.IndirectOffsetOnAxis(sl[q][:, j:j + 1], 0),
                                            in_=xm[q][:, j, :], in_offset=None, bounds_check=NE * CAP - 1,
                                            oob_is_err=False).then_inc(s_sc[q], 16)

            weights.pads(pool)
            pool.memset(ones[:], 1.0)
            pool.memset(tri[:], 1.0).then_inc(s_c, 1)
            pool.iota(lane_i[:], pattern=[[0, G], [1, NE]], base=0, channel_multiplier=0).then_inc(s_c, 1)
            pool.wait_ge(s_c, 2)
            pool.tensor_copy(lane[:], lane_i[:])
            pool.affine_select(out=tri[:], in_=tri[:], compare_op=ALU.is_gt, fill=0.0, base=0,
                               pattern=[[1, NT]], channel_multiplier=-1).then_inc(s_c, 1)
            pool.wait_ge(s_c, 3)
            pool.affine_select(out=tri[:], in_=tri[:], compare_op=ALU.not_equal, fill=1.0, base=-NPT,
                               pattern=[[0, NT]], channel_multiplier=1).then_inc(s_c, 1)
            pool.wait_ge(s_c, 4)
            pool.memset(tri[:, NPT:NPT + 1], 0.0).then_inc(s_c, 1)
            rstd(0, 0)
            rstd(0, 1)
            pool.wait_ge(k.s_xd0, k.xd0)
            with pool.Fori(0, GN // 2 - 1) as i:
                scatter(i, 0)
                rstd(i + 1, 0)
                scatter(i, 1)
                rstd(i + 1, 1)
            scatter(GN // 2 - 1, 0)
            scatter(GN // 2 - 1, 1)

        @block.vector
        def _(dve):
            def ln_stats(i, q):
                for j in range(G):
                    x = dve.bn_stats(st[q][:, j, :], k.sample(i * 8 + (4 * q + j)))
                x.then_inc(s_st, 1)
                dve.wait_ge(s_st, i * 4 + (2 * q + 1))
                dve.sem_inc(k.s_hold, 1)
                for j in range(G):
                    x = dve.bn_aggr(mv[q][:, j, :], st[q][:, j, :])
                x.then_inc(s_st, 1)
                dve.wait_ge(s_st, i * 4 + (2 * q + 2))
                dve.tensor_scalar(rs[q][:], mv[q][:, :, 1], EPS, None, ALU.add).then_inc(s_ve, 1)

            def ln_apply(i, q):
                dve.wait_ge(s_rs, i * 2 + (q + 1))
                if not (isinstance(i, int) and i == 0):
                    dve.wait_ge(s_sc[q], i * (16 * G))
                for j in range(G):
                    x = dve.tensor_scalar(xm[q][:, j, :], k.sample(i * 8 + (4 * q + j)), mv[q][:, j, 0:1],
                                          rs[q][:, j:j + 1], ALU.subtract, ALU.mult)
                x.then_inc(s_x, 1)

            def route_group(i, q):
                n = [0]

                def step(x):
                    n[0] += 1
                    x.then_inc(s_ch, 1)
                    dve.wait_ge(s_ch, i * (2 * STEPS) + (q * STEPS + n[0]))

                b4 = lambda v: v.unsqueeze(2).broadcast_to([NT, G, NE])
                dve.wait_ge(s_lg, i * 2 + (q + 1))
                step(dve.tensor_copy(lg[:].rearrange("p g e -> p (g e)"), bk[2 + q][0:NT, 0:G * NE]))
                dve.sem_inc(k.s_hold, 1)
                for j in range(G):
                    x = dve.max(m8[:, j, :], lg[:, j, :])
                step(x)
                dve.sem_inc(k.s_hold, 1)
                for j in range(G):
                    x = dve.max_index(i8[:, j, :], m8[:, j, :], lg[:, j, :])
                step(x)
                dve.tensor_tensor(dl[q][:], lg[:], b4(m8[:, :, 0]), ALU.subtract).then_inc(s_dl, 1)
                step(dve.tensor_copy(ix[:], i8[:, :, 0]))
                step(dve.tensor_tensor(oh[q][:], lane[:], b4(ix[:]), ALU.is_equal))
                prev, poh = seen[1 - q], oh[1 - q]
                if isinstance(i, int) and i == 0 and q == 0:
                    step(dve.memset(seen[q][:, 0, :], 0.0))
                else:
                    step(dve.tensor_tensor(seen[q][:, 0, :], prev[:, G - 1, :], poh[:, G - 1, :], ALU.add))
                for j in range(1, G):
                    x = dve.tensor_tensor(seen[q][:, j, :], seen[q][:, j - 1, :], oh[q][:, j - 1, :], ALU.add)
                    if j < G - 1:
                        step(x)
                x.then_inc(s_oh, 1)
                dve.wait_ge(s_rk, i * 2 + (q + 1))
                step(dve.tensor_tensor(own[:].rearrange("p g e -> p (g e)"),
                                       oh[q][:].rearrange("p g e -> p (g e)"),
                                       bk[4 + q][0:NT, 0:G * NE], ALU.mult))
                step(dve.tensor_reduce(rk[:], own[:], X, ALU.add))
                step(dve.tensor_scalar(kp[:], rk[:], float(CAP), None, ALU.is_lt))
                step(dve.scalar_tensor_tensor(ad[:], ix[:], float(CAP), rk[:], ALU.mult, ALU.add))
                step(dve.tensor_scalar(ad[:], ad[:], float(NE * CAP), None, ALU.subtract))
                step(dve.tensor_tensor(ad[:], ad[:], kp[:], ALU.mult))
                if not (isinstance(i, int) and i == 0):
                    dve.wait_ge(s_sc[q], i * (16 * G))
                x = dve.tensor_scalar(sl[q][:], ad[:], float(NE * CAP), None, ALU.add)
                x.then_inc(s_sl, 1)
                dve.wait_ge(s_sl, i * 2 + (q + 1))
                step(dve.tensor_copy(k.slot[:, bass.ds(i * 8 + 4 * q, G)], sl[q][:]))
                dve.wait_ge(s_e, i * 2 + (q + 1))
                step(dve.tensor_reduce(se[:], dl[q][:], X, ALU.add))
                step(dve.reciprocal(se[:], se[:]))
                step(dve.tensor_tensor(k.gate[:, bass.ds(i * 8 + 4 * q, G)], se[:], kp[:], ALU.mult))
                assert n[0] == STEPS, n[0]

            def groups(i, nxt):
                route_group(i, 0)
                ln_apply(i, 1)
                if nxt:
                    ln_stats(i + 1, 0)
                route_group(i, 1)
                if nxt:
                    ln_apply(i + 1, 0)
                    ln_stats(i + 1, 1)

            ln_stats(0, 0)
            ln_stats(0, 1)
            ln_apply(0, 0)
            dve.wait_ge(s_c, 5)
            groups(0, True)
            weights.scales(dve)
            with dve.Fori(1, GN // 2 - 1) as i:
                groups(i, True)
            groups(GN // 2 - 1, False)

    clear(nc, used)


def expert_weights(sp, k, ins, e, q):
    pick = lambda n: ins[n][bass.ds(e, 1), :, :].rearrange("a r c -> (a r) c")
    sp.dma_start(k.w1[q][:], pick("L0_ffn_W1").rearrange("(c p) f -> p c f", p=128)).then_inc(k.s_w1[q], 16)
    sp.dma_start(k.w2[q][:], pick("L0_ffn_W2").rearrange("(f p) d -> p f d", p=128)).then_inc(k.s_w2[q], 16)


def experts(nc, k, ins):
    R, J = 92, 3
    NF = FF // 128
    with ExitStack() as ctx:
        sb = lambda n, s, d=F32: ctx.enter_context(nc.sbuf_tensor(n, s, d))
        sem = lambda n: ctx.enter_context(nc.semaphore(n))
        two = lambda n, s, d=F32: [sb(f"{n}{i}", s, d) for i in range(2)]
        xe = two("ex_x", [R, J, D])
        xT = two("ex_xT", [128, 2, CAP])
        hid = two("ex_h", [128, NF, CAP])
        yT = two("ex_yT", [128, 2, CAP])
        ye = two("ex_y", [R, J, D])
        wst = two("ex_tied_w", [128, 4, 2, D])
        s_win = [sem(f"s_ex_tied_w{i}") for i in range(2)]
        s_whi, s_wlo = sem("s_ex_tied_hi"), sem("s_ex_tied_lo")
        s_xe = [sem(f"s_ex_x{i}") for i in range(2)]
        s_T, s_xT, s_h, s_y, s_yT, s_B, s_ye = (
            sem(f"s_ex_{n}") for n in ("turned", "xT", "hidden", "y", "yT", "back", "y_sb"))
        s_hs = [sem("s_ex_h_by_act"), sem("s_ex_h_by_dve")]
        s_out = [sem(f"s_ex_out{i}") for i in range(2)]
        bk = k.bank
        LAST = NE // 2 - 1
        xd = k.xd.rearrange("(e j p) d -> e p j d", e=NE, j=J)
        yd = k.yd.rearrange("(e j p) d -> e p j d", e=NE, j=J)
        pick = lambda t, e: t[bass.ds(e, 1)].rearrange("a p j d -> (a p) j d")
        block = ctx.enter_context(nc.Block())

        @block.gpsimd
        def _(pool):
            tied_weights(nc, k, ins, pool, wst, s_win, s_whi, s_wlo)

        @block.sync
        def _(sp):
            def load(i, q):
                if not (isinstance(i, int) and i == 0):
                    sp.wait_ge(s_T, i * 2 + (q - 1))
                sp.dma_start(xe[q][:], pick(xd, i * 2 + q)).then_inc(s_xe[q], 16)

            def weights(i, q):
                sp.wait_ge(s_y, i * 2 + (q - 1))
                expert_weights(sp, k, ins, i * 2 + q, q)

            def store(i, q):
                sp.wait_ge(s_ye, i * 2 + (q + 1))
                sp.dma_start(pick(yd, i * 2 + q), ye[q][:]).then_inc(s_out[q], 16)

            load(0, 0)
            load(0, 1)
            with sp.Fori(1, NE // 2) as i:
                for q in range(2):
                    load(i, q)
                    weights(i, q)
                    store(i - 1, q)
            store(LAST, 0)
            store(LAST, 1)
            for q in range(2):
                sp.wait_ge(s_out[q], 16 * (NE // 2))

        @block.tensor
        def _(pe):
            def turn(i, q):
                n = i * 2 + q
                pe.wait_ge(s_xe[q], i * 16 + 16)
                if not (isinstance(i, int) and i == 0 and q == 0):
                    pe.wait_ge(s_xT, n)
                for c in range(2):
                    for j in range(J):
                        x = pe.transpose(bk[c][:, R * j:R * j + R], xe[q][:, j, 128 * c:128 * c + 128],
                                         k.ident[0:R, 0:R])
                x.then_inc(s_T, 1)

            def expert(i, q, nxt, prev=True):
                n = i * 2 + q
                pe.wait_ge(s_xT, n + 1)
                pe.wait_ge(k.s_w1[q], i * 16 + 16)
                for f in range(NF):
                    if not (isinstance(i, int) and i == 0 and q == 0 and f < 2):
                        pe.wait_ge(s_hs[f % 2], n * (NF // 2) + f // 2)
                    for c in range(2):
                        x = pe.matmul(bk[2 + f % 2][:, 0:CAP], k.w1[q][:, c, 128 * f:128 * f + 128],
                                      xT[q][:, c, :], start=(c == 0), stop=(c == 1))
                    x.then_inc(s_h, 1)
                    if prev and f == 1:
                        back(*((i, 0) if q == 1 else (i - 1, 1)))
                if nxt:
                    turn(*((i, 1) if q == 0 else (i + 1, 0)))
                pe.wait_ge(k.s_w2[q], i * 16 + 16)
                for e in range(2):
                    pe.wait_ge(s_hs[e], n * (NF // 2) + NF // 2)
                if not (isinstance(i, int) and i == 0 and q == 0):
                    pe.wait_ge(s_yT, n)
                for c in range(2):
                    for f in range(NF):
                        x = pe.matmul(bk[4 + c][:, 0:CAP], k.w2[q][:, f, 128 * c:128 * c + 128], hid[q][:, f, :],
                                      start=(f == 0), stop=(f == NF - 1))
                x.then_inc(s_y, 1)

            def back(i, q):
                n = i * 2 + q
                pe.wait_ge(s_yT, n + 1)
                if not (isinstance(i, int) and i == 0 and q == 0):
                    pe.wait_ge(s_ye, n)
                for j in range(J):
                    for c in range(2):
                        o = D * (j % 2) + 128 * c
                        x = pe.transpose(bk[6 + j // 2][0:R, o:o + 128], yT[q][:, c, R * j:R * j + R], k.ident[:])
                x.then_inc(s_B, 1)

            turn(0, 0)
            expert(0, 0, True, False)
            expert(0, 1, True)
            with pe.Fori(1, LAST) as i:
                expert(i, 0, True)
                expert(i, 1, True)
            expert(LAST, 0, True)
            expert(LAST, 1, False)
            back(LAST, 1)

        @block.scalar
        def _(act):
            def expert(i, q):
                n = i * 2 + q
                for f in range(0, NF, 2):
                    act.wait_ge(s_h, n * NF + f + 1)
                    act.activation(hid[q][:, f, :], bk[2][:, 0:CAP], ACT.Relu).then_inc(s_hs[0], 1)
                act.wait_ge(s_y, n + 1)
                act.activation(yT[q][:], k.ps[:, 4:6, 0:CAP], ACT.Copy).then_inc(s_yT, 1)

            with act.Fori(0, NE // 2) as i:
                expert(i, 0)
                expert(i, 1)

        @block.vector
        def _(dve):
            def rows(i, q):
                dve.wait_ge(s_T, i * 2 + (q + 1))
                dve.tensor_copy(xT[q][:], k.ps[:, 0:2, 0:CAP]).then_inc(s_xT, 1)

            def outputs(i, q):
                dve.wait_ge(s_B, i * 2 + (q + 1))
                if not (isinstance(i, int) and i == 0):
                    dve.wait_ge(s_out[q], i * 16)
                dve.tensor_copy(ye[q][:, 0:2, :].rearrange("p j d -> p (j d)"), bk[6][0:R, :])
                dve.tensor_copy(ye[q][:, 2, :], bk[7][0:R, 0:D]).then_inc(s_ye, 1)

            def expert(i, q, nxt, prev=True):
                n = i * 2 + q
                for f in range(1, NF, 2):
                    dve.wait_ge(s_h, n * NF + f + 1)
                    dve.tensor_scalar(hid[q][:, f, :], bk[3][:, 0:CAP], 0.0, None, ALU.max).then_inc(s_hs[1], 1)
                    if prev and f == 1:
                        outputs(*((i, 0) if q == 1 else (i - 1, 1)))
                if nxt:
                    rows(*((i, 1) if q == 0 else (i + 1, 0)))

            rows(0, 0)
            expert(0, 0, True, False)
            expert(0, 1, True)
            with dve.Fori(1, LAST) as i:
                expert(i, 0, True)
                expert(i, 1, True)
            expert(LAST, 0, True)
            expert(LAST, 1, False)
            outputs(LAST, 1)


def tied_weights(nc, k, ins, pool, wst, s_in, s_hi, s_lo):
    w = ins["L1_attn_weight"].rearrange("(h c p) e -> p h c e", c=2, p=128)

    def load(g):
        pool.dma_start(wst[g % 2][:], w[:, 4 * g:4 * g + 4]).then_inc(s_in[g % 2], 16)

    load(0)
    load(1)
    for g in range(4):
        flat = lambda t: t.rearrange("p h c e -> p (h c e)")
        hi, lo, src = flat(k.wlh[:, 4 * g:4 * g + 4]), flat(k.wll[:, 4 * g:4 * g + 4]), flat(wst[g % 2][:])
        pool.wait_ge(s_in[g % 2], 16 * (g // 2) + 16)
        pool.tensor_copy(hi, src).then_inc(s_hi, 1)
        pool.wait_ge(s_hi, g + 1)
        pool.tensor_tensor(lo, src, hi, ALU.subtract).then_inc(s_lo, 1)
        if g < 2:
            pool.wait_ge(s_lo, g + 1)
            load(g + 2)
    pool.wait_ge(s_lo, 4)


def tied_attention(nc, k, ins):
    with ExitStack() as ctx:
        sb = lambda n, s, d=F32: ctx.enter_context(nc.sbuf_tensor(n, s, d))
        used = []
        sem = lambda n: used.append(ctx.enter_context(nc.semaphore(n))) or used[-1]
        two = lambda n, s, d=F32: [sb(f"{n}{i}", s, d) for i in range(2)]
        four = lambda n, s, d=F32: [sb(f"{n}{i}", s, d) for i in range(4)]
        yg = [two(f"ta_row{p}_", [NT, D]) for p in range(2)]
        sl = two("ta_slot", [NT, 2], U32)
        st = sb("ta_st", [NT, 2, 6])
        mv = sb("ta_mv", [NT, 2, 2])
        rs = sb("ta_rs", [NT, 2])
        nm = sb("ta_nm", [NT, 2])
        xn = two("ta_x", [NT, 2, D])
        xh = sb("ta_xhi", [NT, 4, D], F32R)
        xl = sb("ta_xlo", [NT, 4, D], F32R)
        yT = sb("ta_yT", [128, 2, Q4])
        yd = four("ta_ydiag", [128, HALF])
        eb = four("ta_e", [NT, HALF])
        sm = four("ta_sum", [NT, 8])
        rc = four("ta_rc", [NT, 8])
        ah = two("ta_at_hi", [NT, HALF], F32R)
        al = two("ta_at_lo", [NT, HALF], F32R)
        oh = two("ta_o_hi", [128, 4, 2, Q4], F32R)
        ol = two("ta_o_lo", [128, 4, 2, Q4], F32R)
        wT = sb("ta_wT", [128, 2, Q4])
        s_z, s_sl, s_row, s_st, s_mv, s_ve, s_rs, s_xn = (
            sem(f"s_ta_{n}") for n in ("zeroed", "slot", "row_added", "stats", "mv", "vareps", "rstd", "x"))
        s_yg = [sem(f"s_ta_rows{p}") for p in range(2)]
        s_xh, s_xl, s_F, s_yT = (sem(f"s_ta_{n}") for n in ("xhi", "xlo", "front", "yT"))
        s_yd, s_S, s_exp, s_sum, s_rc, s_nrm, s_T, s_ah, s_al = (
            sem(f"s_ta_{n}") for n in ("ydiag", "scores", "exp", "sum", "recip", "norm", "turned", "at_hi", "at_lo"))
        s_av, s_oh, s_ol = (sem(f"s_ta_{n}") for n in ("av", "o_hi", "o_lo"))
        s_W0 = sem("s_ta_first_half_by_w")
        s_Wg = sem("s_ta_group_by_w")
        s_wT = [sem(f"s_ta_wT{e}") for e in range(2)]
        s_B, s_add = sem("s_ta_back"), sem("s_ta_added")
        st2 = sb("ta_st2", [NT, 2, 6])
        mv2 = sb("ta_mv2", [NT, 2, 2])
        rs2 = sb("ta_rs2", [NT, 2])
        nm2 = sb("ta_nm2", [NT, 2])
        s_nm, s_nm2 = sem("s_ta_nm"), sem("s_ta_next_nm")
        y2 = sb("ta_y2", [NT, 2, D])
        s_st2, s_mv2, s_ve2, s_rs2, s_y2, s_mx, s_z2 = (
            sem(f"s_ta_next_{n}") for n in ("stats", "mv", "vareps", "rstd", "y", "max", "zeroed"))
        sc = k.ps[:, 0:2, :]
        tb = k.ps[:, 2:4, :]
        vb = k.ps[:, 4:6, :]
        wb = [k.bank[6], k.bank[7]]
        QUADS = NB // 4
        LAST = QUADS - 1
        zero = lambda n: isinstance(n, int) and n == 0

        def later(Q, u, d):
            if u + d < 8:
                return Q, u + d
            if isinstance(Q, int) and Q == LAST:
                return None
            return Q + 1, u + d - 8

        def unit(Q, u):
            return Q * 8 + u

        def all_quads(eng, quad):
            quad(0, True, True)
            with eng.Fori(1, LAST) as Q:
                quad(Q, False, True)
            quad(LAST, False, False)

        block = ctx.enter_context(nc.Block())

        @block.tensor
        def _(pe):
            def front(Q, p):
                pe.wait_ge(s_xn, Q * 2 + (p + 1))
                for c in range(2):
                    for j in range(2):
                        o = W2T * c + NT * j
                        x = pe.transpose(vb[:, 1, o:o + NT], xn[p][:, j, 128 * c:128 * c + 128],
                                         k.ident[0:NT, 0:NT])
                x.then_inc(s_F, 1)

            def back(Q, p):
                for e in range(2):
                    pe.wait_ge(s_wT[e], Q + 1)
                for j in range(2):
                    for e in range(2):
                        o, t = D * j + 128 * e, NT * (2 * p + j)
                        x = pe.transpose(vb[0:NT, 0, o:o + 128], wT[:, e, t:t + NT], k.ident[:])
                x.then_inc(s_B, 1)

            def scores(Q, u):
                g, p = u // 2, u % 2
                n = unit(Q, u)
                pe.wait_ge(s_yd, n + 1)
                if not zero(n):
                    pe.wait_ge(s_exp, n)
                for j in range(2):
                    t = NT * (2 * p + j)
                    x = pe.matmul(sc[0:NT, j, 0:CW], yT[:, g // 2, t:t + NT],
                                  yd[u % 4][:, CW * j:CW * j + CW], start=True, stop=True)
                x.then_inc(s_S, 1)

            def turn(Q, u):
                n = unit(Q, u)
                pe.wait_ge(s_nrm, n + 1)
                if not zero(n):
                    pe.wait_ge(s_al, n)
                for h in range(8):
                    x = pe.transpose(tb[0:NT, h // 4, NT * (h % 4):NT * (h % 4) + NT],
                                     eb[u % 4][:, NT * h:NT * h + NT], k.ident[0:NT, 0:NT])
                x.then_inc(s_T, 1)

            def weigh(Q, u, c):
                n, p = unit(Q, u), u % 2
                if not (zero(n) and c == 0):
                    pe.wait_ge(s_ol, n * 2 + c)
                for j in range(2):
                    x_hi = xh[:, 2 * p + j, 128 * c:128 * c + 128]
                    x_lo = xl[:, 2 * p + j, 128 * c:128 * c + 128]
                    a_hi, a_lo = ah[u % 2][:, CW * j:CW * j + CW], al[u % 2][:, CW * j:CW * j + CW]
                    o = vb[:, j, 0:CW]
                    pe.matmul(o, x_hi, a_hi, start=True, stop=False)
                    pe.matmul(o, x_hi, a_lo, start=False, stop=False)
                    x = pe.matmul(o, x_lo, a_hi, start=False, stop=True)
                x.then_inc(s_av, 1)

            def times_w(Q, u, part):
                e, g = u % 2, (u // 2 - 1) % 4
                if e == 0:
                    pe.wait_ge(s_ol, unit(Q, u) * 2 - 1 + part)
                if part == 0 and g == 0 and not zero(Q):
                    pe.wait_ge(s_wT[e], Q)
                for t in (range(3), range(3, 8))[part]:
                    c, h = t // 4, t % 4
                    w_hi = k.wlh[:, 4 * g + h, c, 128 * e:128 * e + 128]
                    w_lo = k.wll[:, 4 * g + h, c, 128 * e:128 * e + 128]
                    o_hi, o_lo = oh[g % 2][:, h, c, :], ol[g % 2][:, h, c, :]
                    o = wb[e][:, 0:Q4]
                    pe.matmul(o, w_hi, o_hi, start=(g == 0 and t == 0), stop=False)
                    pe.matmul(o, w_hi, o_lo, start=False, stop=False)
                    x = pe.matmul(o, w_lo, o_hi, start=False, stop=(g == 3 and t == 7))
                if part == 1 and e == 1:
                    x.then_inc(s_Wg, 1)
                elif part == 1 and g == 3:
                    x.then_inc(s_W0, 1)

            def quad(Q, first, nxt):
                for u in range(8):
                    n = unit(Q, u)
                    w = u >= 2 or not first
                    fr = nxt and u in (5, 6)
                    bk = not first and u in (2, 3)
                    turn(Q, u)
                    n2 = later(Q, u, 2)
                    if n2:
                        scores(*n2)
                    if fr or bk:
                        pe.wait_ge(s_ol, n * 2)
                    if fr:
                        front(Q + 1, u - 5)
                    if bk:
                        back(Q - 1, u - 2)
                    if w:
                        times_w(Q, u, 0)
                    pe.wait_ge(s_al, n + 1)
                    if u < 2:
                        pe.wait_ge(s_xl, Q * 2 + (u + 1))
                    if fr:
                        pe.wait_ge(s_yT, Q * 2 + (u - 2))
                    if bk:
                        pe.wait_ge(s_add, Q * 2 + (u - 3))
                    weigh(Q, u, 0)
                    if w:
                        times_w(Q, u, 1)
                    weigh(Q, u, 1)

            front(0, 0)
            pe.wait_ge(s_yT, 1)
            front(0, 1)
            scores(0, 0)
            scores(0, 1)
            all_quads(pe, quad)
            for u in range(2):
                for part in range(2):
                    times_w(QUADS, u, part)
            back(LAST, 0)
            pe.wait_ge(s_add, 2 * LAST + 1)
            back(LAST, 1)

        @block.scalar
        def _(act):
            def copy(dst, src):
                return act.activation(dst, src, ACT.Copy)

            def turned_tokens(Q, p):
                act.wait_ge(s_F, Q * 2 + (p + 1))
                copy(yT[:, :, W2T * p:W2T * p + W2T],
                     vb[:, 1, 0:2 * W2T].rearrange("p (c t) -> p c t", c=2)).then_inc(s_yT, 1)

            def norm_x(Q, p):
                act.wait_ge(s_nm, Q * 2 + (p + 1))
                if not zero(Q):
                    act.wait_ge(s_F, Q * 2 + (p - 1))
                    act.wait_ge(s_xl, Q * 2 + (p - 1))
                for j in range(2):
                    x = act.activation(xn[p][:, j, :], k.sample(Q * 4 + (2 * p + j)), ACT.Identity,
                                       bias=nm[:, j:j + 1], scale=rs[:, j:j + 1])
                x.then_inc(s_xn, 1)

            def next_y(Q, p):
                act.wait_ge(s_nm2, Q * 2 + (p + 1))
                for j in range(2):
                    x = act.activation(y2[:, j, :], k.sample(Q * 4 + (2 * p + j)), ACT.Identity,
                                       bias=nm2[:, j:j + 1], scale=rs2[:, j:j + 1])
                x.then_inc(s_y2, 1)

            def x_high(Q, p):
                act.wait_ge(s_xn, Q * 2 + (p + 1))
                if not zero(Q):
                    act.wait_ge(s_av, Q * 16 + (2 * p - 2))
                copy(xh[:, 2 * p:2 * p + 2, :], xn[p][:]).then_inc(s_xh, 1)

            def exps(Q, u):
                act.wait_ge(s_S, unit(Q, u) + 1)
                act.activation(eb[u % 4][:].rearrange("p (c t) -> p c t", c=2), sc[0:NT, :, 0:CW], ACT.Exp,
                               scale=HD ** -0.5).then_inc(s_exp, 1)

            def turned(Q, u):
                act.wait_ge(s_T, unit(Q, u) + 1)
                copy(ah[u % 2][:].rearrange("p (c t) -> p c t", c=2), tb[0:NT, :, 0:CW]).then_inc(s_ah, 1)

            def values(Q, u, c):
                g, p = u // 2, u % 2
                act.wait_ge(s_av, unit(Q, u) * 2 + (c + 1))
                if c == 0 and p == 0 and not (zero(Q) and g < 2):
                    act.wait_ge(s_Wg, Q * 4 + (g - 1))
                copy(oh[g % 2][:, :, c, W2T * p:W2T * p + W2T].rearrange("p h (j t) -> p j h t", j=2),
                     vb[:, :, 0:CW].rearrange("p j (h t) -> p j h t", h=4)).then_inc(s_oh, 1)

            def product(Q, e):
                act.wait_ge(s_W0 if e == 0 else s_Wg, Q + 1 if e == 0 else Q * 4 + 4)
                copy(wT[:, e, :], wb[e][:, 0:Q4]).then_inc(s_wT[e], 1)

            def quad(Q, first, nxt):
                for u in range(8):
                    turned(Q, u)
                    n2 = later(Q, u, 2)
                    if n2:
                        exps(*n2)
                    if nxt and u in (5, 6):
                        turned_tokens(Q + 1, u - 5)
                    if nxt and u == 7:
                        x_high(Q + 1, 0)
                    if not first and u == 0:
                        x_high(Q, 1)
                    values(Q, u, 0)
                    if not first and u in (6, 7):
                        next_y(Q - 1, u - 6)
                    if nxt and u in (3, 5):
                        norm_x(Q + 1, (u - 3) // 2)
                    values(Q, u, 1)
                    if not first and u < 2:
                        product(Q - 1, u)

            for p in range(2):
                norm_x(0, p)
                turned_tokens(0, p)
                x_high(0, p)
            exps(0, 0)
            exps(0, 1)
            all_quads(act, quad)
            product(LAST, 0)
            product(LAST, 1)
            next_y(LAST, 0)
            next_y(LAST, 1)

        @block.vector
        def _(dve):
            def add_rows(Q, p):
                dve.wait_ge(s_yg[p], Q * 32 + 32)
                for j in range(2):
                    h = k.sample(Q * 4 + (2 * p + j))
                    x = dve.scalar_tensor_tensor(h, yg[p][j][:], k.gate[:, bass.ds(Q * 4 + (2 * p + j), 1)], h,
                                                 ALU.mult, ALU.add)
                x.then_inc(s_row, 1)

            def ln_stats(Q, p):
                m = Q * 2 + (p + 1)
                dve.wait_ge(s_row, m)
                dve.sem_inc(k.s_hold, 1)
                for j in range(2):
                    x = dve.bn_stats(st[:, j, :], k.sample(Q * 4 + (2 * p + j)))
                x.then_inc(s_st, 1)
                dve.wait_ge(s_st, m)
                dve.sem_inc(k.s_hold, 1)
                for j in range(2):
                    x = dve.bn_aggr(mv[:, j, :], st[:, j, :])
                x.then_inc(s_mv, 1)
                dve.wait_ge(s_mv, m)
                if not (zero(Q) and p == 0):
                    dve.wait_ge(s_xn, Q * 2 + p)
                dve.tensor_scalar(rs[:], mv[:, :, 1], EPS, None, ALU.add).then_inc(s_ve, 1)

            def ln_shift(Q, p):
                m = Q * 2 + (p + 1)
                dve.wait_ge(s_rs, m)
                dve.scalar_tensor_tensor(nm[:], mv[:, :, 0], -1.0, rs[:], ALU.mult, ALU.mult).then_inc(s_nm, 1)

            def sums(Q, u):
                n = unit(Q, u)
                dve.wait_ge(s_exp, n + 1)
                dve.tensor_reduce(sm[u % 4][:], eb[u % 4][:].rearrange("p (h t) -> p h t", h=8), X,
                                  ALU.add).then_inc(s_sum, 1)
                dve.wait_ge(s_sum, n + 1)
                dve.reciprocal(rc[u % 4][:], sm[u % 4][:]).then_inc(s_rc, 1)

            def turned(Q, u):
                dve.wait_ge(s_ah, unit(Q, u) + 1)
                r = lambda t: t.rearrange("p (c t) -> p c t", c=2)
                dve.tensor_tensor(r(al[u % 2][:]), tb[0:NT, :, 0:CW], r(ah[u % 2][:]),
                                  ALU.subtract).then_inc(s_al, 1)

            def values(Q, u, c):
                g, p = u // 2, u % 2
                dve.wait_ge(s_oh, unit(Q, u) * 2 + (c + 1))
                r = lambda t: t[g % 2][:, :, c, W2T * p:W2T * p + W2T].rearrange("p h (j t) -> p j h t", j=2)
                dve.tensor_tensor(r(ol), vb[:, :, 0:CW].rearrange("p j (h t) -> p j h t", h=4), r(oh),
                                  ALU.subtract).then_inc(s_ol, 1)

            def add(Q, p):
                dve.wait_ge(s_B, Q * 2 + (p + 1))
                h = k.samples(Q * 4 + 2 * p, 2)
                dve.tensor_tensor(h, h, vb[0:NT, 0, :], ALU.add).then_inc(s_add, 1)

            def next_stats(Q, p):
                m = Q * 2 + (p + 1)
                dve.wait_ge(s_add, m)
                dve.sem_inc(k.s_hold, 1)
                for j in range(2):
                    x = dve.bn_stats(st2[:, j, :], k.sample(Q * 4 + (2 * p + j)))
                x.then_inc(s_st2, 1)

            def next_var(Q, p):
                m = Q * 2 + (p + 1)
                dve.wait_ge(s_st2, m)
                dve.sem_inc(k.s_hold, 1)
                for j in range(2):
                    x = dve.bn_aggr(mv2[:, j, :], st2[:, j, :])
                x.then_inc(s_mv2, 1)
                dve.wait_ge(s_mv2, m)
                dve.tensor_scalar(rs2[:], mv2[:, :, 1], EPS, None, ALU.add)
                dve.tensor_copy(k.mv[:, bass.ds(Q * 4 + 2 * p, 2), :].rearrange("p a s -> p (a s)"),
                                mv2[:].rearrange("p a s -> p (a s)")).then_inc(s_ve2, 1)

            def next_shift(Q, p):
                m = Q * 2 + (p + 1)
                dve.wait_ge(s_rs2, m)
                dve.tensor_copy(k.rs[:, bass.ds(Q * 4 + 2 * p, 2)], rs2[:])
                dve.scalar_tensor_tensor(nm2[:], mv2[:, :, 0], -1.0, rs2[:], ALU.mult, ALU.mult).then_inc(s_nm2, 1)

            def next_max(Q, p):
                dve.wait_ge(s_y2, Q * 2 + (p + 1))
                dve.tensor_reduce(k.amx[0:NT, bass.ds(Q * 4 + 2 * p, 2)], y2[:], X, ALU.max,
                                  apply_absolute_value=True).then_inc(s_mx, 1)

            def quad(Q, first, nxt):
                for u in range(8):
                    turned(Q, u)
                    n1 = later(Q, u, 1)
                    if not first and u in (2, 3):
                        add(Q - 1, u - 2)
                    if n1:
                        sums(*n1)
                    if nxt and u in (3, 5):
                        ln_shift(Q + 1, (u - 3) // 2)
                    if not first and u in (6, 7):
                        next_shift(Q - 1, u - 6)
                    values(Q, u, 0)
                    if nxt and u in (1, 3):
                        add_rows(Q + 1, (u - 1) // 2)
                    if nxt and u in (2, 4):
                        ln_stats(Q + 1, (u - 2) // 2)
                    if not first and u in (6, 7):
                        next_max(Q - 1, u - 6)
                    if not first and u in (5, 6):
                        next_stats(Q - 1, u - 5)
                    values(Q, u, 1)
                    if not first and u in (5, 6):
                        next_var(Q - 1, u - 5)

            dve.memset(k.amx[:], 0.0).then_inc(s_z2, 1)
            dve.wait_ge(s_z2, 1)
            for p in range(2):
                add_rows(0, p)
                ln_stats(0, p)
                ln_shift(0, p)
            sums(0, 0)
            all_quads(dve, quad)
            for p in range(2):
                add(LAST, p)
                if p == 1:
                    next_shift(LAST, 0)
                    next_max(LAST, 0)
                next_stats(LAST, p)
                next_var(LAST, p)
            next_shift(LAST, 1)
            next_max(LAST, 1)

        @block.gpsimd
        def _(pool):
            def rows(Q, p):
                if not zero(Q):
                    pool.wait_ge(s_row, Q * 2 + (p - 1))
                    pool.sem_inc(k.s_hold, 1)
                pool.tensor_copy(sl[p][:], k.slot[:, bass.ds(Q * 4 + 2 * p, 2)]).then_inc(s_sl, 1)
                pool.wait_ge(s_sl, Q * 2 + (p + 1))
                pool.sem_inc(k.s_hold, 1)
                for j in range(2):
                    pool.indirect_dma_start(out=yg[p][j][:], out_offset=None, in_=k.yd[:],
                                            in_offset=bass.IndirectOffsetOnAxis(sl[p][:, j:j + 1], 0),
                                            bounds_check=NE * CAP - 1, oob_is_err=False).then_inc(s_yg[p], 16)

            def rstd(Q, p):
                pool.wait_ge(s_ve, Q * 2 + (p + 1))
                pool.tensor_tensor(rs[:], rs[:], k.mhalf[0:NT, 0:2], ALU.pow).then_inc(s_rs, 1)

            def next_rstd(Q, p):
                pool.wait_ge(s_ve2, Q * 2 + (p + 1))
                pool.tensor_tensor(rs2[:], rs2[:], k.mhalf[0:NT, 0:2], ALU.pow).then_inc(s_rs2, 1)

            def x_low(Q, p):
                pool.wait_ge(s_xh, Q * 2 + (p + 1))
                v = slice(2 * p, 2 * p + 2)
                pool.tensor_tensor(xl[:, v, :], xn[p][:], xh[:, v, :], ALU.subtract).then_inc(s_xl, 1)

            def diagonal(Q, u):
                g, p = u // 2, u % 2
                if u < 2:
                    pool.wait_ge(s_yT, Q * 2 + (u + 1))
                y = yT[:, g // 2, W2T * p:W2T * p + W2T].rearrange("p (j t) -> p j t", j=2)
                mask = k.mask[:, 4 * (g % 2):4 * (g % 2) + 4]
                pool.tensor_tensor(yd[u % 4][:].rearrange("p (j h t) -> p j h t", j=2, h=4),
                                   y.unsqueeze(2).broadcast_to([128, 2, 4, NT]),
                                   mask.unsqueeze(1).unsqueeze(3).broadcast_to([128, 2, 4, NT]),
                                   ALU.mult).then_inc(s_yd, 1)

            def norm(Q, u):
                pool.wait_ge(s_rc, unit(Q, u) + 1)
                e = eb[u % 4][:].rearrange("p (h t) -> p h t", h=8)
                pool.tensor_tensor(e, e, rc[u % 4][:].unsqueeze(2).broadcast_to([NT, 8, NT]),
                                   ALU.mult).then_inc(s_nrm, 1)

            def quad(Q, first, nxt):
                for u in range(8):
                    n1, n3 = later(Q, u, 1), later(Q, u, 3)
                    if n1:
                        norm(*n1)
                    if n3:
                        diagonal(*n3)
                    if nxt and u == 7:
                        x_low(Q + 1, 0)
                    if not first and u == 0:
                        x_low(Q, 1)
                    if nxt and u in (0, 1):
                        rows(Q + 1, u)
                    if nxt and u in (2, 4):
                        rstd(Q + 1, (u - 2) // 2)
                    if not first and u in (5, 6):
                        next_rstd(Q - 1, u - 5)

            for p in range(2):
                for j in range(2):
                    pool.memset(yg[p][j][:], 0.0).then_inc(s_z, 1)
            pool.wait_ge(s_z, 4)
            rows(0, 0)
            rows(0, 1)
            rstd(0, 0)
            rstd(0, 1)
            for u in range(3):
                diagonal(0, u)
            x_low(0, 0)
            x_low(0, 1)
            norm(0, 0)
            all_quads(pool, quad)
            next_rstd(LAST, 0)
            next_rstd(LAST, 1)

    clear(nc, used)


QMAX = 127.0
ROUND = 1.5 * 2.0 ** 23
FI = 704
MI = (FI + 127) // 128
PART = [min(128, FI - 128 * m) for m in range(MI)]


def mlp_tables(nc, k, sb, sem):
    k.identb = sb("ml_ident", [128, 128], BF16)
    k.wgT = sb("ml_wgT", [128, 2, FI], BF16)
    k.wuT = sb("ml_wuT", [128, 2, FI], BF16)
    k.wdT = sb("ml_wdT", [128, MI, D], BF16)
    k.sg = sb("ml_sg", [128, MI])
    k.su = sb("ml_su", [128, MI])
    k.srow = sb("ml_srow", [NT, D])
    k.sig = sb("ml_sig", [128, 2])
    k.mv = sb("ml_mv", [NT, NB, 2])
    k.rs = sb("ml_rs", [NT, NB])
    k.amx = sb("ml_amx", [128, NB])


class MlpWeights:

    def __init__(self, nc, k, ins, ctx, sem):
        sb = lambda n, s, d=F32: ctx.enter_context(nc.sbuf_tensor(n, s, d))
        self.k, self.ins = k, ins
        self.wg, self.wu = sb("mw_g", [128, MI, D]), sb("mw_u", [128, MI, D])
        self.wd = sb("mw_d", [128, 2, FI])
        self.wgb, self.wub = sb("mw_gb", [128, MI, D], BF16), sb("mw_ub", [128, MI, D], BF16)
        self.wdb = sb("mw_db", [128, 2, FI], BF16)
        self.sd = sb("mw_sd", [128, 2])
        self.inv = sb("mw_inv", [128, 2 * MI + 2])
        self.clip = sb("mw_clip", [128, 2])
        self.magic = sb("mw_magic", [128, 2])
        (self.s_w, self.s_z, self.s_id, self.s_ch, self.s_inv, self.s_r, self.s_q, self.s_T, self.s_e,
         self.s_clip) = (sem(f"s_mw_{n}") for n in ("loaded", "zero", "ident", "step", "inverse", "rounded",
                                                    "whole", "turned", "sb", "clip"))

    def load(self, sp):
        sp.wait_ge(self.s_z, 2)
        for w, n in ((self.wg, "w_gate"), (self.wu, "w_up")):
            src = self.ins[f"L1_ffn_{n}"]
            sp.dma_start(w[:, 0:MI - 1, :], src[0:128 * (MI - 1), :]
                         .rearrange("(m p) d -> p m d", p=128)).then_inc(self.s_w, 16)
            sp.dma_start(w[0:PART[-1], MI - 1, :], src[128 * (MI - 1):FI, :]).then_inc(self.s_w, 16)
        sp.dma_start(self.wd[:], self.ins["L1_ffn_w_down"].rearrange("(c p) i -> p c i", p=128)).then_inc(self.s_w, 16)
        for j, n in enumerate(("x", "down")):
            sp.dma_start(self.clip[:, j:j + 1], self.ins[f"L1_ffn_clip_{n}"].rearrange("(a b) -> a b", a=1)
                         .broadcast_to([128, 1])).then_inc(self.s_clip, 16)

    def pads(self, pool):
        pool.memset(self.wg[:, MI - 1, :], 1.0).then_inc(self.s_z, 1)
        pool.memset(self.wu[:, MI - 1, :], 1.0).then_inc(self.s_z, 1)
        pool.memset(self.magic[:, 0:1], ROUND).then_inc(self.s_z, 1)
        pool.memset(self.magic[:, 1:2], -ROUND).then_inc(self.s_z, 1)
        pool.tensor_copy(self.k.identb[:], self.k.ident[:]).then_inc(self.s_id, 1)

    def scales(self, dve):
        k = self.k
        dve.wait_ge(self.s_w, 80)
        for w, s in ((self.wg, k.sg), (self.wu, k.su), (self.wd, self.sd)):
            x = dve.tensor_reduce(s[:], w[:], X, ALU.max, apply_absolute_value=True)
        x.then_inc(self.s_ch, 1)
        dve.wait_ge(self.s_ch, 1)
        for s in (k.sg, k.su, self.sd):
            x = dve.tensor_scalar(s[:], s[:], 1.0 / QMAX, None, ALU.mult)
        x.then_inc(self.s_ch, 1)
        dve.wait_ge(self.s_ch, 2)
        dve.reciprocal(self.inv[:, 0:MI], k.sg[:])
        dve.reciprocal(self.inv[:, MI:2 * MI], k.su[:])
        dve.reciprocal(self.inv[:, 2 * MI:2 * MI + 2], self.sd[:]).then_inc(self.s_inv, 1)

    def sigmoid(self, act):
        act.wait_ge(self.s_clip, 32)
        act.activation(self.k.sig[:], self.clip[:], ACT.Sigmoid)

    def rounded(self, act, t):
        w, o, m = ((self.wg, 0, MI), (self.wu, MI, MI), (self.wd, 2 * MI, 2))[t]
        if t == 0:
            act.wait_ge(self.s_inv, 1)
            act.wait_ge(self.s_z, 4)
        for j in range(m):
            x = act.activation(w[:, j, :], w[:, j, :], ACT.Identity, bias=self.magic[:, 0:1],
                               scale=self.inv[:, o + j:o + j + 1])
        x.then_inc(self.s_r, 1)

    def whole(self, act):
        act.wait_ge(self.s_r, 3)
        for w, b in ((self.wg, self.wgb), (self.wu, self.wub), (self.wd, self.wdb)):
            act.activation(b[:].rearrange("p m d -> p (m d)"), w[:].rearrange("p m d -> p (m d)"), ACT.Identity,
                           bias=self.magic[:, 1:2]).then_inc(self.s_q, 1)

    def turn(self, pe, t):
        k, bkb, b = self.k, [b.bitcast(BF16) for b in self.k.bank], (self.wgb, self.wub)[t]
        if t == 0:
            pe.wait_ge(self.s_id, 1)
            pe.wait_ge(self.s_q, 3)
        else:
            pe.wait_ge(self.s_e, 1)
        for c in range(2):
            for m in range(MI):
                x = pe.transpose(bkb[6 + c][:, 128 * m:128 * m + PART[m]],
                                 b[0:PART[m], m, 128 * c:128 * c + 128],
                                 k.identb[0:PART[m], 0:PART[m]])
        x.then_inc(self.s_T, 1)

    def turn_down(self, pe):
        k, bkb = self.k, [b.bitcast(BF16) for b in self.k.bank]
        pe.wait_ge(self.s_e, 2)
        for m in range(MI):
            for c in range(2):
                o = D * (m % 4) + 128 * c
                x = pe.transpose(bkb[6 + m // 4][0:PART[m], o:o + 128],
                                 self.wdb[:, c, 128 * m:128 * m + PART[m]], k.identb[:])
        x.then_inc(self.s_T, 1)
        pe.wait_ge(self.s_e, 3)
        for c in range(2):
            x = pe.matmul(k.bank[6][0:NT, 128 * c:128 * c + 128], self.sd[:, c:c + 1].broadcast_to([128, NT]),
                          k.ident[:], start=True, stop=True)
        x.then_inc(self.s_T, 1)

    def turned(self, act, t):
        w, bkb = (self.k.wgT, self.k.wuT)[t], [b.bitcast(BF16) for b in self.k.bank]
        act.wait_ge(self.s_T, t + 1)
        for c in range(2):
            x = act.activation(w[:, c, :], bkb[6 + c][:, 0:FI], ACT.Copy)
        x.then_inc(self.s_e, 1)

    def turned_down(self, act):
        k, bkb = self.k, [b.bitcast(BF16) for b in self.k.bank]
        act.wait_ge(self.s_T, 3)
        act.activation(k.wdT[:, 0:4, :].rearrange("p m d -> p (m d)"), bkb[6][:, 0:4 * D], ACT.Copy)
        act.activation(k.wdT[:, 4, :], bkb[7][:, 0:D], ACT.Copy)
        act.activation(k.wdT[0:PART[-1], 5, :], bkb[7][0:PART[-1], D:2 * D], ACT.Copy).then_inc(self.s_e, 1)
        act.wait_ge(self.s_T, 4)
        act.activation(k.srow[:], k.bank[6][0:NT, 0:D], ACT.Copy)


def mlp(nc, k, ins, out):
    G = 4
    GN = NB // G
    GT = G * NT
    with ExitStack() as ctx:
        sb = lambda n, s, d=F32: ctx.enter_context(nc.sbuf_tensor(n, s, d))
        sem = lambda n: ctx.enter_context(nc.semaphore(n))
        identb, wgT, wuT, wdT, sg, su, srow, sig = k.identb, k.wgT, k.wuT, k.wdT, k.sg, k.su, k.srow, k.sig
        gmx = sb("ml_gmx", [128, 1])
        amax = sb("ml_amax", [128, 1])
        sx = sb("ml_sx", [128, 1])
        ix = sb("ml_ix", [128, 1])
        hh = sb("ml_h", [128, MI, NB * NT])
        hmx = sb("ml_hmx", [128, GN * MI])
        sh = sb("ml_sh", [128, 1])
        ih = sb("ml_ih", [128, 1])
        bk = k.bank
        bkb = [b.bitcast(BF16) for b in bk]

        with ExitStack() as c2:
            s_g, s_gd, s_i = (sem(f"s_ml_{n}") for n in ("gmax", "over_partitions", "inverse"))
            with nc.Block() as block:
                @block.vector
                def _(dve):
                    dve.tensor_reduce(gmx[:], k.amx[:], X, ALU.max).then_inc(s_g, 1)
                    dve.wait_ge(s_gd, 1)
                    dve.scalar_tensor_tensor(sx[:], amax[:], 1.0 / QMAX, sig[:, 0:1], ALU.mult, ALU.mult).then_inc(s_g, 1)
                    dve.wait_ge(s_g, 2)
                    dve.reciprocal(ix[:], sx[:]).then_inc(s_i, 1)
                    dve.tensor_scalar(sg[:], sg[:], sx[:, 0:1], None, ALU.mult)
                    dve.tensor_scalar(su[:], su[:], sx[:, 0:1], None, ALU.mult)
                    dve.wait_ge(s_i, 1)
                    dve.tensor_scalar(k.rs[:], k.rs[:], ix[0:NT, 0:1], None, ALU.mult)

                @block.gpsimd
                def _(pool):
                    pool.wait_ge(s_g, 1)
                    pool.partition_all_reduce(amax[:], gmx[:], 128, bass.bass_isa.ReduceOp.max).then_inc(s_gd, 1)

        with ExitStack() as c2:
            xq = [c2.enter_context(nc.sbuf_tensor(f"ml_xq{i}", [NT, G, D], F32)) for i in range(2)]
            xb = [c2.enter_context(nc.sbuf_tensor(f"ml_xb{i}", [NT, G, D], BF16)) for i in range(2)]
            xT = [c2.enter_context(nc.sbuf_tensor(f"ml_xT{i}", [128, 2, GT], BF16)) for i in range(2)]
            gt = [c2.enter_context(nc.sbuf_tensor(f"ml_gt{i}", [128, GT], F32)) for i in range(2)]
            magic = c2.enter_context(nc.sbuf_tensor("ml_magic", [128, 2], F32))
            s_z, s_q0, s_q1, s_q2, s_xb, s_T, s_xT, s_gate, s_up, s_gt, s_h, s_mx, s_g, s_gd = (
                sem(f"s_mg_{n}") for n in ("zero", "scaled", "clipped", "rounded", "xb", "turned", "xT", "gate", "up", "silu", "h", "max",
                                           "gmax", "scale"))
            with nc.Block() as block:
                @block.gpsimd
                def _(pool):
                    pool.memset(hmx[:], 0.0).then_inc(s_z, 1)
                    pool.memset(hh[:, MI - 1, :], 0.0).then_inc(s_z, 1)
                    pool.memset(magic[:, 0:1], ROUND).then_inc(s_z, 1)
                    pool.memset(magic[:, 1:2], -ROUND).then_inc(s_z, 1)
                    pool.wait_ge(s_g, 1)
                    pool.partition_all_reduce(amax[:], gmx[:], 128, bass.bass_isa.ReduceOp.max).then_inc(s_gd, 1)

                @block.tensor
                def _(pe):
                    def turn(i, q):
                        n = i * 2 + q
                        pe.wait_ge(s_xb, n + 1)
                        if not (isinstance(i, int) and i == 0 and q == 0):
                            pe.wait_ge(s_xT, n)
                        for c in range(2):
                            for j in range(G):
                                x = pe.transpose(bkb[c][:, (NT + 1) * j:(NT + 1) * j + NT],
                                                 xb[q][:, j, 128 * c:128 * c + 128], identb[0:NT, 0:NT])
                        x.then_inc(s_T, 1)

                    def group(i, q, nxt):
                        n = i * 2 + q
                        pe.wait_ge(s_xT, n + 1)
                        for m in range(MI):
                            if m == MI - 1 and nxt:
                                turn(*((i, 1) if q == 0 else (i + 1, 0)))
                            r = n * MI + m
                            b = m % 2
                            if not (isinstance(i, int) and i == 0 and q == 0 and m < 2):
                                pe.wait_ge(s_gt, r - 1)
                            for c in range(2):
                                x = pe.matmul(bk[2 + b][0:PART[m], 0:GT], wgT[:, c, 128 * m:128 * m + PART[m]],
                                              xT[q][:, c, :], start=(c == 0), stop=(c == 1))
                            x.then_inc(s_gate, 1)
                            if not (isinstance(i, int) and i == 0 and q == 0 and m < 2):
                                pe.wait_ge(s_h, r - 1)
                            for c in range(2):
                                x = pe.matmul(bk[4 + b][0:PART[m], 0:GT], wuT[:, c, 128 * m:128 * m + PART[m]],
                                              xT[q][:, c, :], start=(c == 0), stop=(c == 1))
                            x.then_inc(s_up, 1)

                    turn(0, 0)
                    group(0, 0, True)
                    group(0, 1, True)
                    with pe.Fori(1, GN // 2 - 1) as i:
                        group(i, 0, True)
                        group(i, 1, True)
                    group(GN // 2 - 1, 0, True)
                    group(GN // 2 - 1, 1, False)

                @block.scalar
                def _(act):
                    def rounded(i, q):
                        act.wait_ge(s_q1, i * 2 + (q + 1))
                        act.activation(xq[q][:], xq[q][:], ACT.Identity, bias=magic[0:NT, 0:1]).then_inc(s_q2, 1)

                    def whole(i, q):
                        n = i * 2 + q
                        act.wait_ge(s_q2, n + 1)
                        if not (isinstance(i, int) and i == 0):
                            act.wait_ge(s_T, n - 1)
                        act.activation(xb[q][:], xq[q][:], ACT.Identity, bias=magic[0:NT, 1:2]).then_inc(s_xb, 1)

                    def turned(i, q):
                        n = i * 2 + q
                        act.wait_ge(s_T, n + 1)
                        for c in range(2):
                            x = act.activation(xT[q][:, c, :].rearrange("p (j t) -> p j t", j=G),
                                               bkb[c][:, 0:G * (NT + 1)].rearrange("p (j t) -> p j t", j=G)[:, :, 0:NT],
                                               ACT.Copy)
                        x.then_inc(s_xT, 1)

                    def group(i, q, nxt):
                        n = i * 2 + q
                        ahead = (i, 1) if q == 0 else (i + 1, 0)
                        for m in range(MI):
                            r = n * MI + m
                            act.wait_ge(s_gate, r + 1)
                            if not (isinstance(i, int) and i == 0 and q == 0 and m < 2):
                                act.wait_ge(s_h, r - 1)
                            p = PART[m]
                            act.activation(gt[m % 2][0:p, :], bk[2 + m % 2][0:p, 0:GT], ACT.Silu,
                                           scale=sg[0:p, m:m + 1]).then_inc(s_gt, 1)
                            if m == 1 and nxt:
                                rounded(*ahead)
                            if m == 2 and nxt:
                                whole(*ahead)
                            if m == MI - 2 and nxt:
                                turned(*ahead)

                    act.wait_ge(s_z, 4)
                    rounded(0, 0)
                    whole(0, 0)
                    turned(0, 0)
                    group(0, 0, True)
                    group(0, 1, True)
                    with act.Fori(1, GN // 2 - 1) as i:
                        group(i, 0, True)
                        group(i, 1, True)
                    group(GN // 2 - 1, 0, True)
                    group(GN // 2 - 1, 1, False)

                @block.vector
                def _(dve):
                    def scaled(i, q):
                        if not (isinstance(i, int) and i == 0):
                            dve.wait_ge(s_xb, i * 2 + (q - 1))
                        for j in range(G):
                            b = i * (2 * G) + (q * G + j)
                            x = dve.tensor_scalar(xq[q][:, j, :], k.sample(b), k.mv[:, bass.ds(b, 1), 0],
                                                  k.rs[:, bass.ds(b, 1)], ALU.subtract, ALU.mult)
                        x.then_inc(s_q0, 1)
                        dve.wait_ge(s_q0, i * 2 + (q + 1))
                        v = xq[q][:].rearrange("p j d -> p (j d)")
                        dve.tensor_scalar(v, v, QMAX, -QMAX - 1.0, ALU.min, ALU.max).then_inc(s_q1, 1)

                    def largest(i, q, m):
                        r = (i * 2 + q) * MI + m
                        dve.wait_ge(s_h, r + 1)
                        dve.tensor_reduce(hmx[0:PART[m], bass.ds(r, 1)],
                                          hh[0:PART[m], m, bass.ds(i * (2 * GT) + q * GT, GT)], X, ALU.max,
                                          apply_absolute_value=True).then_inc(s_mx, 1)

                    def group(i, q, nxt):
                        n = i * 2 + q
                        for m in range(MI):
                            r = n * MI + m
                            p = PART[m]
                            if m == 0 and nxt:
                                scaled(*((i, 1) if q == 0 else (i + 1, 0)))
                            dve.wait_ge(s_up, r + 1)
                            dve.wait_ge(s_gt, r + 1)
                            h = hh[0:p, m, bass.ds(i * (2 * GT) + q * GT, GT)]
                            dve.scalar_tensor_tensor(h, bk[4 + m % 2][0:p, 0:GT], su[0:p, m:m + 1],
                                                     gt[m % 2][0:p, :], ALU.mult, ALU.mult).then_inc(s_h, 1)
                            if m >= 1:
                                largest(i, q, m - 1)
                        largest(i, q, MI - 1)

                    dve.wait_ge(s_z, 4)
                    scaled(0, 0)
                    group(0, 0, True)
                    group(0, 1, True)
                    with dve.Fori(1, GN // 2 - 1) as i:
                        group(i, 0, True)
                        group(i, 1, True)
                    group(GN // 2 - 1, 0, True)
                    group(GN // 2 - 1, 1, False)
                    dve.wait_ge(s_mx, GN * MI)
                    dve.tensor_reduce(gmx[:], hmx[:], X, ALU.max).then_inc(s_g, 1)
                    dve.wait_ge(s_gd, 1)
                    dve.scalar_tensor_tensor(sh[:], amax[:], 1.0 / QMAX, sig[:, 1:2], ALU.mult, ALU.mult).then_inc(s_g, 1)
                    dve.wait_ge(s_g, 2)
                    dve.reciprocal(ih[:], sh[:])
                    dve.tensor_scalar(srow[:], srow[:], sh[0:NT, 0:1], None, ALU.mult)

        with ExitStack() as c2:
            hq = [c2.enter_context(nc.sbuf_tensor(f"ml_hq{i}", [128, MI, GT], F32)) for i in range(2)]
            hb = [c2.enter_context(nc.sbuf_tensor(f"ml_hb{i}", [128, MI, G, NT + 1], BF16)) for i in range(2)]
            dn = [c2.enter_context(nc.sbuf_tensor(f"ml_dn{i}", [NT, G, D], F32)) for i in range(2)]
            magic = c2.enter_context(nc.sbuf_tensor("ml_magic2", [128, 1], F32))
            s_z, s_q1, s_q2, s_hb, s_D, s_dn, s_res = (
                sem(f"s_md_{n}") for n in ("zero", "q1", "q2", "hb", "down", "scaled", "residual"))
            s_out = sem("s_out")
            with nc.Block() as block:
                @block.sync
                def _(sp):
                    with sp.Fori(0, GN) as g:
                        sp.wait_ge(s_res, g + 1)
                        for a, b, c in ((0, NPT, 1), (NPT, NPT + 1, 0), (NPT + 1, NT, NPT + 1)):
                            sp.dma_start(out[bass.ds(g * G, G), c:c + b - a, :].rearrange("b s d -> s b d"),
                                         k.H[a:b, bass.ds(g * G, G), :]).then_inc(s_out, 16)
                    sp.wait_ge(s_out, 48 * GN)

                @block.gpsimd
                def _(pool):
                    pool.memset(magic[:], -ROUND).then_inc(s_z, 1)
                    with pool.Fori(0, GN // 2) as i:
                        for q in range(2):
                            pool.wait_ge(s_dn, i * (2 * G) + (q * G + G))
                            h = k.samples(i * (2 * G) + q * G, G)
                            pool.tensor_tensor(h, h, dn[q][:].rearrange("p j d -> p (j d)"), ALU.add).then_inc(s_res, 1)

                @block.vector
                def _(dve):
                    def scaled(i, q):
                        n = i * 2 + q
                        if not (isinstance(i, int) and i == 0):
                            dve.wait_ge(s_hb, n - 1)
                        h = hh[:, :, bass.ds(i * (2 * GT) + q * GT, GT)]
                        dve.tensor_scalar(hq[q][:], h, ih[:, 0:1], QMAX, ALU.mult, ALU.min).then_inc(s_q1, 1)
                        dve.wait_ge(s_q1, n + 1)
                        v = hq[q][:].rearrange("p m t -> p (m t)")
                        dve.tensor_scalar(v, v, -QMAX - 1.0, ROUND, ALU.max, ALU.add).then_inc(s_q2, 1)

                    def group(i, q, nxt):
                        if nxt:
                            scaled(*((i, 1) if q == 0 else (i + 1, 0)))
                        if not (isinstance(i, int) and i == 0):
                            dve.wait_ge(s_res, i * 2 + (q - 1))
                        for j in range(G):
                            dve.wait_ge(s_D, i * (2 * G) + (q * G + j + 1))
                            dve.tensor_tensor(dn[q][:, j, :], bk[j % 4][0:NT, 0:D], srow[:], ALU.mult).then_inc(s_dn, 1)

                    scaled(0, 0)
                    group(0, 0, True)
                    group(0, 1, True)
                    with dve.Fori(1, GN // 2 - 1) as i:
                        group(i, 0, True)
                        group(i, 1, True)
                    group(GN // 2 - 1, 0, True)
                    group(GN // 2 - 1, 1, False)

                @block.scalar
                def _(act):
                    act.wait_ge(s_z, 1)

                    def whole(i, q):
                        n = i * 2 + q
                        act.wait_ge(s_q2, n + 1)
                        if not (isinstance(i, int) and i == 0):
                            act.wait_ge(s_D, i * (2 * G) + (q * G - G))
                        act.activation(hb[q][:, :, :, 0:NT].rearrange("p m j t -> p (m j) t"),
                                       hq[q][:].rearrange("p m (j t) -> p (m j) t", j=G), ACT.Identity,
                                       bias=magic[:, 0:1]).then_inc(s_hb, 1)

                    whole(0, 0)
                    whole(0, 1)
                    with act.Fori(1, GN // 2) as i:
                        whole(i, 0)
                        whole(i, 1)

                @block.tensor
                def _(pe):
                    def group(i, q):
                        pe.wait_ge(s_hb, i * 2 + (q + 1))
                        for j in range(G):
                            if not (isinstance(i, int) and i == 0 and q == 0):
                                pe.wait_ge(s_dn, i * (2 * G) + (q * G + j - G + 1))
                            for m in range(MI):
                                p = PART[m]
                                x = pe.matmul(bk[j % 4][0:NT, 0:D], hb[q][0:p, m, j, 0:NT], wdT[0:p, m, :],
                                              start=(m == 0), stop=(m == MI - 1))
                            x.then_inc(s_D, 1)

                    group(0, 0)
                    group(0, 1)
                    with pe.Fori(1, GN // 2) as i:
                        group(i, 0)
                        group(i, 1)


def build(nc, ins, out):
    with ExitStack() as ctx:
        sb = lambda n, s, d=F32: ctx.enter_context(nc.sbuf_tensor(n, s, d))
        sem = lambda n: ctx.enter_context(nc.semaphore(n))
        k = Shared()
        k.ps = ctx.enter_context(nc.psum_tensor("ps", [128, 8, 512], F32))
        k.bank = [k.ps[:, b, :] for b in range(8)]
        k.H = sb("H", [NT, NB, D])
        k.sample = lambda b: k.H[:, bass.ds(b, 1), :].rearrange("p a d -> p (a d)")
        k.samples = lambda b, n: k.H[:, bass.ds(b, n), :].rearrange("p a d -> p (a d)")
        k.ident = sb("ident", [128, 128])
        k.mhalf = sb("minus_half", [128, 8])
        k.mask = sb("head_mask", [128, 8])
        k.sem = sem
        k.s_go = sem("s_constants")
        k.s_hold = sem("s_waits_held")
        constants(nc, k, sem)
        k.slot = sb("slot", [NT, NB], U32)
        k.gate = sb("gate", [NT, NB])
        k.xd = nc.dram_tensor("expert_rows", (NE * CAP, D), F32).ap()
        k.yd = nc.dram_tensor("expert_outputs", (NE * CAP, D), F32).ap()
        k.s_xd0 = sem("s_table_zeroed")
        mlp_tables(nc, k, sb, sem)
        attn = ExitStack()
        attention_tables(nc, k, attn)
        tokens(nc, k, ins)
        attention(nc, k, ins)
        attn.close()
        with ExitStack() as tied:
            k.wlh = tied.enter_context(nc.sbuf_tensor("tied_w_hi", [128, NH, 2, D], F32R))
            k.wll = tied.enter_context(nc.sbuf_tensor("tied_w_lo", [128, NH, 2, D], F32R))
            with ExitStack() as moe:
                k.w1 = [moe.enter_context(nc.sbuf_tensor(f"w1_{q}", [128, 2, FF], F32)) for q in range(2)]
                k.w2 = [moe.enter_context(nc.sbuf_tensor(f"w2_{q}", [128, FF // 128, D], F32)) for q in range(2)]
                k.s_w1 = [sem(f"s_w1_{q}") for q in range(2)]
                k.s_w2 = [sem(f"s_w2_{q}") for q in range(2)]
                route(nc, k, ins)
                experts(nc, k, ins)
            tied_attention(nc, k, ins)
        mlp(nc, k, ins, out)


def constants(nc, k, sem):
    s_zero = sem("s_ident_zeroed")
    s_mask = sem("s_mask_step")
    with nc.Block() as block:
        @block.gpsimd
        def _(pool):
            pool.memset(k.mhalf[:], -0.5)
            pool.memset(k.mask[:], 1.0).then_inc(s_mask, 1)
            pool.wait_ge(s_mask, 1)
            pool.affine_select(out=k.mask[:], in_=k.mask[:], compare_op=ALU.is_ge, fill=0.0, base=0,
                               pattern=[[-HD, 8]], channel_multiplier=1).then_inc(s_mask, 1)
            pool.wait_ge(s_mask, 2)
            pool.affine_select(out=k.mask[:], in_=k.mask[:], compare_op=ALU.is_ge, fill=0.0, base=HD - 1,
                               pattern=[[HD, 8]], channel_multiplier=-1)
            pool.memset(k.ident[:], 0.0).then_inc(s_zero, 1)
            pool.wait_ge(s_zero, 1)
            pool.affine_select(out=k.ident[:], in_=k.ident[:], compare_op=ALU.not_equal, fill=1.0, base=0,
                               pattern=[[-1, 128]], channel_multiplier=1).then_inc(k.s_go, 1)


_INS = ["x", "txt", "L0_tok_ln1_g", "L0_tok_ln1_b", "L0_tok_W_proj", "L0_tok_b_proj", "L0_tok_ln2_g", "L0_tok_ln2_b",
        "L0_tok_cls_token", "L0_tok_pos_emb", "L0_attn_w_qkv", "L0_attn_w_proj", "L0_attn_b_proj", "L0_ffn_Wr",
        "L0_ffn_W1", "L0_ffn_W2", "L1_attn_weight", "L1_ffn_clip_x", "L1_ffn_clip_down", "L1_ffn_w_gate",
        "L1_ffn_w_up", "L1_ffn_w_down"]


def kernel(**inputs):
    import numpy as _np
    import concourse.bacc as _bacc
    from concourse import mybir as _mybir
    from concourse.bass_utils import run_bass_kernel_spmd as _run

    nc = _bacc.Bacc("TRN2", target_bir_lowering=False, num_devices=1)
    arrays, args = {}, {}
    for name in _INS:
        a = _np.ascontiguousarray(inputs[name])
        arrays[f"in_{name}"] = a
        args[name] = nc.dram_tensor(f"in_{name}", a.shape, _mybir.dt.from_np(a.dtype), kind="ExternalInput").ap()
    out = nc.dram_tensor("out_0", (NB, NT, D), F32, kind="ExternalOutput").ap()
    build(nc, args, out)
    r = _run(nc, [arrays], core_ids=[0])
    return r.results[0]["out_0"]
```
